# Optimizing a Trainium2 kernel written in Bass

```python
import numpy as np
import jax
import jax.numpy as jnp

def _softmax(x, axis=-1):
    return jax.nn.softmax(x, axis=axis)

def _gelu(x):
    return jax.nn.gelu(x, approximate=True)

def _silu(x):
    return jax.nn.silu(x)

def _sigmoid(x):
    return jax.nn.sigmoid(x)

def _layernorm(x, axis=-1, eps=1e-05):
    m = jnp.mean(x, axis=axis, keepdims=True)
    v = jnp.var(x, axis=axis, keepdims=True)
    return (x - m) / jnp.sqrt(v + eps)

def _scatter_add(tgt, idx, src, axis=0):
    return tgt.at[idx].add(src)

def _segment_sum(src, seg, n):
    return jax.ops.segment_sum(src, seg, n)
kernel_name = 'mk_flamingo_gated_d2_seqx_r8_5703f4'

def setup_inputs(seed: int=0):
    np.random.seed(seed)
    _w = jnp.asarray

    def _rec_inputs():
        import jax
        import jax.numpy as jnp
        _rk = jax.random.key(seed)
        x = -0.0005146 + 1 * jax.random.normal(jax.random.fold_in(_rk, 1), (2, 512, 128), jnp.float32)
        _lenS = 512 - jax.random.randint(jax.random.fold_in(_rk, 7), (2,), 0, max(1, 512 // 4) + 1, jnp.int32)
        _lenS2 = 154 - jax.random.randint(jax.random.fold_in(_rk, 8), (2,), 0, max(1, 154 // 4) + 1, jnp.int32)
        _ctx_768P = jax.random.normal(jax.random.fold_in(_rk, 11), (2, 16, 96), jnp.float32)
        _ctx_768c = jax.random.dirichlet(jax.random.fold_in(_rk, 511), 0.3 * jnp.ones((16,), jnp.float32), (2, 154))
        _ctx_768t = jnp.einsum('bsk,bkd->bsd', _ctx_768c, _ctx_768P)
        _ctx_768t = _ctx_768t * jax.lax.rsqrt(jnp.mean(jnp.square(_ctx_768t)) + 1e-12) * 0.953939
        ctx_768 = -0.00040386 + 0.999972 * (_ctx_768t + 0.3 * jax.random.normal(jax.random.fold_in(_rk, 611), (2, 154, 96), jnp.float32))
        _validS = jnp.arange(512)[None, :] < _lenS[:, None]
        _validS2 = jnp.arange(154)[None, :] < _lenS2[:, None]
        _causal = jnp.tril(jnp.ones((512, 512), dtype=bool))
        mask_BxS2_bk0 = jnp.logical_not(jnp.broadcast_to(_validS2[:, :], (2, 154)))
        _g = jax.random.normal(jax.random.fold_in(_rk, 9001), (2, 2), jnp.float32)
        _g = jnp.sign(_g) * jnp.maximum(jnp.abs(_g), 1.0) + (_g == 0) * 1.0
        g_xattn = _g[0]
        g_ffn = _g[1]
        return (x, ctx_768, mask_BxS2_bk0, g_xattn, g_ffn)
    x, ctx_768, mask_BxS2_bk0, g_xattn, g_ffn = _rec_inputs()

    def _L0_xattn_setup():
        import jax, jax.numpy as jnp
        import numpy as np
        DIM_IN, DIM_LAT, DIM_HEAD = (96, 128, 64)
        INNER = max(DIM_LAT, DIM_IN)
        HEADS = INNER // DIM_HEAD
        SCALE = DIM_HEAD ** (-0.5)
        RMS_EPS = 1e-08
        LN_EPS = 1e-05

        def layernorm(x, g, b):
            mu = jnp.mean(x, axis=-1, keepdims=True)
            var = jnp.mean((x - mu) ** 2, axis=-1, keepdims=True)
            return (x - mu) * jax.lax.rsqrt(var + LN_EPS) * g + b

        def rmsnorm(x, gamma):
            norm = jnp.sqrt(jnp.sum(x * x, axis=-1, keepdims=True)) * x.shape[-1] ** (-0.5)
            return x / jnp.maximum(norm, RMS_EPS) * gamma
        key = jax.random.key(seed)
        ks = jax.random.split(key, 12)
        b, n, m = (4, 512, 64)
        x = jax.random.normal(ks[0], (b, n, DIM_IN), jnp.float32)
        latents = jax.random.normal(ks[1], (b, m, DIM_LAT), jnp.float32)
        mask = jax.random.randint(ks[2], (b, n), 0, 2).astype(bool)
        s = lambda k, sh, fan: jax.random.normal(k, sh, jnp.float32) * fan ** (-0.5)
        return {'x': x, 'latents': latents, 'mask': mask, 'ln_x_g': jnp.ones((DIM_IN,), jnp.float32), 'ln_x_b': jnp.zeros((DIM_IN,), jnp.float32), 'ln_l_g': jnp.ones((DIM_LAT,), jnp.float32), 'ln_l_b': jnp.zeros((DIM_LAT,), jnp.float32), 'qn_g': jnp.ones((DIM_HEAD,), jnp.float32), 'kn_g': jnp.ones((DIM_HEAD,), jnp.float32), 'Wq': s(ks[3], (INNER, DIM_LAT), DIM_LAT), 'Wkv': s(ks[4], (2 * INNER, DIM_IN), DIM_IN), 'Wlkv': s(ks[5], (2 * INNER, DIM_LAT), DIM_LAT), 'Wo': s(ks[6], (DIM_LAT, INNER), INNER), 'bo': jnp.zeros((DIM_LAT,), jnp.float32)}
    _L0_xattn_all = _L0_xattn_setup()
    _L0_xattn_in = {k: v for k, v in _L0_xattn_all.items() if k in ('ln_x_g', 'ln_x_b', 'ln_l_g', 'ln_l_b', 'qn_g', 'kn_g', 'Wq', 'Wkv', 'Wlkv', 'Wo', 'bo')}
    del _L0_xattn_all

    def _L0_ffn_setup():
        import jax, jax.numpy as jnp
        import numpy as np
        D_MODEL = 128
        HIDDEN = 512
        NUM_EXPERTS = 8
        TOP_K = 2
        DEPTH = 12
        DEPTH_SCALE = 1.0 / np.sqrt(DEPTH)
        key = jax.random.key(seed)
        k_x, k_r, k_g, k_u, k_d = jax.random.split(key, 5)
        s_in = 1.0 / np.sqrt(D_MODEL)
        s_hid = 1.0 / np.sqrt(HIDDEN)
        return {'x': jax.random.normal(k_x, (2, 256, D_MODEL), dtype=jnp.float32), 'Wr': jax.random.normal(k_r, (D_MODEL, NUM_EXPERTS), dtype=jnp.float32) * s_in, 'Wg': jax.random.normal(k_g, (NUM_EXPERTS, D_MODEL, HIDDEN), dtype=jnp.float32) * s_in, 'Wu': jax.random.normal(k_u, (NUM_EXPERTS, D_MODEL, HIDDEN), dtype=jnp.float32) * s_in, 'Wd': jax.random.normal(k_d, (NUM_EXPERTS, HIDDEN, D_MODEL), dtype=jnp.float32) * s_hid}
    _L0_ffn_all = _L0_ffn_setup()
    _L0_ffn_in = {k: v for k, v in _L0_ffn_all.items() if k in ('Wr', 'Wg', 'Wu', 'Wd')}
    del _L0_ffn_all

    def _L1_xattn_setup():
        import jax, jax.numpy as jnp
        import numpy as np
        N_HEADS = 16
        DIM_EMBED = 128
        DIM_CROSS = 96
        DIM_HEAD = DIM_EMBED // N_HEADS
        key = jax.random.key(seed)
        ks = jax.random.split(key, 10)
        B, Sq, Sk = (8, 512, 77)
        s_e = 1.0 / np.sqrt(DIM_EMBED)
        s_c = 1.0 / np.sqrt(DIM_CROSS)
        return {'x': jax.random.normal(ks[0], (B, Sq, DIM_EMBED), jnp.float32), 'y': jax.random.normal(ks[1], (B, Sk, DIM_CROSS), jnp.float32), 'wq': jax.random.normal(ks[2], (DIM_EMBED, DIM_EMBED), jnp.float32) * s_e, 'bq': jax.random.normal(ks[3], (DIM_EMBED,), jnp.float32) * 0.01, 'wk': jax.random.normal(ks[4], (DIM_CROSS, DIM_EMBED), jnp.float32) * s_c, 'bk': jax.random.normal(ks[5], (DIM_EMBED,), jnp.float32) * 0.01, 'wv': jax.random.normal(ks[6], (DIM_CROSS, DIM_EMBED), jnp.float32) * s_c, 'bv': jax.random.normal(ks[7], (DIM_EMBED,), jnp.float32) * 0.01, 'wo': jax.random.normal(ks[8], (DIM_EMBED, DIM_EMBED), jnp.float32) * s_e, 'bo': jax.random.normal(ks[9], (DIM_EMBED,), jnp.float32) * 0.01}
    _L1_xattn_all = _L1_xattn_setup()
    _L1_xattn_in = {k: v for k, v in _L1_xattn_all.items() if k in ('wq', 'bq', 'wk', 'bk', 'wv', 'bv', 'wo', 'bo')}
    del _L1_xattn_all

    def _L1_ffn_setup():
        import jax, jax.numpy as jnp
        import numpy as np
        D = 128
        E = 12
        HS = 2 * D
        HR = 3 * D
        TAU = 1.5

        def _geglu(h):
            a, g = jnp.split(h, 2, axis=-1)
            return a * jax.nn.gelu(g, approximate=False)
        key = jax.random.key(seed)
        ks = jax.random.split(key, 12)

        def xavier(k, shape):
            fan_in, fan_out = (shape[-2], shape[-1])
            lim = jnp.sqrt(6.0 / (fan_in + fan_out))
            return jax.random.uniform(k, shape, jnp.float32, -lim, lim)
        x = jax.random.normal(ks[0], (2, 128, D), jnp.float32)
        Ws1 = xavier(ks[1], (D, 2 * HS))
        bs1 = jnp.zeros((2 * HS,), jnp.float32)
        Ws2 = xavier(ks[2], (HS, D))
        bs2 = jnp.zeros((D,), jnp.float32)
        We1 = xavier(ks[3], (E, D, 2 * HR))
        be1 = jnp.zeros((E, 2 * HR), jnp.float32)
        We2 = xavier(ks[4], (E, HR, D))
        be2 = jnp.zeros((E, D), jnp.float32)
        Wr = xavier(ks[5], (D, E))
        br = jnp.zeros((E,), jnp.float32)
        return {'x': x, 'Ws1': Ws1, 'bs1': bs1, 'Ws2': Ws2, 'bs2': bs2, 'We1': We1, 'be1': be1, 'We2': We2, 'be2': be2, 'Wr': Wr, 'br': br}
    _L1_ffn_all = _L1_ffn_setup()
    _L1_ffn_in = {k: v for k, v in _L1_ffn_all.items() if k in ('Ws1', 'bs1', 'Ws2', 'bs2', 'We1', 'be1', 'We2', 'be2', 'Wr', 'br')}
    del _L1_ffn_all
    return {'x': x, 'ctx_768': ctx_768, 'mask_BxS2_bk0': mask_BxS2_bk0, 'g_xattn': g_xattn, 'g_ffn': g_ffn, 'L0_xattn_ln_x_g': _L0_xattn_in['ln_x_g'], 'L0_xattn_ln_x_b': _L0_xattn_in['ln_x_b'], 'L0_xattn_ln_l_g': _L0_xattn_in['ln_l_g'], 'L0_xattn_ln_l_b': _L0_xattn_in['ln_l_b'], 'L0_xattn_qn_g': _L0_xattn_in['qn_g'], 'L0_xattn_kn_g': _L0_xattn_in['kn_g'], 'L0_xattn_Wq': _L0_xattn_in['Wq'], 'L0_xattn_Wkv': _L0_xattn_in['Wkv'], 'L0_xattn_Wlkv': _L0_xattn_in['Wlkv'], 'L0_xattn_Wo': _L0_xattn_in['Wo'], 'L0_xattn_bo': _L0_xattn_in['bo'], 'L0_ffn_Wr': _L0_ffn_in['Wr'], 'L0_ffn_Wg': _L0_ffn_in['Wg'], 'L0_ffn_Wu': _L0_ffn_in['Wu'], 'L0_ffn_Wd': _L0_ffn_in['Wd'], 'L1_xattn_wq': _L1_xattn_in['wq'], 'L1_xattn_bq': _L1_xattn_in['bq'], 'L1_xattn_wk': _L1_xattn_in['wk'], 'L1_xattn_bk': _L1_xattn_in['bk'], 'L1_xattn_wv': _L1_xattn_in['wv'], 'L1_xattn_bv': _L1_xattn_in['bv'], 'L1_xattn_wo': _L1_xattn_in['wo'], 'L1_xattn_bo': _L1_xattn_in['bo'], 'L1_ffn_Ws1': _L1_ffn_in['Ws1'], 'L1_ffn_bs1': _L1_ffn_in['bs1'], 'L1_ffn_Ws2': _L1_ffn_in['Ws2'], 'L1_ffn_bs2': _L1_ffn_in['bs2'], 'L1_ffn_We1': _L1_ffn_in['We1'], 'L1_ffn_be1': _L1_ffn_in['be1'], 'L1_ffn_We2': _L1_ffn_in['We2'], 'L1_ffn_be2': _L1_ffn_in['be2'], 'L1_ffn_Wr': _L1_ffn_in['Wr'], 'L1_ffn_br': _L1_ffn_in['br']}

def reference(x, ctx_768, mask_BxS2_bk0, g_xattn, g_ffn, L0_xattn_ln_x_g, L0_xattn_ln_x_b, L0_xattn_ln_l_g, L0_xattn_ln_l_b, L0_xattn_qn_g, L0_xattn_kn_g, L0_xattn_Wq, L0_xattn_Wkv, L0_xattn_Wlkv, L0_xattn_Wo, L0_xattn_bo, L0_ffn_Wr, L0_ffn_Wg, L0_ffn_Wu, L0_ffn_Wd, L1_xattn_wq, L1_xattn_bq, L1_xattn_wk, L1_xattn_bk, L1_xattn_wv, L1_xattn_bv, L1_xattn_wo, L1_xattn_bo, L1_ffn_Ws1, L1_ffn_bs1, L1_ffn_Ws2, L1_ffn_bs2, L1_ffn_We1, L1_ffn_be1, L1_ffn_We2, L1_ffn_be2, L1_ffn_Wr, L1_ffn_br):
    import jax
    import jax.numpy as jnp

    def _L0_xattn_ref(x, latents, mask, ln_x_g, ln_x_b, ln_l_g, ln_l_b, qn_g, kn_g, Wq, Wkv, Wlkv, Wo, bo):
        import jax, jax.numpy as jnp
        import numpy as np
        DIM_IN, DIM_LAT, DIM_HEAD = (96, 128, 64)
        INNER = max(DIM_LAT, DIM_IN)
        HEADS = INNER // DIM_HEAD
        SCALE = DIM_HEAD ** (-0.5)
        RMS_EPS = 1e-08
        LN_EPS = 1e-05

        def layernorm(x, g, b):
            mu = jnp.mean(x, axis=-1, keepdims=True)
            var = jnp.mean((x - mu) ** 2, axis=-1, keepdims=True)
            return (x - mu) * jax.lax.rsqrt(var + LN_EPS) * g + b

        def rmsnorm(x, gamma):
            norm = jnp.sqrt(jnp.sum(x * x, axis=-1, keepdims=True)) * x.shape[-1] ** (-0.5)
            return x / jnp.maximum(norm, RMS_EPS) * gamma
        b, n, _ = x.shape
        m = latents.shape[1]
        xn = layernorm(x, ln_x_g, ln_x_b)
        ln = layernorm(latents, ln_l_g, ln_l_b)
        q = ln @ Wq.T
        kv = jnp.concatenate([xn @ Wkv.T, ln @ Wlkv.T], axis=1)
        k, v = (kv[..., :INNER], kv[..., INNER:])
        split_heads = lambda t: t.reshape(t.shape[0], t.shape[1], HEADS, DIM_HEAD).transpose(0, 2, 1, 3)
        q, k, v = (split_heads(q), split_heads(k), split_heads(v))
        qn = rmsnorm(q, qn_g) * SCALE
        kn = rmsnorm(k, kn_g)
        attn = jnp.einsum('bhid,bhjd->bhij', qn, kn)
        full_mask = jnp.pad(mask, ((0, 0), (0, m)), constant_values=True)
        attn = jnp.where(full_mask[:, None, None, :], attn, -jnp.finfo(attn.dtype).max)
        attn = jax.nn.softmax(attn, axis=-1)
        out = jnp.einsum('bhij,bhjd->bhid', attn, v)
        out = out.transpose(0, 2, 1, 3).reshape(b, m, INNER)
        return out @ Wo.T + bo

    def _L0_ffn_ref(x, Wr, Wg, Wu, Wd):
        import jax, jax.numpy as jnp
        import numpy as np
        D_MODEL = 128
        HIDDEN = 512
        NUM_EXPERTS = 8
        TOP_K = 2
        DEPTH = 12
        DEPTH_SCALE = 1.0 / np.sqrt(DEPTH)
        B, T, C = x.shape
        flat_x = x.reshape(-1, C)
        logits = flat_x @ Wr
        top_vals, top_idx = jax.lax.top_k(logits, TOP_K)
        rw = jax.nn.softmax(top_vals.astype(jnp.float32), axis=-1).astype(x.dtype)
        combine = jnp.sum(rw[..., None] * jax.nn.one_hot(top_idx, NUM_EXPERTS, dtype=x.dtype), axis=1)
        g = jnp.einsum('nc,ech->neh', flat_x, Wg)
        u = jnp.einsum('nc,ech->neh', flat_x, Wu)
        h = jax.nn.silu(g) * u
        eo = jnp.einsum('neh,ehc->nec', h, Wd) * DEPTH_SCALE
        out = jnp.einsum('ne,nec->nc', combine, eo)
        return out.reshape(B, T, C)

    def _L1_xattn_ref(x, y, wq, bq, wk, bk, wv, bv, wo, bo):
        import jax, jax.numpy as jnp
        import numpy as np
        N_HEADS = 16
        DIM_EMBED = 128
        DIM_CROSS = 96
        DIM_HEAD = DIM_EMBED // N_HEADS
        B, Sq, E = x.shape
        H, D = (N_HEADS, DIM_HEAD)
        q = (x @ wq + bq).reshape(B, Sq, H, D).transpose(0, 2, 1, 3)
        k = (y @ wk + bk).reshape(B, -1, H, D).transpose(0, 2, 1, 3)
        v = (y @ wv + bv).reshape(B, -1, H, D).transpose(0, 2, 1, 3)
        scores = jnp.einsum('bhqd,bhkd->bhqk', q, k) / jnp.sqrt(jnp.asarray(D, x.dtype))
        attn = jax.nn.softmax(scores, axis=-1)
        out = jnp.einsum('bhqk,bhkd->bhqd', attn, v)
        out = out.transpose(0, 2, 1, 3).reshape(B, Sq, E)
        return out @ wo + bo

    def _L1_ffn_ref(x, Ws1, bs1, Ws2, bs2, We1, be1, We2, be2, Wr, br):
        import jax, jax.numpy as jnp
        import numpy as np
        D = 128
        E = 12
        HS = 2 * D
        HR = 3 * D
        TAU = 1.5

        def _geglu(h):
            a, g = jnp.split(h, 2, axis=-1)
            return a * jax.nn.gelu(g, approximate=False)
        B, T, Dm = x.shape
        xf = x.reshape(-1, Dm)
        ys = _geglu(xf @ Ws1 + bs1) @ Ws2 + bs2
        logits = (xf @ Wr + br) / TAU
        top_val, top_idx = jax.lax.top_k(logits, 2)
        top_w = jax.nn.softmax(top_val, axis=-1)
        onehot = jax.nn.one_hot(top_idx, E, dtype=x.dtype)
        w = jnp.einsum('nke,nk->ne', onehot, top_w)
        h = jnp.einsum('nd,edh->enh', xf, We1) + be1[:, None, :]
        act = _geglu(h)
        yE = jnp.einsum('enh,ehd->end', act, We2) + be2[:, None, :]
        yr = jnp.einsum('end,ne->nd', yE, w)
        return (ys + yr).reshape(B, T, Dm)
    x = x + jnp.tanh(g_xattn[0]) * _L0_xattn_ref(ctx_768, _layernorm(x, axis=-1), mask_BxS2_bk0, L0_xattn_ln_x_g, L0_xattn_ln_x_b, L0_xattn_ln_l_g, L0_xattn_ln_l_b, L0_xattn_qn_g, L0_xattn_kn_g, L0_xattn_Wq, L0_xattn_Wkv, L0_xattn_Wlkv, L0_xattn_Wo, L0_xattn_bo)
    x = x + jnp.tanh(g_ffn[0]) * _L0_ffn_ref(_layernorm(x, axis=-1), L0_ffn_Wr, L0_ffn_Wg, L0_ffn_Wu, L0_ffn_Wd)
    x = x + jnp.tanh(g_xattn[1]) * _L1_xattn_ref(_layernorm(x, axis=-1), ctx_768, L1_xattn_wq, L1_xattn_bq, L1_xattn_wk, L1_xattn_bk, L1_xattn_wv, L1_xattn_bv, L1_xattn_wo, L1_xattn_bo)
    x = x + jnp.tanh(g_ffn[1]) * _L1_ffn_ref(_layernorm(x, axis=-1), L1_ffn_Ws1, L1_ffn_bs1, L1_ffn_Ws2, L1_ffn_bs2, L1_ffn_We1, L1_ffn_be1, L1_ffn_We2, L1_ffn_be2, L1_ffn_Wr, L1_ffn_br)
    return x

_drawn_inputs = setup_inputs


def setup_inputs(seed=0):
    import zlib

    import numpy as np

    out = dict(_drawn_inputs(seed))
    spreads = {'g_ffn': (-1.0, 0.6),
     'L0_xattn_ln_x_g': (1.0, 0.6),
     'L0_xattn_ln_x_b': (0.0, 0.711),
     'L0_xattn_ln_l_g': (1.0, 0.2),
     'L0_xattn_ln_l_b': (0.0, 0.1),
     'L0_xattn_qn_g': (1.0, 0.6),
     'L0_xattn_kn_g': (1.0, 0.6),
     'L0_xattn_bo': (0.0, 0.1),
     'L1_ffn_bs1': (0.0, 0.1),
     'L1_ffn_bs2': (0.0, 0.1),
     'L1_ffn_be1': (0.0, 0.28),
     'L1_ffn_be2': (0.0, 0.1),
     'L1_ffn_br': (0.0, 0.1)}
    factors = {'L1_xattn_bq': 8.0, 'L1_xattn_bk': 8.0, 'L1_xattn_bv': 4.445, 'L1_xattn_bo': 4.293}
    for name, (base, spread) in spreads.items():
        noise = np.random.default_rng([zlib.crc32(name.encode()), seed]).standard_normal(out[name].shape)
        drawn = base * np.exp(spread * noise) if base else spread * noise
        out[name] = jnp.asarray(drawn.astype(out[name].dtype))
    for name, factor in factors.items():
        out[name] = (out[name] * factor).astype(out[name].dtype)
    return out
```

```python
from contextlib import ExitStack

import concourse.bass as bass
from concourse import mybir
from concourse.alu_op_type import AluOpType as ALU

ACT = mybir.ActivationFunctionType
AX = mybir.AxisListType
F32 = mybir.dt.float32
F32R = mybir.dt.float32r
U8 = mybir.dt.uint8
I32 = mybir.dt.int32

P = 128
B, S, D = 2, 512, 128
T = B * S // P
TB = S // P
N = B * S
CK, DC = 154, 96
KR = CK - P
H0, HD0 = 2, 64
H1, HD1 = 16, 8
G1 = 4
E0, E1 = 8, 12
LN_EPS = 1e-5
RMS_EPS2 = 1e-16
TAU = 1.5
DEPTH_SCALE = 1.0 / 12 ** 0.5
BIG = 1e30
LO = 16

BANKS = 8
COLS = 512


class Layer:

    def __init__(self, experts, blocks, function, shared_blocks):
        self.experts, self.blocks, self.function = experts, blocks, function
        self.shared_blocks = shared_blocks
        self.pairs = experts // 2
        self.steps = 4 * blocks
        self.all_experts = experts + (1 if shared_blocks else 0)

    def place(self, s, last):
        if last and s >= self.steps and self.shared_blocks:
            r = s - self.steps
            return 4 + r // self.shared_blocks, r % self.shared_blocks, self.shared_blocks
        return s // self.blocks, s % self.blocks, self.blocks

    def last_steps(self):
        return self.steps + 2 * self.shared_blocks


def flamingo(nc, A, out):
    with ExitStack() as ctx:
        def sb(name, shape, dt=F32):
            return ctx.enter_context(nc.sbuf_tensor(name, shape, dt))

        def sem(name):
            return ctx.enter_context(nc.semaphore(name))

        xres = sb("xres", [P, T, D])
        z = sb("z", [P, T, D])
        zT = sb("zT", [P, N])
        ident = sb("ident", [P, P])
        sel = sb("sel", [P, 13, P], F32R)
        rev = sb("rev", [P, 16])
        revi = sb("revi", [P, 16], I32)
        zero = sb("zero", [P, 1])
        half = sb("half", [P, 32])
        stats = sb("stats", [P, T, 6])
        mv = sb("mv", [P, T, 2])
        rstd = sb("rstd", [P, T])
        cstats = sb("cstats", [P, 4, 6])
        cmv = sb("cmv", [P, 4, 2])
        crstd = sb("crstd", [P, 4])
        ctx_rows = sb("ctx_rows", [P, 4, DC])
        ctx_z = sb("ctx_z", [P, 4, DC])
        cT = sb("cT", [DC, 4, P])
        rT = sb("rT", [DC, 4, P])
        gates = sb("gates", [P, 4])
        tg = sb("tg", [P, 4])
        colv = sb("colv", [P, 4])
        gq = sb("gq", [P, HD0])
        gk = sb("gk", [P, HD0])
        gqk = sb("gqk", [P, HD0])
        bo0 = sb("bo0", [P, D])
        b1 = sb("b1", [P, 4, D])
        br = sb("br", [P, E1])
        wr0 = sb("wr0", [P, E0])
        wr1 = sb("wr1", [P, E1])
        wq0 = sb("wq0", [P, P])
        wlkv = sb("wlkv", [P, 2, P])
        wkv = sb("wkv", [P, 2, DC])
        wo0 = sb("wo0", [P, P])
        wcat = sb("wcat", [P, 3 * P])
        wkvT = sb("wkvT", [DC, 2 * P])
        woT = sb("woT", [P, P])
        w1 = sb("w1", [P, 2, P])
        w1c = sb("w1c", [DC, 2, P])
        beR = sb("beR", [P, P])
        beT = sb("beT", [P, 76])
        be2 = sb("be2", [P, P])
        mask8 = sb("mask8", [P, B * CK], U8)
        maskB = sb("maskB", [P, B, CK])
        mcol8 = sb("mcol8", [P, 4], U8)
        mcol = sb("mcol", [P, 4])
        pad1 = sb("pad1", [P, 1])
        qkv = sb("qkv", [P, T, 3 * P])
        ckv = sb("ckv", [P, 4, 2 * P])
        ss = sb("ss", [P, T, 4])
        rn = sb("rn", [P, T, 4])
        css = sb("css", [P, 4, 2])
        crn = sb("crn", [P, 4, 2])
        stage = sb("stage", [P, 6144])
        q_s = sb("q_s", [P, 4096], F32R)
        k_a = sb("k_a", [P, 5120], F32R)
        k_b = sb("k_b", [P, 1024], F32R)
        v_a = sb("v_a", [P, 4352])
        v_b = sb("v_b", [P, 1280])
        probs = sb("probs", [P, 4, COLS])
        mx = sb("mx", [P, T, 32])
        mtmp = sb("mtmp", [P, 2, 160])
        small = sb("small", [P, 16, T * 12])
        comb_st = sb("comb_st", [P, T, P])
        combT = sb("combT", [P, N], F32R)
        comb_w = sb("comb_w", [P, T, 13])
        biases = sb("biases", [P, 2, 6])
        selp = sb("selp", [P, 2, P], F32R)
        selpk = sb("selpk", [P, P], F32R)
        raw = sb("raw", [P, 2, 1536])
        wh = sb("wh", [P, 2, 1536], F32R)
        wl = sb("wl", [P, 2, 1536], F32R)
        zh, zl = q_s[:, 0:N], q_s[:, N:2 * N]
        hh = q_s[:, 2 * N:3 * N].rearrange("p (a n) -> p a n", a=2)
        hl = q_s[:, 3 * N:4 * N].rearrange("p (a n) -> p a n", a=2)
        act_out = qkv[:, :, :].rearrange("p t c -> p (t c)")[:, 0:N].rearrange("p (a n) -> p a n", a=2)
        yT = qkv[:, :, :].rearrange("p t c -> p (t c)")[:, 2 * N:3 * N]
        oT = zT
        cbs = probs[:, 0:2, :]
        ytmp = probs[:, 2:4, :]
        rcp = act_out
        ps = ctx.enter_context(nc.psum_tensor("ps", [P, BANKS, COLS], F32))

        dve_link, act_link, pool_link = sem("dve_link"), sem("act_link"), sem("pool_link")
        x_in, ctx_in, w0_in, vec_in, w1_in = (sem(n) for n in ("x_in", "ctx_in", "w0_in", "vec_in", "w1_in"))
        const_ready, zeroed = sem("const_ready"), sem("zeroed")
        var_ready, rstd_ready, z_ready, zT_psum, zT_ready = (
            sem(n) for n in ("var_ready", "rstd_ready", "z_ready", "zT_psum", "zT_ready"))
        gate_ready = sem("gate_ready")
        wT_psum, wT_ready, cT_psum, cT_ready, cz_ready = (
            sem(n) for n in ("wT_psum", "wT_ready", "cT_psum", "cT_ready", "cz_ready"))
        proj_psum, proj_used, cproj_psum, cproj_used = (
            sem(n) for n in ("proj_psum", "proj_used", "cproj_psum", "cproj_used"))
        ss_ready, rn_ready = sem("ss_ready"), sem("rn_ready")
        staged, turn_psum, turned_a, turned_v = (sem(n) for n in ("staged", "turn_psum", "turned_a", "turned_v"))
        kv_ready = sem("kv_ready")
        mx_psum, mx_used, zh_ready, zl_ready = (sem(n) for n in ("mx_psum", "mx_used", "zh_ready", "zl_ready"))
        q1_psum, kv1_psum, k1_staged, k1_psum, k1_ready, q1_staged, q1_turned = (
            sem(n) for n in ("q1_psum", "kv1_psum", "k1_staged", "k1_psum", "k1_ready", "q1_staged", "q1_turned"))
        q1_turn_psum, q1_full_psum, q1_full, mx1_psum, mx1_used, shift1_staged = (
            sem(n) for n in ("q1_turn_psum", "q1_full_psum", "q1_full", "mx1_psum", "mx1_used", "shift1_staged"))
        beT_psum, beT_ready, yinit_psum, y_init = (sem(n) for n in ("beT_psum", "beT_ready", "yinit_psum", "y_init"))
        shift_staged, shift_psum, shift_ready = sem("shift_staged"), sem("shift_psum"), sem("shift_ready")
        scores_ready, probs_ready, pv_done = sem("scores_ready"), sem("probs_ready"), sem("pv_done")
        oT_ready, o_psum, res_ready = sem("oT_ready"), sem("o_psum"), sem("res_ready")
        route_psum, gap_ready, e_ready, comb_staged, comb_psum, comb_ready = (
            sem(n) for n in ("route_psum", "gap_ready", "e_ready", "comb_staged", "comb_psum", "comb_ready"))
        y_turned, y_added, out_done = sem("y_turned"), sem("y_added"), sem("out_done")
        ffn_sem = [{n: sem(f"{n}_{i}") for n in (
            "w_in_a", "w_in_b", "w_high", "w_split", "g_ready", "u_ready", "act_ready", "hid_ready", "hh_ready",
            "hl_ready", "down_done", "y_used", "y_summed", "c_ready", "c_copied")} for i in range(2)]
        HEAD_START = {"hid_ready": 1, "hl_ready": 2, "down_done": 2, "y_used": 2, "c_copied": 2}

        LAYERS = [Layer(E0, 4, ACT.Silu, 0), Layer(E1, 3, ACT.Gelu, 2)]

        def bcast(ap, *shape):
            return ap.broadcast_to(list(shape))

        def linked(eng, link):
            count = [0]

            def do(ins, wait=True):
                count[0] += 1
                ins.then_inc(link, 1)
                if wait:
                    eng.wait_ge(link, count[0])
            return do

        st_q0 = stage[:, 0:2048].rearrange("p (t h c) -> p t h c", t=T, h=H0)
        st_k0 = stage[:, 2048:6144].rearrange("p (s t h c) -> p s t h c", s=2, t=T, h=H0)
        st_c0 = [x[:, :, :].rearrange("p a (m h c) -> p (a m) h c", m=2, h=H0) for x in (hh, hl)]
        q_s0 = q_s[:, 0:2048].rearrange("p (h n) -> p h n", h=H0)
        k_a0 = k_a[:, :].rearrange("p (s b h k) -> p s b h k", s=2, b=B, h=H0)
        k_b0 = k_b[:, :].rearrange("p (s b h k) -> p s b h k", s=2, b=B, h=H0)
        v_a0 = v_a[:, 0:2560].rearrange("p (t h c) -> p t h c", h=H0, c=P)
        v_b0 = v_b[:, 0:512].rearrange("p (b h c) -> p b h c", b=B, h=H0)
        st_q1 = stage[:, 0:4096].rearrange("p (t h c) -> p t h c", t=T, h=H1)
        st_k1 = stage[:, 4096:6144].rearrange("p (m h c) -> p m h c", m=4, h=H1)
        q_s1 = q_s[:, :].rearrange("p (g n) -> p g n", g=G1)
        k_a1 = k_a[:, 0:4096].rearrange("p (b g j k) -> p b g j k", b=B, g=G1, j=4)
        k_b1 = k_b[:, :].rearrange("p (b g k) -> p b g k", b=B, g=G1)
        v_a1 = v_a[:, :].rearrange("p (b a c) -> p b a c", b=B, a=2)
        v_b1 = v_b[:, :].rearrange("p (b a c) -> p b a c", b=B, a=2)

        block = ctx.enter_context(nc.Block())

        @block.sync
        def _(sp):
            x_rows = A["x"].rearrange("b (t p) d -> p (b t) d", p=P)
            sp.dma_start(xres[:, :, :], x_rows).then_inc(x_in, 16)
            sp.dma_start(ctx_rows[:, 0:2, :], A["ctx_768"][:, 0:P, :].rearrange("b p c -> p b c")).then_inc(ctx_in, 16)
            sp.dma_start(ctx_rows[0:KR, 2:4, :],
                         A["ctx_768"][:, P:CK, :].rearrange("b p c -> p b c")).then_inc(ctx_in, 16)
            for dst, src in (
                    (wq0[:, :], A["L0_xattn_Wq"]),
                    (wlkv[:, :, :], A["L0_xattn_Wlkv"].rearrange("(a p) c -> p a c", p=P)),
                    (wkv[:, :, :], A["L0_xattn_Wkv"].rearrange("(a p) c -> p a c", p=P)),
                    (wo0[:, :], A["L0_xattn_Wo"])):
                sp.dma_start(dst, src).then_inc(w0_in, 16)
            for dst, src in (
                    (colv[:, 0:1], A["L0_xattn_ln_l_g"].unsqueeze(1)), (colv[:, 1:2], A["L0_xattn_ln_l_b"].unsqueeze(1)),
                    (colv[0:DC, 2:3], A["L0_xattn_ln_x_g"].unsqueeze(1)),
                    (colv[0:DC, 3:4], A["L0_xattn_ln_x_b"].unsqueeze(1)),
                    (gates[:, 0:2], A["g_xattn"].partition_broadcast(P)),
                    (gates[:, 2:4], A["g_ffn"].partition_broadcast(P)),
                    (gq[:, :], A["L0_xattn_qn_g"].partition_broadcast(P)),
                    (gk[:, :], A["L0_xattn_kn_g"].partition_broadcast(P)),
                    (mask8[:, :], A["mask_BxS2_bk0"].rearrange("b k -> (b k)").partition_broadcast(P)),
                    (bo0[:, :], A["L0_xattn_bo"].partition_broadcast(P)),
                    (wr0[:, :], A["L0_ffn_Wr"])):
                sp.dma_start(dst, src).then_inc(vec_in, 16)
            sp.wait_ge(const_ready, 1)
            for b in range(B):
                sp.dma_start(mcol8[:, b:b + 1], A["mask_BxS2_bk0"][b, 0:P].unsqueeze(1)).then_inc(vec_in, 16)
                for j in range(H0):
                    sp.dma_start(mcol8[64 * j:64 * j + KR, 2 + b:3 + b],
                                 A["mask_BxS2_bk0"][b, P:CK].unsqueeze(1)).then_inc(vec_in, 16)

            def expert_loads(layer, e, b):
                into = ffn_sem[layer][("w_in_a", "w_in_b")[b]]
                w = LAYERS[layer].blocks * P
                if layer == 0:
                    srcs = [A["L0_ffn_Wg"][e, :, :].rearrange("a p n -> p (a n)"),
                            A["L0_ffn_Wu"][e, :, :].rearrange("a p n -> p (a n)")]
                    sp.dma_start(raw[:, b, 0:w], srcs[0]).then_inc(into, 16)
                    sp.dma_start(raw[:, b, w:2 * w], srcs[1]).then_inc(into, 16)
                    down = A["L0_ffn_Wd"][e, :, :]
                else:
                    sp.dma_start(raw[:, b, 0:2 * w], A["L1_ffn_We1"][e, :, :].rearrange("a p n -> p (a n)")).then_inc(into, 32)
                    down = A["L1_ffn_We2"][e, :, :]
                sp.dma_start(raw[:, b, 2 * w:3 * w].rearrange("p (c n) -> p c n", n=P),
                             down.rearrange("a (c p) n -> p (a c) n", p=P)).then_inc(into, 16)

            def layer_loads(layer):
                L, q = LAYERS[layer], ffn_sem[layer]
                if layer == 1:
                    sp.wait_ge(ffn_sem[0]["w_split"], E0)
                for b in range(2):
                    expert_loads(layer, slice(b, b + 1), b)
                with sp.Fori(1, L.pairs) as k:
                    for b in range(2):
                        sp.wait_ge(q["w_split"], 2 * k + b - 1)
                        expert_loads(layer, bass.ds(2 * k + b, 1), b)

            layer_loads(0)
            sp.wait_ge(const_ready, 7)
            for dst, src in (
                    (w1[:, 0, :], A["L1_xattn_wq"]), (w1[:, 1, :], A["L1_xattn_wo"]),
                    (w1c[:, 0, :], A["L1_xattn_wk"]), (w1c[:, 1, :], A["L1_xattn_wv"]),
                    (b1[:, 0, :], A["L1_xattn_bq"].partition_broadcast(P)),
                    (b1[:, 1, :], A["L1_xattn_bk"].partition_broadcast(P)),
                    (b1[:, 2, :], A["L1_xattn_bv"].partition_broadcast(P)),
                    (b1[:, 3, :], A["L1_xattn_bo"].partition_broadcast(P)),
                    (br[:, :], A["L1_ffn_br"].partition_broadcast(P)),
                    (wr1[:, :], A["L1_ffn_Wr"]),
                    (beR[0:72, :], A["L1_ffn_be1"].rearrange("e (c n) -> (e c) n", n=P)),
                    (beR[72:76, :], A["L1_ffn_bs1"].rearrange("(c n) -> c n", n=P)),
                    (be2[0:E1, :], A["L1_ffn_be2"]), (be2[LO:LO + E1, :], A["L1_ffn_be2"]),
                    (be2[E1:E1 + 1, :], A["L1_ffn_bs2"].unsqueeze(0)),
                    (be2[LO + E1:LO + E1 + 1, :], A["L1_ffn_bs2"].unsqueeze(0))):
                sp.dma_start(dst, src).then_inc(w1_in, 16)
            layer_loads(1)
            sp.wait_ge(ffn_sem[1]["w_split"], E1 - 1)
            sp.dma_start(raw[:, 0, 0:4 * P], A["L1_ffn_Ws1"]).then_inc(ffn_sem[1]["w_in_a"], 32)
            sp.dma_start(raw[:, 0, 4 * P:6 * P].rearrange("p (c n) -> p c n", n=P),
                         A["L1_ffn_Ws2"].rearrange("(c p) n -> p c n", p=P)).then_inc(ffn_sem[1]["w_in_a"], 16)
            for m in range(2):
                sp.wait_ge(y_added, 2 + m + 1)
                sp.dma_start(out.rearrange("b (t p) d -> p (b t) d", p=P)[:, 4 * m:4 * m + 4, :],
                             xres[:, 4 * m:4 * m + 4, :]).then_inc(out_done, 16)
            sp.wait_ge(out_done, 32)

        N_W0, N_VEC, N_W1 = 4 * 16, (11 + 6) * 16, 16 * 16

        def turned_to0(i):
            if i < 4:
                h, c = divmod(i, 2)
                return q_s0[:, h, c * COLS:(c + 1) * COLS].rearrange("p (a k) -> p a k", a=4)
            if i < 12:
                part, b, h = (i - 4) // 4, (i - 4) // 2 % 2, (i - 4) % 2
                return k_a0[:, part, b, h, P:5 * P].rearrange("p (a k) -> p a k", a=4)
            part, packed = divmod(i - 12, 2)
            dst = k_b0[:, part, :, :, :] if packed else k_a0[:, part, :, :, 0:P]
            return dst

        def turned_from0(i, a):
            if i < 4:
                h, c = divmod(i, 2)
                return st_q0[:, 4 * c + a, h, :]
            if i < 12:
                part, b, h = (i - 4) // 4, (i - 4) // 2 % 2, (i - 4) % 2
                return st_k0[:, part, 4 * b + a, h, :]
            part, packed = divmod(i - 12, 2)
            b, h = divmod(a, 2)
            return st_c0[part][:, 2 * packed + b, h, :].bitcast(F32)

        def turned_bank0(i):
            shape = "p (a k) -> p a k" if i < 12 else "p (b h k) -> p b h k"
            return ps[:, i % 8, :].rearrange(shape, k=P, **({} if i < 12 else {"b": B}))

        def row_scores1(pe, t):
            b = t // TB
            pe.wait_ge(q1_turned, t + 1)
            for g in range(G1 + 1):
                if t >= 1 and g < G1:
                    pe.wait_ge(mx1_used, 5 * (t - 1) + g + 1)
                if t >= 2 and g == G1:
                    pe.wait_ge(mx1_used, 5 * (t - 1))
                if g < G1:
                    pe.matmul(ps[:, g, :], q_s1[:, g, t * P:(t + 1) * P],
                              k_a1[:, b, g, :, :].rearrange("p j k -> p (j k)"), start=True, stop=True)\
                        .then_inc(mx1_psum, 1)
                    continue
                for gg in range(G1):
                    last = pe.matmul(ps[:, 4 + t % 2, gg * P:(gg + 1) * P], q_s1[:, gg, t * P:(t + 1) * P],
                                     k_b1[:, b, gg, :], start=True, stop=True)
                last.then_inc(mx1_psum, 1)

        @block.gpsimd
        def _(pool):
            do = linked(pool, pool_link)
            pool.memset(mcol8[:, :], 0).then_inc(const_ready, 1)
            pool.memset(zero[:, :], 0.0)
            pool.memset(half[:, :], -0.5).then_inc(const_ready, 1)
            do(pool.memset(ident[:, :], 0.0))
            pool.affine_select(out=ident[:, :], in_=ident[:, :], compare_op=ALU.not_equal, fill=1.0, base=0,
                               pattern=[[-1, P]], channel_multiplier=1).then_inc(const_ready, 1)
            pool.memset(comb_st[:, :, :], 0.0).then_inc(zeroed, 1)
            pool.memset(cT[:, 2:4, :], 0.0).then_inc(zeroed, 1)
            pool.memset(rT[:, 2:4, :], 0.0).then_inc(zeroed, 1)
            for q in ffn_sem:
                for name, count in HEAD_START.items():
                    pool.sem_inc(q[name], count)

            def power(count, dst, exponents, x=None):
                pool.wait_ge(var_ready, count)
                pool.tensor_tensor(dst, dst if x is None else x, exponents, ALU.pow).then_inc(rstd_ready, 1)

            pool.wait_ge(const_ready, 3)
            power(1, crstd[:, :], half[:, 0:4])
            power(2, rstd[:, :], half[:, 0:T])
            for x in (hh, hl):
                pool.memset(x[:, :, :].bitcast(F32), 0.0).then_inc(zeroed, 1)
            pool.memset(v_a[:, 0:2560], 1.0).then_inc(zeroed, 1)
            pool.memset(v_b[:, :], 0.0).then_inc(zeroed, 1)
            power(3, crn[:, :, :], half[:, 0:8].rearrange("p (a b) -> p a b", a=4), css[:, :, :])
            power(4, rn[:, :, :], half[:, :].rearrange("p (a b) -> p a b", a=T), ss[:, :, :])
            selF = probs[:, :, :].rearrange("p a n -> p (a n)")[:, 0:13 * P].rearrange("p (e m) -> p e m", e=13)
            do(pool.memset(selF, 0.0))
            for base in (0, -LO):
                do(pool.affine_select(out=selF, in_=selF, compare_op=ALU.not_equal, fill=1.0, base=base,
                                      pattern=[[-1, 13], [0, P]], channel_multiplier=1))
            do(pool.tensor_copy(sel[:, :, :], selF))
            for h in range(H0):
                last = pool.tensor_copy(selpk[:, 64 * h:64 * h + 64], sel[:, h, 0:64].bitcast(F32))
            last.then_inc(const_ready, 1)
            do(pool.iota(revi[:, :], pattern=[[-1, 16]], base=12, channel_multiplier=0))
            pool.tensor_copy(rev[:, :], revi[:, :]).then_inc(const_ready, 1)
            do(pool.memset(pad1[:, :], 0.0))
            for j in range(4):
                rows = pad1[32 * j:32 * j + 32, :]
                do(pool.affine_select(out=rows, in_=rows, compare_op=ALU.is_ge, fill=-BIG, base=KR - 1,
                                      pattern=[[0, 1]], channel_multiplier=-1))
            pool.memset(beR[:, :], 0.0).then_inc(const_ready, 1)
            pool.memset(be2[:, :], 0.0).then_inc(const_ready, 1)

            def ffn(layer, between):
                L, q = LAYERS[layer], ffn_sem[layer]
                width = 3 * L.blocks * P

                def split(e, k, b, w):
                    pool.wait_ge(q[("w_in_a", "w_in_b")[b]], 48 * (k + 1))
                    pool.tensor_tensor(wh[:, b, 0:w], raw[:, b, 0:w], zero[:, 0:1].broadcast_to([P, w]), ALU.add)\
                        .then_inc(q["w_high"], 1)
                    expert = slice(e, e + 1) if isinstance(e, int) else bass.ds(e, 1)
                    pool.tensor_copy(selp[:, b:b + 1, :], sel[:, expert, :])
                    if layer == 1:
                        cols = slice(6 * e, min(6 * e + 6, 76)) if isinstance(e, int) else bass.ds(6 * e, 6)
                        pool.tensor_copy(biases[:, b, 0:4 if isinstance(e, int) and e == E1 else 6], beT[:, cols])
                    pool.wait_ge(q["w_high"], e + 1)
                    pool.tensor_tensor(wl[:, b, 0:w], raw[:, b, 0:w], wh[:, b, 0:w].bitcast(F32),
                                       ALU.subtract).then_inc(q["w_split"], 1)

                def add_y(m, n):
                    pool.wait_ge(q["y_used"], m + 3)
                    pool.wait_ge(q["y_summed"], m + 1)
                    part = yT[:, n * COLS:(n + 1) * COLS]
                    pool.tensor_tensor(part, part, ytmp[:, n, :], ALU.add).then_inc(q["y_summed"], 1)

                if layer == 1:
                    pool.wait_ge(beT_ready, 1)
                    pool.wait_ge(ffn_sem[0]["down_done"], LAYERS[0].pairs * LAYERS[0].steps + 2)
                for e in range(2):
                    split(e, 0, e, width)
                between()
                with pool.Fori(0, L.pairs - 1) as k:
                    for b in range(2):
                        for n in range(2):
                            add_y(4 * k + 2 * b + n, n)
                        pool.wait_ge(q["down_done"], L.steps * k + (b + 1) * 2 * L.blocks + 2)
                        split(2 * k + 2 + b, k + 1, b, width)
                k = L.pairs - 1
                for b in range(2):
                    for n in range(2):
                        add_y(4 * k + 2 * b + n, n)
                    if b == 0 and L.shared_blocks:
                        pool.wait_ge(q["down_done"], L.steps * k + 2 * L.blocks + 2)
                        split(2 * k + 2, k + 1, 0, 3 * L.shared_blocks * P)
                if L.shared_blocks:
                    for n in range(2):
                        add_y(4 * k + 4 + n, n)

            def before_layer0():
                power(5, rstd[:, :], half[:, 0:T])
                do(pool.memset(yT[:, :], 0.0))
                pool.sem_inc(ffn_sem[0]["y_summed"], 2)
                pool.memset(stage[:, :], 0.0).then_inc(zeroed, 1)
                pool.memset(v_a[:, :], 0.0).then_inc(zeroed, 1)
                pool.memset(v_b[:, :], 0.0).then_inc(zeroed, 1)
                pool.memset(k_a[:, :].bitcast(F32), 0.0).then_inc(zeroed, 1)

            def before_layer1():
                power(7, rstd[:, :], half[:, 0:T])
                pool.wait_ge(y_init, 2)
                pool.sem_inc(ffn_sem[1]["y_summed"], 2)

            ffn(0, before_layer0)
            power(6, rstd[:, :], half[:, 0:T])
            ffn(1, before_layer1)

        @block.scalar
        def _(act):
            def copy(dst, src):
                return act.activation(dst, src, ACT.Copy)

            def ffn(layer):
                L, q = LAYERS[layer], ffn_sem[layer]

                def gate(k, s, last):
                    u, j, blocks = L.place(s, last)
                    g = L.steps * k + s
                    act.wait_ge(q["g_ready"], g + 1)
                    act.wait_ge(q["hid_ready"], max(g, 1) if isinstance(g, int) else g)
                    bias = 0.0
                    if layer == 1:
                        act.wait_ge(q["w_split"], 2 * k + u // 2 + 1)
                        bias = biases[:, (u // 2) % 2, blocks + j:blocks + j + 1]
                    act.activation(act_out[:, s % 2, :], ps[:, s % 2, :], L.function, bias=bias)\
                        .then_inc(q["act_ready"], 1)

                def high(k, s, last):
                    u, j, blocks = L.place(s, last)
                    g = L.steps * k + s
                    act.wait_ge(q["hid_ready"], g + 2)
                    act.wait_ge(q["down_done"], g + 1)
                    copy(hh[:, s % 2, :], ps[:, 2 + s % 4, :]).then_inc(q["hh_ready"], 1)
                    if j == 0:
                        m, n = 4 * k + u, u % 2
                        act.wait_ge(q["c_ready"], m + 1)
                        act.wait_ge(q["y_used"], m + 1)
                        copy(cbs[:, n, :], ps[:, 6 + n, :]).then_inc(q["c_copied"], 1)

                gate(0, 0, False)
                with act.Fori(0, L.pairs - 1) as k:
                    for s in range(L.steps):
                        gate(k, s + 1, False)
                        high(k, s, False)
                k = L.pairs - 1
                for s in range(L.last_steps()):
                    if s + 1 < L.last_steps():
                        gate(k, s + 1, True)
                    high(k, s, True)

            def exponentials(units, base, bias_of):
                for u in range(units):
                    act.wait_ge(scores_ready, base + u + 1)
                    if u >= 4:
                        act.wait_ge(pv_done, base + u - 3)
                    act.activation(probs[:, u % 4, :], ps[:, u % 4, :], ACT.Exp, bias=bias_of(u))\
                        .then_inc(probs_ready, 1)

            def turned_tokens(count, first_bank, parts):
                for m in range(2):
                    act.wait_ge(zT_psum, count + m + 1)
                    cols = slice(m * COLS, (m + 1) * COLS)
                    copy(zT[:, cols], ps[:, first_bank + m, :]).then_inc(zT_ready, 1)
                    if parts:
                        copy(zh[:, cols], ps[:, first_bank + m, :]).then_inc(zh_ready, 1)

            def gap_exponential(count):
                act.wait_ge(gap_ready, count)
                act.activation(small[:, 15, 0:T], small[:, 15, 0:T], ACT.Exp).then_inc(e_ready, 1)

            def combine_columns(count):
                for m in range(2):
                    act.wait_ge(comb_psum, count + m + 1)
                    copy(combT[:, m * COLS:(m + 1) * COLS], ps[:, 5 + m, :]).then_inc(comb_ready, 1)

            act.wait_ge(vec_in, N_VEC)
            act.activation(tg[:, :], gates[:, :], ACT.Tanh).then_inc(gate_ready, 1)
            act.wait_ge(wT_psum, 1)
            copy(wcat[:, :], ps[:, 2, 0:3 * P])
            copy(wkvT[:, :], ps[0:DC, 3, 0:2 * P])
            copy(woT[:, :], ps[:, 3, 2 * P:3 * P]).then_inc(wT_ready, 1)
            act.wait_ge(cT_psum, 1)
            act.wait_ge(zeroed, 3)
            gain, shift = colv[0:DC, 2:3], colv[0:DC, 3:4]
            act.activation(cT[:, 0:2, :], ps[0:DC, 4, 0:2 * P].rearrange("p (b k) -> p b k", b=B), ACT.Identity,
                           scale=gain, bias=shift)
            copy(rT[:, 0:2, :], ps[0:DC, 5, 0:2 * P].rearrange("p (b k) -> p b k", b=B))
            for b in range(B):
                left = slice(2 * P + 32 * b, 2 * P + 32 * b + KR)
                for j in range(H0):
                    act.activation(cT[:, 2 + b, 64 * j:64 * j + KR], ps[0:DC, 4, left], ACT.Identity,
                                   scale=gain, bias=shift)
                for j in range(4):
                    last = copy(rT[:, 2 + b, 32 * j:32 * j + KR], ps[0:DC, 5, left])
            last.then_inc(cT_ready, 1)
            for m in range(2):
                act.wait_ge(zT_psum, m + 1)
                act.activation(zT[:, m * COLS:(m + 1) * COLS], ps[:, m, :], ACT.Identity,
                               scale=colv[:, 0:1], bias=colv[:, 1:2]).then_inc(zT_ready, 1)
            act.wait_ge(cproj_psum, 1)
            for m in range(2):
                copy(ckv[:, 2 * m:2 * m + 2, :], ps[:, 6 + m, :].rearrange("p (b c) -> p b c", b=B))\
                    .then_inc(cproj_used, 1)
            for t in range(T):
                act.wait_ge(proj_psum, t + 1)
                copy(qkv[:, t, :], ps[:, t % 4, 0:3 * P]).then_inc(proj_used, 1)
            act.wait_ge(zeroed, 7)
            act.wait_ge(proj_used, T)
            for b in range(B):
                for h in range(H0):
                    vals = slice(2 * P + HD0 * h, 2 * P + HD0 * h + HD0)
                    copy(v_a0[:, 5 * b + 1:5 * b + 5, h, 0:HD0], qkv[:, TB * b:TB * b + TB, vals])
            act.wait_ge(cproj_used, 2)
            for b in range(B):
                copy(v_a0[:, 5 * b, :, 0:HD0], ckv[:, b, P:2 * P].rearrange("p (h c) -> p h c", h=H0))
                for h in range(H0):
                    rows = slice(64 * h, 64 * h + 64)
                    last = copy(v_b0[rows, b, h, 0:HD0], ckv[rows, 2 + b, P + HD0 * h:P + HD0 * h + HD0])
            last.then_inc(kv_ready, 1)
            for i in range(0, 16, 2):
                act.wait_ge(turn_psum, i + 1)
                copy(turned_to0(i), turned_bank0(i)).then_inc(turned_a, 1)
            for m in range(2):
                act.wait_ge(shift_psum, m + 1)
                copy(combT[:, m * COLS:(m + 1) * COLS], ps[:, m, :]).then_inc(shift_ready, 1)

            def bias0(u):
                b, r = divmod(u, 11)
                if r == 10:
                    return mcol[:, 2 + b:3 + b]
                return mcol[:, b:b + 1] if r % 5 == 0 else 0.0

            exponentials(22, 0, bias0)

            turned_tokens(2, 2, True)
            gap_exponential(1)
            combine_columns(0)
            ffn(0)

            act.wait_ge(beT_psum, 1)
            copy(beT[:, :], ps[:, 7, 0:76]).then_inc(beT_ready, 1)
            turned_tokens(4, 0, False)
            def queries(done, t):
                copy(q_s1[:, :, t * P:(t + 1) * P], ps[:, 6 if done is q1_turned else 7, :]
                     .rearrange("p (g k) -> p g k", g=G1)).then_inc(done, 1)

            for t in range(T + 1):
                if t < T:
                    act.wait_ge(q1_turn_psum, t + 1)
                    queries(q1_turned, t)
                if t >= 2:
                    act.wait_ge(q1_full_psum, t - 1)
                    queries(q1_full, t - 2)
            act.wait_ge(q1_full_psum, T)
            queries(q1_full, T - 1)
            exponentials(40, 22, lambda u: pad1[:, :] if u % 5 == 4 else 0.0)

            turned_tokens(6, 2, True)
            gap_exponential(2)
            combine_columns(2)
            for m in range(2):
                act.wait_ge(yinit_psum, m + 1)
                copy(yT[:, m * COLS:(m + 1) * COLS], ps[:, (4, 7)[m], :]).then_inc(y_init, 1)
            ffn(1)

        @block.tensor
        def _(pe):
            def turn(dst, src, rows=P):
                return pe.transpose(dst, src, ident[0:rows, 0:rows])

            def ffn(layer):
                L, q = LAYERS[layer], ffn_sem[layer]

                def up(k, s, last):
                    u, j, blocks = L.place(s, last)
                    g = L.steps * k + s
                    e, b, n = 2 * k + u // 2, (u // 2) % 2, u % 2
                    if j == 0 and n == 0:
                        pe.wait_ge(q["w_split"], e + 1)
                    if not isinstance(g, int) or g >= 2:
                        pe.wait_ge(q["act_ready"], g - 1)
                        pe.wait_ge(q["hl_ready"], g - 1)
                    cols = slice(n * COLS, (n + 1) * COLS)
                    for bank, at, done in ((s % 2, layer, "g_ready"), (2 + s % 4, 1 - layer, "u_ready")):
                        w = slice((at * blocks + j) * P, (at * blocks + j + 1) * P)
                        pe.matmul(ps[:, bank, :], wl[:, b, w], zh[:, cols], start=True, stop=False)
                        pe.matmul(ps[:, bank, :], wh[:, b, w], zl[:, cols], start=False, stop=False)
                        pe.matmul(ps[:, bank, :], wh[:, b, w], zh[:, cols], start=False, stop=True)\
                            .then_inc(q[done], 1)

                def spread(m, b, n):
                    pe.wait_ge(q["y_used"], m + 1)
                    pe.matmul(ps[:, 6 + n, :], selp[:, b, :], combT[:, n * COLS:(n + 1) * COLS],
                              start=True, stop=True).then_inc(q["c_ready"], 1)

                def down(k, s, last):
                    u, j, blocks = L.place(s, last)
                    g = L.steps * k + s
                    m, b, n = 4 * k + u, (u // 2) % 2, u % 2
                    if j == 0:
                        pe.wait_ge(q["c_copied"], m + 3)
                    pe.wait_ge(q["hh_ready"], g + 1)
                    pe.wait_ge(q["hl_ready"], g + 3)
                    w = slice((2 * blocks + j) * P, (2 * blocks + j + 1) * P)
                    bank = ps[:, 6 + n, :]
                    pe.matmul(bank, wl[:, b, w], hh[:, s % 2, :], start=(j == 0), stop=False)
                    pe.matmul(bank, wh[:, b, w], hl[:, s % 2, :], start=False, stop=False)
                    pe.matmul(bank, wh[:, b, w], hh[:, s % 2, :], start=False, stop=(j == blocks - 1))\
                        .then_inc(q["down_done"], 1)
                    if j == blocks - 1 and not (last and s + 1 == L.last_steps()):
                        spread(m + 1, ((u + 1) // 2) % 2, (u + 1) % 2)

                LEAD = 3
                for s in range(LEAD):
                    up(0, s, False)
                spread(0, 0, 0)
                with pe.Fori(0, L.pairs - 1) as k:
                    for s in range(L.steps):
                        up(k, s + LEAD, False)
                        down(k, s, False)
                k = L.pairs - 1
                for s in range(L.last_steps()):
                    if s + LEAD < L.last_steps():
                        up(k, s + LEAD, True)
                    down(k, s, True)

            def turn_tokens(index, first_bank):
                for t in range(T):
                    pe.wait_ge(z_ready, T * index + t + 1)
                    last = turn(ps[:, first_bank + t // 4, t % 4 * P:(t % 4 + 1) * P], z[:, t, :])
                    if t % 4 == 3:
                        last.then_inc(zT_psum, 1)

            def attend(units, base, scores, values):
                def score(u):
                    if u >= 4:
                        pe.wait_ge(probs_ready, base + u - 3)
                    scores(u, ps[:, u % 4, :]).then_inc(scores_ready, 1)

                score(0)
                score(1)
                for u in range(units):
                    if u + 2 < units:
                        score(u + 2)
                    pe.wait_ge(probs_ready, base + u + 1)
                    values(u, probs[:, u % 4, :]).then_inc(pv_done, 1)

            def project_out(layer, w):
                for t in range(T):
                    if t % 4 == 0:
                        pe.wait_ge(oT_ready, 4 * layer + 2 * (t // 4) + 2)
                    last = pe.matmul(ps[:, t // 4, t % 4 * P:(t % 4 + 1) * P], oT[:, t * P:(t + 1) * P], w,
                                     start=True, stop=True)
                    if t % 4 == 3:
                        last.then_inc(o_psum, 1)

            def route(layer, w, experts):
                pe.wait_ge(zT_ready, 4 + 4 * layer)
                for t in range(T):
                    last = pe.matmul(ps[:, 4, t * 16:t * 16 + experts], zT[:, t * P:(t + 1) * P], w,
                                     start=True, stop=True)
                last.then_inc(route_psum, 1)

            def turn_combine(layer):
                pe.wait_ge(comb_staged, layer + 1)
                for t in range(T):
                    last = turn(ps[:, 5 + t // 4, t % 4 * P:(t % 4 + 1) * P], comb_st[:, t, :])
                    if t % 4 == 3:
                        last.then_inc(comb_psum, 1)

            def before_experts(layer):
                pe.wait_ge(zh_ready, 2 * layer + 2)
                pe.wait_ge(zl_ready, 2 * layer + 2)
                pe.wait_ge(comb_ready, 2 * layer + 2)

            def turn_result(layer):
                q, units = ffn_sem[layer], 2 * LAYERS[layer].all_experts
                pe.wait_ge(q["y_summed"], units + 2)
                for t in range(T):
                    last = turn(ps[:, t // 4, t % 4 * P:(t % 4 + 1) * P], yT[:, t * P:(t + 1) * P])
                    if t % 4 == 3:
                        last.then_inc(y_turned, 1)

            pe.wait_ge(const_ready, 3)
            pe.wait_ge(w0_in, N_W0)
            turn(ps[:, 2, 0:P], wq0[:, :])
            turn(ps[:, 2, P:2 * P], wlkv[:, 0, :])
            turn(ps[:, 2, 2 * P:3 * P], wlkv[:, 1, :])
            turn(ps[0:DC, 3, 0:P], wkv[:, 0, :])
            turn(ps[0:DC, 3, P:2 * P], wkv[:, 1, :])
            turn(ps[:, 3, 2 * P:3 * P], wo0[:, :]).then_inc(wT_psum, 1)
            pe.wait_ge(ctx_in, 32)
            pe.wait_ge(cz_ready, 4)
            for bank, src in ((4, ctx_z), (5, ctx_rows)):
                for b in range(B):
                    turn(ps[0:DC, bank, b * P:(b + 1) * P], src[:, b, :])
                    last = turn(ps[0:DC, bank, 2 * P + 32 * b:2 * P + 32 * b + KR], src[0:KR, 2 + b, :], KR)
            last.then_inc(cT_psum, 1)
            turn_tokens(0, 0)
            pe.wait_ge(wT_ready, 1)
            pe.wait_ge(cT_ready, 1)
            for m in range(4):
                last = pe.matmul(ps[:, 6 + m // 2, m % 2 * 256:m % 2 * 256 + 256], cT[:, m, :], wkvT[:, :],
                                 start=True, stop=True)
            last.then_inc(cproj_psum, 1)
            pe.wait_ge(zT_ready, 2)
            for t in range(T):
                if t >= 4:
                    pe.wait_ge(proj_used, t - 3)
                pe.matmul(ps[:, t % 4, 0:3 * P], zT[:, t * P:(t + 1) * P], wcat[:, :], start=True, stop=True)\
                    .then_inc(proj_psum, 1)
            pe.wait_ge(proj_used, T)
            pe.wait_ge(cproj_used, 2)
            for i in range(16):
                pe.wait_ge(staged, 2 if i < 4 else 3)
                if i >= 8:
                    done = turned_v if i % 2 else turned_a
                    pe.wait_ge(done, (i - 8) // 2 + 1)
                for a in range(4):
                    last = turn(ps[:, i % 8, a * P:(a + 1) * P], turned_from0(i, a))
                last.then_inc(turn_psum, 1)
            pe.wait_ge(turned_a, 8)
            pe.wait_ge(turned_v, 8)
            for u in range(2 * T):
                t, h = divmod(u, 2)
                b = t // TB
                if u >= 4:
                    pe.wait_ge(mx_used, u - 3)
                q = q_s0[:, h, t * P:(t + 1) * P]
                lat, con = ps[:, 2 * (u % 4), :], ps[:, 2 * (u % 4) + 1, :]
                pe.matmul(lat, q, k_a0[:, 0, b, h, P:5 * P], start=True, stop=True)
                pe.matmul(con[:, 0:P], q, k_a0[:, 0, b, h, 0:P], start=True, stop=True)
                pe.matmul(con[:, P:CK], q, k_b0[:, 0, b, h, 64 * h:64 * h + KR], start=True, stop=True)\
                    .then_inc(mx_psum, 1)
            pe.wait_ge(mx_used, 2 * T)
            pe.wait_ge(shift_staged, 1)
            for t in range(T):
                last = turn(ps[:, t // 4, t % 4 * P:(t % 4 + 1) * P], comb_st[:, t, :])
                if t % 4 == 3:
                    last.then_inc(shift_psum, 1)

            def scores0(u, bank):
                b, r = divmod(u, 11)
                heads = (0, 1) if r == 10 else (r // 5,)
                n = slice(b * COLS, (b + 1) * COLS)
                for i, h in enumerate(heads):
                    for part in range(2):
                        k = k_b0[:, part, b, h, :] if r == 10 else k_a0[:, part, b, h, r % 5 * P:(r % 5 + 1) * P]
                        last = pe.matmul(bank, k, q_s0[:, h, n], start=(i == 0 and part == 0), stop=False)
                if r == 10:
                    last = pe.matmul(bank, selpk[:, :], combT[:, n], start=False, stop=True)
                else:
                    last = pe.matmul(bank, sel[:, heads[0], :], combT[:, n], start=False, stop=True)
                return last

            def values0(u, p):
                b, r = divmod(u, 11)
                if r < 10:
                    return pe.matmul(ps[:, 4 + 2 * b + r // 5, :], v_a0[:, 5 * b + r % 5, r // 5, :], p,
                                     start=(r % 5 == 0), stop=False, skip_group_check=True)
                for h in range(H0):
                    last = pe.matmul(ps[:, 4 + 2 * b + h, :], v_b0[:, b, h, :], p, start=False, stop=True,
                                     skip_group_check=True)
                return last

            pe.wait_ge(const_ready, 4)
            pe.wait_ge(shift_ready, 2)
            pe.wait_ge(kv_ready, 2)
            attend(22, 0, scores0, values0)
            project_out(0, woT[:, :])

            turn_tokens(1, 2)
            route(0, wr0[:, :], E0)
            turn_combine(0)
            before_experts(0)
            ffn(0)
            turn_result(0)

            pe.wait_ge(w1_in, N_W1)
            turn(ps[:, 7, 0:P], beR[:, :]).then_inc(beT_psum, 1)
            for m in range(4):
                last = pe.matmul(ps[:, 4 + m // 2, m % 2 * 256:m % 2 * 256 + 256], rT[:, m, :],
                                 w1c[:, :, :].rearrange("p a c -> p (a c)"), start=True, stop=True)
            last.then_inc(kv1_psum, 1)
            pe.wait_ge(k1_staged, 1)
            for i in range(4):
                if i == 1:
                    pe.wait_ge(beT_ready, 1)
                for g in range(G1):
                    last = turn(ps[:, (6, 7, 4, 5)[i], g * P:(g + 1) * P],
                                st_k1[:, i, 4 * g:4 * g + 4, :].rearrange("p h c -> p (h c)"))
                last.then_inc(k1_psum, 1)
            turn_tokens(2, 0)
            pe.wait_ge(zT_ready, 6)
            for t in range(T):
                last = pe.matmul(ps[:, 2 + t // 4, t % 4 * P:(t % 4 + 1) * P], zT[:, t * P:(t + 1) * P],
                                 w1[:, 0, :], start=True, stop=True)
                if t % 4 == 3:
                    last.then_inc(q1_psum, 1)
            pe.wait_ge(k1_ready, 4)

            def turn_queries(t, bank, done):
                for g in range(G1):
                    last = turn(ps[:, bank, g * P:(g + 1) * P],
                                st_q1[:, t, 4 * g:4 * g + 4, :].rearrange("p h c -> p (h c)"))
                last.then_inc(done, 1)

            def full_queries(t):
                pe.wait_ge(shift1_staged, t + 1)
                if t >= 1:
                    pe.wait_ge(q1_full, t)
                turn_queries(t, 7, q1_full_psum)

            for t in range(T):
                pe.wait_ge(q1_staged, t // 4 + 1)
                if t >= 1:
                    pe.wait_ge(q1_turned, t)
                turn_queries(t, 6, q1_turn_psum)
                if t >= 1:
                    row_scores1(pe, t - 1)
                if t >= 2:
                    full_queries(t - 2)
            row_scores1(pe, T - 1)
            full_queries(T - 2)
            full_queries(T - 1)

            def scores1(u, bank):
                b, r = divmod(u, 20)
                g, j = divmod(r, 5)
                k = k_b1[:, b, g, :] if j == 4 else k_a1[:, b, g, j, :]
                return pe.matmul(bank, k, q_s1[:, g, b * COLS:(b + 1) * COLS], start=True, stop=True)

            def values1(u, p):
                b, r = divmod(u, 20)
                g, j = divmod(r, 5)
                a, c = divmod(g, 2)
                if j == 4:
                    v = v_b1[:, b, a, c * P:(c + 1) * P]
                else:
                    v = v_a1[:, b, a, (4 * c + j) * P:(4 * c + j + 1) * P]
                return pe.matmul(ps[:, 4 + 2 * b + a, :], v, p, start=(c == 0 and j == 0), stop=(c == 1 and j == 4))

            pe.wait_ge(q1_full, T)
            pe.wait_ge(mx1_used, 5 * T)
            attend(40, 22, scores1, values1)
            project_out(1, w1[:, 1, :])

            turn_tokens(3, 2)
            route(1, wr1[:, :], E1)
            turn_combine(1)
            before_experts(1)
            for m in range(2):
                pe.matmul(ps[:, (4, 7)[m], :], be2[:, :], combT[:, m * COLS:(m + 1) * COLS].bitcast(F32),
                          start=True, stop=True).then_inc(yinit_psum, 1)
            pe.wait_ge(y_init, 2)
            ffn(1)
            turn_result(1)

        @block.vector
        def _(dve):
            do = linked(dve, dve_link)

            def statistics(x, st, out_mv, parts):
                for i, (rows, m) in enumerate(parts):
                    do(dve.bn_stats(st[0:rows, m, :], x[0:rows, m, :]), i == len(parts) - 1)
                for i, (rows, m) in enumerate(parts):
                    do(dve.bn_aggr(out_mv[0:rows, m, :], st[0:rows, m, :]), i == len(parts) - 1)

            def normalize(index, twice=False):
                statistics(xres, stats, mv, [(P, t) for t in range(T)])
                var = mv[:, :, 1:2].rearrange("p t o -> p (t o)")
                a, c = (1 + LN_EPS, LN_EPS * LN_EPS) if twice else (1.0, LN_EPS)
                dve.tensor_scalar(rstd[:, :], var, a, c, ALU.mult, ALU.add).then_inc(var_ready, 1)
                dve.wait_ge(rstd_ready, (2, 5, 6, 7)[index])
                for t in range(T):
                    dve.tensor_scalar(z[:, t, :], xres[:, t, :], mv[:, t, 0:1], rstd[:, t:t + 1],
                                      ALU.subtract, ALU.mult).then_inc(z_ready, 1)

            def add_bias(index, bias):
                dve.wait_ge(gate_ready, 1)
                dve.wait_ge(z_ready, T * (index + 1))
                do(dve.scalar_tensor_tensor(out=xres[:, :, :], in0=bias.unsqueeze(1).broadcast_to([P, T, D]),
                                            scalar=tg[:, index // 2:index // 2 + 1], in1=xres[:, :, :],
                                            op0=ALU.mult, op1=ALU.add))

            def divide_by_sums(layer, units):
                for b in range(B):
                    dve.wait_ge(pv_done, 22 * layer + units * (b + 1))
                    for i in range(2):
                        bank = ps[:, 4 + 2 * b + i, :]
                        do(dve.reciprocal(rcp[0:64, i, :], bank[64:P, :]))
                        dve.tensor_tensor(oT[64 * i:64 * i + 64, b * COLS:(b + 1) * COLS], bank[0:64, :],
                                          rcp[0:64, i, :], ALU.mult).then_inc(oT_ready, 1)

            def add_attention(layer):
                for m in range(2):
                    dve.wait_ge(o_psum, 2 * layer + m + 1)
                    part = xres[:, 4 * m:4 * m + 4, :].rearrange("p t d -> p (t d)")
                    do(dve.scalar_tensor_tensor(out=part, in0=ps[:, m, :], scalar=tg[:, layer:layer + 1],
                                                in1=part, op0=ALU.mult, op1=ALU.add))

            def low_tokens(layer):
                for m in range(2):
                    dve.wait_ge(zh_ready, 2 * layer + m + 1)
                    cols = slice(m * COLS, (m + 1) * COLS)
                    dve.tensor_tensor(zl[:, cols], ps[:, 2 + m, :], zh[:, cols].bitcast(F32), ALU.subtract)\
                        .then_inc(zl_ready, 1)

            def choose(layer, experts):
                def v(i, n=experts):
                    return small[:, i, 0:T * n].rearrange("p (t e) -> p t e", t=T)

                def row(i):
                    return small[:, i, 0:T]

                def over(i, n=experts):
                    return small[:, i, 0:T].unsqueeze(2).broadcast_to([P, T, n])

                first = rev[:, 0:experts].unsqueeze(1).broadcast_to([P, T, experts])
                dve.wait_ge(const_ready, 7)
                dve.wait_ge(route_psum, layer + 1)
                logits = ps[:, 4, 0:T * 16].rearrange("p (t e) -> p t e", t=T)[:, :, 0:experts]
                if layer == 0:
                    do(dve.tensor_copy(v(0), logits))
                else:
                    do(dve.tensor_tensor(v(0), logits, br[:, :].unsqueeze(1).broadcast_to([P, T, experts]), ALU.add))
                    do(dve.tensor_scalar(v(0), v(0), 1.0 / TAU, None, ALU.mult))
                for i, source in ((0, 0), (1, 5)):
                    do(dve.tensor_reduce(row(13 + i), v(source), AX.X, ALU.max))
                    do(dve.tensor_tensor(v(3), v(source), over(13 + i), ALU.is_equal))
                    do(dve.tensor_tensor(v(3), v(3), first, ALU.mult))
                    do(dve.tensor_reduce(row(4), v(3), AX.X, ALU.max))
                    do(dve.tensor_tensor(v(1 + i), v(3), over(4), ALU.is_equal))
                    if i == 0:
                        do(dve.scalar_tensor_tensor(out=v(5), in0=v(1), scalar=-BIG, in1=v(0), op0=ALU.mult, op1=ALU.add))
                dve.tensor_tensor(row(15), row(14), row(13), ALU.subtract).then_inc(gap_ready, 1)
                dve.wait_ge(e_ready, layer + 1)
                do(dve.tensor_scalar(row(6), row(15), 1.0, None, ALU.add))
                do(dve.reciprocal(row(7), row(6)))
                scale = DEPTH_SCALE if layer == 0 else 1.0
                do(dve.tensor_scalar(row(7), row(7), tg[:, 2 + layer:3 + layer], scale, ALU.mult, ALU.mult))
                do(dve.tensor_tensor(row(8), row(15), row(7), ALU.mult))
                do(dve.tensor_tensor(v(9), v(1), over(7), ALU.mult))
                do(dve.tensor_tensor(v(10), v(2), over(8), ALU.mult))
                cols = LAYERS[layer].all_experts
                w = comb_w[:, :, 0:cols]
                do(dve.tensor_tensor(comb_w[:, :, 0:experts], v(9), v(10), ALU.add))
                if cols > experts:
                    do(dve.tensor_copy(comb_w[:, :, experts:cols], tg[:, 3:4].unsqueeze(1).broadcast_to([P, T, 1])))
                do(dve.tensor_copy(comb_st[:, :, 0:cols].bitcast(F32R), w))
                dve.tensor_tensor(comb_st[:, :, LO:LO + cols].bitcast(F32R), w, comb_st[:, :, 0:cols], ALU.subtract)\
                    .then_inc(comb_staged, 1)

            def ffn(layer):
                L, q = LAYERS[layer], ffn_sem[layer]

                def multiply(k, s, last):
                    bank = ps[:, 2 + s % 4, :]
                    u, j, blocks = L.place(s, last)
                    g = L.steps * k + s
                    dve.wait_ge(q["act_ready"], g + 1)
                    dve.wait_ge(q["u_ready"], g + 1)
                    if layer == 0:
                        ins = dve.tensor_tensor(bank, bank, act_out[:, s % 2, :], ALU.mult)
                    else:
                        ins = dve.scalar_tensor_tensor(
                            out=bank, in0=bank, scalar=biases[:, (u // 2) % 2, j:j + 1],
                            in1=act_out[:, s % 2, :], op0=ALU.add, op1=ALU.mult)
                    ins.then_inc(q["hid_ready"], 1)

                def low(k, s):
                    g = L.steps * k + s
                    dve.wait_ge(q["hid_ready"], g + 2)
                    dve.wait_ge(q["hh_ready"], g + 1)
                    dve.wait_ge(q["down_done"], g + 1)
                    dve.tensor_tensor(hl[:, s % 2, :], ps[:, 2 + s % 4, :], hh[:, s % 2, :].bitcast(F32),
                                      ALU.subtract).then_inc(q["hl_ready"], 1)

                def weigh(k, u, end):
                    m, n = 4 * k + u, u % 2
                    dve.wait_ge(q["down_done"], L.steps * k + end + 2)
                    dve.wait_ge(q["c_copied"], m + 3)
                    dve.wait_ge(q["y_summed"], m + 1)
                    dve.tensor_tensor(ytmp[:, n, :], ps[:, 6 + n, :], cbs[:, n, :], ALU.mult).then_inc(q["y_used"], 1)

                multiply(0, 0, False)
                multiply(0, 1, False)
                low(0, 0)
                with dve.Fori(0, L.pairs - 1) as k:
                    for s in range(1, L.steps + 1):
                        multiply(k, s + 1, False)
                        low(k, s)
                        if s % L.blocks == 0:
                            weigh(k, s // L.blocks - 1, s)
                k, total = L.pairs - 1, L.last_steps()
                for s in range(1, total + 1):
                    if s + 1 < total:
                        multiply(k, s + 1, True)
                    if s < total:
                        low(k, s)
                    u, j, blocks = L.place(s - 1, True)
                    if j == blocks - 1:
                        weigh(k, u, s)

            def add_result(layer):
                for m in range(2):
                    dve.wait_ge(y_turned, 2 * layer + m + 1)
                    part = xres[:, 4 * m:4 * m + 4, :].rearrange("p t d -> p (t d)")
                    dve.tensor_tensor(part, part, ps[:, m, :], ALU.add).then_inc(y_added, 1)
                dve.wait_ge(y_added, 2 * layer + 2)

            do(dve.memset(crstd[:, :], 1.0))
            dve.wait_ge(ctx_in, 32)
            statistics(ctx_rows, cstats, cmv, [(P, 0), (P, 1), (KR, 2), (KR, 3)])
            do(dve.tensor_scalar(crstd[:, 0:2], cmv[:, 0:2, 1:2].rearrange("p a o -> p (a o)"), LN_EPS, None, ALU.add))
            dve.tensor_scalar(crstd[0:KR, 2:4], cmv[0:KR, 2:4, 1:2].rearrange("p a o -> p (a o)"), LN_EPS, None,
                              ALU.add).then_inc(var_ready, 1)
            dve.wait_ge(rstd_ready, 1)
            for m in range(4):
                rows = slice(0, P if m < 2 else KR)
                dve.tensor_scalar(ctx_z[rows, m, :], ctx_rows[rows, m, :], cmv[rows, m, 0:1], crstd[rows, m:m + 1],
                                  ALU.subtract, ALU.mult).then_inc(cz_ready, 1)
            dve.wait_ge(x_in, 16)
            normalize(0, twice=True)
            dve.wait_ge(vec_in, N_VEC)
            add_bias(0, bo0[:, :])
            do(dve.tensor_scalar(maskB[:, :, :].rearrange("p b k -> p (b k)"), mask8[:, :], BIG, -BIG, ALU.mult, ALU.add))
            do(dve.tensor_scalar(mcol[:, :], mcol8[:, :], BIG, -BIG, ALU.mult, ALU.add))
            do(dve.tensor_tensor(gqk[:, :], gq[:, :], gk[:, :], ALU.mult))
            do(dve.tensor_scalar(gqk[:, :], gqk[:, :], HD0 ** -0.5, None, ALU.mult))

            dve.wait_ge(cproj_used, 2)
            ckeys = ckv[:, :, 0:P].rearrange("p m (h c) -> p m h c", h=H0)
            csq = stage[:, 0:4 * P].rearrange("p (m h c) -> p m h c", m=4, h=H0)
            do(dve.tensor_tensor(csq, ckeys, ckeys, ALU.mult))
            do(dve.tensor_reduce(css[:, :, :], csq, AX.X, ALU.add))
            dve.tensor_scalar(css[:, :, :], css[:, :, :], 1.0 / HD0, RMS_EPS2, ALU.mult, ALU.max).then_inc(var_ready, 1)
            dve.wait_ge(rstd_ready, 3)
            do(dve.tensor_tensor(ckeys, ckeys, crn[:, :, :].unsqueeze(3).broadcast_to([P, 4, H0, HD0]), ALU.mult))
            dve.wait_ge(zeroed, 5)
            for rows, blocks, heads in ((slice(0, P), slice(0, 2), slice(0, 2)),
                                        (slice(0, 64), slice(2, 4), slice(0, 1)), (slice(64, P), slice(2, 4), slice(1, 2))):
                src = ckeys[rows, blocks, heads, :]
                for dup in range(2):
                    do(dve.tensor_copy(st_c0[0][rows, blocks, heads, 64 * dup:64 * dup + 64], src))
                for dup in range(2):
                    last = dve.tensor_tensor(st_c0[1][rows, blocks, heads, 64 * dup:64 * dup + 64], src,
                                             st_c0[0][rows, blocks, heads, 0:64].bitcast(F32), ALU.subtract)
            last.then_inc(staged, 1)
            dve.wait_ge(proj_used, T)
            qk = qkv[:, :, 0:2 * P].rearrange("p t (h c) -> p t h c", h=4)
            sq = stage[:, 0:2048].rearrange("p (t h c) -> p t h c", t=T, h=4)
            do(dve.tensor_tensor(sq, qk, qk, ALU.mult))
            do(dve.tensor_reduce(ss[:, :, :], sq, AX.X, ALU.add))
            dve.tensor_scalar(ss[:, :, :], ss[:, :, :], 1.0 / HD0, RMS_EPS2, ALU.mult, ALU.max).then_inc(var_ready, 1)
            dve.wait_ge(rstd_ready, 4)
            do(dve.tensor_tensor(qk, qk, rn[:, :, :].unsqueeze(3).broadcast_to([P, T, 4, HD0]), ALU.mult))
            for h in range(H0):
                qh = qk[:, :, h, :]
                do(dve.tensor_tensor(qh, qh, gqk[:, :].unsqueeze(1).broadcast_to([P, T, HD0]), ALU.mult))
            qq, kk = qk[:, :, 0:2, :], qk[:, :, 2:4, :]
            do(dve.tensor_copy(st_q0[:, :, :, 0:64].bitcast(F32R), qq))
            dve.tensor_tensor(st_q0[:, :, :, 64:P].bitcast(F32R), qq, st_q0[:, :, :, 0:64], ALU.subtract)\
                .then_inc(staged, 1)
            for dup in range(2):
                do(dve.tensor_copy(st_k0[:, 0, :, :, 64 * dup:64 * dup + 64].bitcast(F32R), kk))
            for dup in range(2):
                last = dve.tensor_tensor(st_k0[:, 1, :, :, 64 * dup:64 * dup + 64].bitcast(F32R), kk,
                                         st_k0[:, 0, :, :, 0:64], ALU.subtract)
            last.then_inc(staged, 1)
            dve.wait_ge(zeroed, 7)
            for h in range(H0):
                last = dve.memset(v_b0[64 * h:64 * h + 64, :, h, 64:P], 1.0)
            last.then_inc(kv_ready, 1)
            for i in range(1, 16, 2):
                dve.wait_ge(turn_psum, i + 1)
                dve.tensor_copy(turned_to0(i), turned_bank0(i)).then_inc(turned_v, 1)
            for u in range(2 * T):
                t, h = divmod(u, 2)
                dve.wait_ge(mx_psum, u + 1)
                lat, con = ps[:, 2 * (u % 4), :], ps[:, 2 * (u % 4) + 1, 0:CK]
                do(dve.tensor_tensor(mtmp[:, u % 2, 0:CK], con, maskB[:, t // TB, :], ALU.add))
                do(dve.tensor_reduce(mx[:, t, 2 * h + 1:2 * h + 2], mtmp[:, u % 2, 0:CK], AX.X, ALU.max), False)
                dve.tensor_reduce(mx[:, t, 2 * h:2 * h + 1], lat, AX.X, ALU.max).then_inc(mx_used, 1)
            dve.wait_ge(mx_used, 2 * T)
            pair = mx[:, :, 0:4].rearrange("p t (h i) -> p t h i", h=H0)
            do(dve.tensor_reduce(small[:, 0, 0:2 * T].rearrange("p (t h) -> p t h", t=T), pair, AX.X, ALU.max))
            dve.wait_ge(zeroed, 1)
            dve.tensor_scalar(comb_st[:, :, 0:2].bitcast(F32R), small[:, 0, 0:2 * T].rearrange("p (t h) -> p t h", t=T),
                              -1.0, None, ALU.mult).then_inc(shift_staged, 1)
            divide_by_sums(0, 11)
            add_attention(0)

            normalize(1)
            low_tokens(0)
            choose(0, E0)
            ffn(0)
            add_result(0)

            normalize(2)
            dve.wait_ge(w1_in, N_W1)
            add_bias(2, b1[:, 3, :])
            for m in range(2):
                dve.wait_ge(kv1_psum, 1)
                do(dve.tensor_tensor(ckv[:, 2 * m:2 * m + 2, :], ps[:, 4 + m, :].rearrange("p (b c) -> p b c", b=B),
                                     b1[:, 1:3, :].rearrange("p a c -> p (a c)").unsqueeze(1).broadcast_to([P, B, 2 * P]),
                                     ALU.add))
            dve.wait_ge(zeroed, 11)
            for rows, blocks, j in [(slice(0, P), slice(0, 2), None)] + \
                    [(slice(32 * j, 32 * j + 32), slice(2, 4), j) for j in range(4)]:
                heads = slice(0, H1) if j is None else slice(j, H1, 4)
                src = ckv[rows, blocks, 0:P].rearrange("p m (h d) -> p m h d", h=H1)[:, :, heads, :]
                dst = st_k1[rows, blocks, heads, :]
                do(dve.tensor_copy(dst[:, :, :, 0:8].bitcast(F32R), src))
                dve.tensor_copy(dst[:, :, :, 8:16].bitcast(F32R), src)
                dve.tensor_tensor(dst[:, :, :, 16:24].bitcast(F32R), src, dst[:, :, :, 0:8], ALU.subtract)
                last = dve.memset(dst[:, :, :, 24:25], 1.0)
            last.then_inc(k1_staged, 1)
            for b in range(B):
                va = v_a1[:, b, :, :].rearrange("p a (r s) -> p a r s", s=136)
                do(dve.tensor_copy(va[:, :, :, 0:8], ckv[:, b, P:2 * P].rearrange("p (a r d) -> p a r d", a=2, r=8)), False)
                do(dve.memset(va[:, :, :, 64:72], 1.0), False)
            vb = v_b[:, :].rearrange("p (b g s) -> p b g s", b=B, g=G1)
            for j in range(4):
                rows = slice(32 * j, 32 * j + 32)
                src = ckv[rows, 2:4, P:2 * P].rearrange("p b (g j d) -> p b g j d", g=G1, j=4)[:, :, :, j, :]
                do(dve.tensor_copy(vb[rows, :, :, 8 * j:8 * j + 8], src), False)
                do(dve.memset(vb[rows, :, :, 64 + 8 * j:72 + 8 * j], 1.0), j == 3)
            do(dve.tensor_scalar(b1[:, 0, :], b1[:, 0, :], HD1 ** -0.5, None, ALU.mult))
            for m in range(2):
                dve.wait_ge(q1_psum, m + 1)
                dst = qkv[:, 4 * m:4 * m + 4, 0:P]
                do(dve.scalar_tensor_tensor(out=dst, in0=ps[:, 2 + m, :].rearrange("p (t c) -> p t c", t=4),
                                            scalar=HD1 ** -0.5, in1=b1[:, 0, :].unsqueeze(1).broadcast_to([P, 4, P]),
                                            op0=ALU.mult, op1=ALU.add))
                src = dst.rearrange("p t (h d) -> p t h d", h=H1)
                st = st_q1[:, 4 * m:4 * m + 4, :, :]
                do(dve.tensor_copy(st[:, :, :, 0:8].bitcast(F32R), src))
                dve.tensor_copy(st[:, :, :, 16:24].bitcast(F32R), src)
                dve.tensor_tensor(st[:, :, :, 8:16].bitcast(F32R), src, st[:, :, :, 0:8], ALU.subtract)\
                    .then_inc(q1_staged, 1)
            for i in range(4):
                dve.wait_ge(k1_psum, i + 1)
                bank = ps[:, (6, 7, 4, 5)[i], :].rearrange("p (g k) -> p g k", g=G1)
                if i >= 2:
                    dve.tensor_copy(k_b1[:, i - 2, :, :], bank).then_inc(k1_ready, 1)
                    continue
                for j in range(4):
                    rows = slice(32 * j, 32 * j + 32)
                    last = dve.tensor_copy(k_a1[rows, i, :, j, :], bank[rows, :, :])
                last.then_inc(k1_ready, 1)
            for t in range(T):
                for g in range(G1 + 1):
                    dve.wait_ge(mx1_psum, 5 * t + g + 1)
                    if g < G1:
                        dve.tensor_reduce(mx[:, t, 4 * g:4 * g + 4], ps[:, g, :].rearrange("p (j k) -> p j k", j=4),
                                          AX.X, ALU.max).then_inc(mx1_used, 1)
                    else:
                        dve.tensor_reduce(mx[:, t, H1:2 * H1], ps[:, 4 + t % 2, :].rearrange("p (h k) -> p h k", h=H1)
                                          [:, :, 0:KR], AX.X, ALU.max).then_inc(mx1_used, 1)
                dve.wait_ge(mx1_used, 5 * t + 5)
                do(dve.tensor_tensor(small[:, t % 2, 0:H1], mx[:, t, 0:H1], mx[:, t, H1:2 * H1], ALU.max))
                dve.tensor_scalar(st_q1[:, t, :, 24:25].rearrange("p h o -> p (h o)").bitcast(F32R),
                                  small[:, t % 2, 0:H1], -1.0, None, ALU.mult).then_inc(shift1_staged, 1)
            divide_by_sums(1, 20)
            add_attention(1)

            normalize(3)
            low_tokens(1)
            choose(1, E1)
            ffn(1)
            add_result(1)


_INS = ["x", "ctx_768", "mask_BxS2_bk0", "g_xattn", "g_ffn", "L0_xattn_ln_x_g", "L0_xattn_ln_x_b",
        "L0_xattn_ln_l_g", "L0_xattn_ln_l_b", "L0_xattn_qn_g", "L0_xattn_kn_g", "L0_xattn_Wq", "L0_xattn_Wkv",
        "L0_xattn_Wlkv", "L0_xattn_Wo", "L0_xattn_bo", "L0_ffn_Wr", "L0_ffn_Wg", "L0_ffn_Wu", "L0_ffn_Wd",
        "L1_xattn_wq", "L1_xattn_bq", "L1_xattn_wk", "L1_xattn_bk", "L1_xattn_wv", "L1_xattn_bv", "L1_xattn_wo",
        "L1_xattn_bo", "L1_ffn_Ws1", "L1_ffn_bs1", "L1_ffn_Ws2", "L1_ffn_bs2", "L1_ffn_We1", "L1_ffn_be1",
        "L1_ffn_We2", "L1_ffn_be2", "L1_ffn_Wr", "L1_ffn_br"]


def kernel(**inputs):
    import numpy as np
    import concourse.bacc as bacc
    from concourse.bass_utils import run_bass_kernel_spmd

    nc = bacc.Bacc("TRN2", target_bir_lowering=False, num_devices=1)
    arrays, aps = {}, {}
    for name in _INS:
        a = np.ascontiguousarray(inputs[name])
        arrays[f"in_{name}"] = a
        aps[name] = nc.dram_tensor(f"in_{name}", a.shape, mybir.dt.from_np(a.dtype), kind="ExternalInput").ap()
    out = nc.dram_tensor("out_x", (B, S, D), F32, kind="ExternalOutput").ap()
    flamingo(nc, aps, out)
    r = run_bass_kernel_spmd(nc, [arrays], core_ids=[0])
    return r.results[0]["out_x"]
```

```python
import math
from contextlib import ExitStack

import concourse.bass as bass
from concourse import mybir
from concourse.alu_op_type import AluOpType as ALU

ACT = mybir.ActivationFunctionType
AX = mybir.AxisListType
F32 = mybir.dt.float32
F32R = mybir.dt.float32r
U8 = mybir.dt.uint8
I32 = mybir.dt.int32

P = 128
B, S, D = 2, 512, 128
T = B * S // P
TB = S // P
N = B * S
CK, DC = 154, 96
KR = CK - P
H0, HD0 = 2, 64
H1, HD1 = 16, 8
G1 = 4
E0, E1 = 8, 12
LN_EPS = 1e-5
RMS_EPS2 = 1e-16
TAU = 1.5
DEPTH_SCALE = 1.0 / 12 ** 0.5
BIG = 1e30
LO = 16

BANKS = 8
COLS = 512


class Layer:

    def __init__(self, experts, blocks, function, shared_blocks):
        self.experts, self.blocks, self.function = experts, blocks, function
        self.shared_blocks = shared_blocks
        self.pairs = experts // 2
        self.steps = 4 * blocks
        self.all_experts = experts + (1 if shared_blocks else 0)

    def place(self, s, last):
        if last and s >= self.steps and self.shared_blocks:
            r = s - self.steps
            return 4 + r // self.shared_blocks, r % self.shared_blocks, self.shared_blocks
        return s // self.blocks, s % self.blocks, self.blocks

    def last_steps(self):
        return self.steps + 2 * self.shared_blocks


def flamingo(nc, A, out):
    with ExitStack() as ctx:
        def sb(name, shape, dt=F32):
            return ctx.enter_context(nc.sbuf_tensor(name, shape, dt))

        def sem(name):
            return ctx.enter_context(nc.semaphore(name))

        xres = sb("xres", [P, T, D])
        z = sb("z", [P, T, D])
        zT = sb("zT", [P, N])
        ident = sb("ident", [P, P])
        sel = sb("sel", [P, 13, P], F32R)
        rev = sb("rev", [P, 16])
        revi = sb("revi", [P, 16], I32)
        zero = sb("zero", [P, 1])
        half = sb("half", [P, 32])
        euler = sb("euler", [P, T])
        stats = sb("stats", [P, T, 6])
        mv = sb("mv", [P, T, 2])
        rstd = sb("rstd", [P, T])
        cstats = sb("cstats", [P, 4, 6])
        cmv = sb("cmv", [P, 4, 2])
        crstd = sb("crstd", [P, 4])
        ctx_rows = sb("ctx_rows", [P, 4, DC])
        ctx_z = sb("ctx_z", [P, 4, DC])
        cT = sb("cT", [DC, 4, P])
        rT = sb("rT", [DC, 4, P])
        gates = sb("gates", [P, 4])
        tg = sb("tg", [P, 4])
        colv = sb("colv", [P, 4])
        gq = sb("gq", [P, HD0])
        gk = sb("gk", [P, HD0])
        gqk = sb("gqk", [P, HD0])
        bo0 = sb("bo0", [P, D])
        b1 = sb("b1", [P, 4, D])
        br = sb("br", [P, E1])
        wr0 = sb("wr0", [P, E0])
        wr1 = sb("wr1", [P, E1])
        wq0 = sb("wq0", [P, P])
        wlkv = sb("wlkv", [P, 2, P])
        wkv = sb("wkv", [P, 2, DC])
        wo0 = sb("wo0", [P, P])
        wcat = sb("wcat", [P, 3 * P])
        wkvT = sb("wkvT", [DC, 2 * P])
        woT = sb("woT", [P, P])
        w1 = sb("w1", [P, 2, P])
        w1c = sb("w1c", [DC, 2, P])
        beR = sb("beR", [P, P])
        beT = sb("beT", [P, 76])
        be2 = sb("be2", [P, P])
        mask8 = sb("mask8", [1, B * CK], U8)
        mask_row = sb("mask_row", [1, B, CK], F32R)
        mcol8 = sb("mcol8", [P, 4], U8)
        mcol = sb("mcol", [P, 4])
        pad1 = sb("pad1", [P, 1])
        qkv = sb("qkv", [P, T, 3 * P])
        ckv = sb("ckv", [P, 4, 2 * P])
        ss = sb("ss", [P, T, 4])
        rn = sb("rn", [P, T, 4])
        css = sb("css", [P, 4, 2])
        crn = sb("crn", [P, 4, 2])
        stage = sb("stage", [P, 6144])
        q_s = sb("q_s", [P, 4096], F32R)
        k_a = sb("k_a", [P, 5120], F32R)
        k_b = sb("k_b", [P, 1024], F32R)
        v_a = sb("v_a", [P, 4352])
        v_b = sb("v_b", [P, 1280])
        probs = sb("probs", [P, 4, COLS])
        mx = sb("mx", [P, T, 32])
        small = sb("small", [P, 16, T * 12])
        comb_st = sb("comb_st", [P, T, P])
        combT = sb("combT", [P, N], F32R)
        comb_w = sb("comb_w", [P, T, 13])
        biases = sb("biases", [P, 2, 6])
        selp = sb("selp", [P, 2, P], F32R)
        selpk = sb("selpk", [P, P], F32R)
        raw = sb("raw", [P, 2, 1536])
        wh = sb("wh", [P, 2, 1536], F32R)
        wl = sb("wl", [P, 2, 1536], F32R)
        zh, zl = q_s[:, 0:N], q_s[:, N:2 * N]
        free = qkv[:, :, :].rearrange("p t c -> p (t c)")
        hh = q_s[:, 2 * N:3 * N].rearrange("p (a n) -> p a n", a=2)
        hl = q_s[:, 3 * N:4 * N].rearrange("p (a n) -> p a n", a=2)
        act_out = free[:, 0:N].rearrange("p (a n) -> p a n", a=2)
        yT = free[:, 2 * N:3 * N]
        oT = zT
        cbs = probs[:, 0:2, :]
        ytmp = probs[:, 2:4, :]
        rcp = z[0:64, TB:T, :].rearrange("p t d -> p (t d)")
        ps = ctx.enter_context(nc.psum_tensor("ps", [P, BANKS, COLS], F32))

        dve_link, act_link, pool_link = sem("dve_link"), sem("act_link"), sem("pool_link")
        x_in, ctx_in, w0_in, vec_in, w1_in = (sem(n) for n in ("x_in", "ctx_in", "w0_in", "vec_in", "w1_in"))
        const_ready, zeroed = sem("const_ready"), sem("zeroed")
        var_ready, rstd_ready, z_ready, zT_psum, zT_ready = (
            sem(n) for n in ("var_ready", "rstd_ready", "z_ready", "zT_psum", "zT_ready"))
        gate_ready = sem("gate_ready")
        wT_psum, wT_ready, cT_psum, cT_ready, cz_ready = (
            sem(n) for n in ("wT_psum", "wT_ready", "cT_psum", "cT_ready", "cz_ready"))
        proj_psum, proj_used, cproj_psum, cproj_used = (
            sem(n) for n in ("proj_psum", "proj_used", "cproj_psum", "cproj_used"))
        ss_ready, rn_ready = sem("ss_ready"), sem("rn_ready")
        staged, turn_psum, turned_a, turned_v = (sem(n) for n in ("staged", "turn_psum", "turned_a", "turned_v"))
        kv_ready = sem("kv_ready")
        mx_psum, mx_used, zh_ready, zl_ready = (sem(n) for n in ("mx_psum", "mx_used", "zh_ready", "zl_ready"))
        q1_psum, kv1_psum, k1_staged, k1_psum, k1_ready, v1_ready, q1_staged, q1_turned = (
            sem(n) for n in ("q1_psum", "kv1_psum", "k1_staged", "k1_psum", "k1_ready", "v1_ready", "q1_staged", "q1_turned"))
        q1_turn_psum, q1_full_psum, q1_full, mx1_psum, mx1_used, shift1_staged = (
            sem(n) for n in ("q1_turn_psum", "q1_full_psum", "q1_full", "mx1_psum", "mx1_used", "shift1_staged"))
        beT_psum, beT_ready, yinit_psum, y_init = (sem(n) for n in ("beT_psum", "beT_ready", "yinit_psum", "y_init"))
        shift_staged, shift_psum, shift_ready = sem("shift_staged"), sem("shift_psum"), sem("shift_ready")
        scores_ready, probs_ready, pv_done = sem("scores_ready"), sem("probs_ready"), sem("pv_done")
        oT_ready, o_psum, res_ready = sem("oT_ready"), sem("o_psum"), sem("res_ready")
        route_psum, gap_ready, e_ready, comb_staged, comb_psum, comb_ready = (
            sem(n) for n in ("route_psum", "gap_ready", "e_ready", "comb_staged", "comb_psum", "comb_ready"))
        y_turned, y_added, out_done = sem("y_turned"), sem("y_added"), sem("out_done")
        ffn_sem = [{n: sem(f"{n}_{i}") for n in (
            "w_in_a", "w_in_b", "w_high", "up_split", "w_split", "g_ready", "u_ready", "act_ready", "hid_ready", "hh_ready",
            "hl_ready", "down_done", "y_used", "y_summed", "c_ready", "c_copied")} for i in range(2)]
        HEAD_START = {"hid_ready": 1, "hl_ready": 2, "down_done": 2, "y_used": 2, "c_copied": 2}

        LAYERS = [Layer(E0, 4, ACT.Silu, 0), Layer(E1, 3, ACT.Gelu, 2)]

        def bcast(ap, *shape):
            return ap.broadcast_to(list(shape))

        def linked(eng, link):
            count = [0]

            def do(ins, wait=True):
                count[0] += 1
                ins.then_inc(link, 1)
                if wait:
                    eng.wait_ge(link, count[0])
            return do

        st_q0 = stage[:, 0:2048].rearrange("p (t h c) -> p t h c", t=T, h=H0)
        st_k0 = stage[:, 2048:6144].rearrange("p (s t h c) -> p s t h c", s=2, t=T, h=H0)
        st_c0 = [x[:, :, :].rearrange("p a (m h c) -> p (a m) h c", m=2, h=H0) for x in (hh, hl)]
        q_s0 = q_s[:, 0:2048].rearrange("p (h n) -> p h n", h=H0)
        k_a0 = k_a[:, :].rearrange("p (s b h k) -> p s b h k", s=2, b=B, h=H0)
        k_b0 = k_b[:, :].rearrange("p (s b h k) -> p s b h k", s=2, b=B, h=H0)
        v_a0 = v_a[:, 0:2560].rearrange("p (t h c) -> p t h c", h=H0, c=P)
        v_b0 = v_b[:, 0:512].rearrange("p (b h c) -> p b h c", b=B, h=H0)
        st_q1 = stage[:, 0:4096].rearrange("p (t h c) -> p t h c", t=T, h=H1)
        st_k1 = stage[:, 4096:6144].rearrange("p (m h c) -> p m h c", m=4, h=H1)
        q_s1 = q_s[:, :].rearrange("p (g n) -> p g n", g=G1)
        k_a1 = k_a[:, 0:4096].rearrange("p (b g j k) -> p b g j k", b=B, g=G1, j=4)
        k_b1 = k_b[:, :].rearrange("p (b g k) -> p b g k", b=B, g=G1)
        v_a1 = v_a[:, :].rearrange("p (b a c) -> p b a c", b=B, a=2)
        v_b1 = v_b[:, :].rearrange("p (b a c) -> p b a c", b=B, a=2)

        OWN = (5, 7)
        KEYS1, PROJECT0, TURN0, ROUTE0 = 3, 14, 17, 19
        PROJECT1, TURN1, ROUTE1 = 26, 33, 37
        LEAD = 3

        block = ctx.enter_context(nc.Block())

        @block.sync
        def _(sp):
            x_rows = A["x"].rearrange("b (t p) d -> p (b t) d", p=P)
            sp.dma_start(xres[:, :, :], x_rows).then_inc(x_in, 16)
            sp.dma_start(ctx_rows[:, 0:2, :], A["ctx_768"][:, 0:P, :].rearrange("b p c -> p b c")).then_inc(ctx_in, 16)
            sp.dma_start(ctx_rows[0:KR, 2:4, :],
                         A["ctx_768"][:, P:CK, :].rearrange("b p c -> p b c")).then_inc(ctx_in, 16)
            for dst, src in (
                    (wq0[:, :], A["L0_xattn_Wq"]),
                    (wlkv[:, :, :], A["L0_xattn_Wlkv"].rearrange("(a p) c -> p a c", p=P)),
                    (wkv[:, :, :], A["L0_xattn_Wkv"].rearrange("(a p) c -> p a c", p=P)),
                    (wo0[:, :], A["L0_xattn_Wo"])):
                sp.dma_start(dst, src).then_inc(w0_in, 16)
            for dst, src in (
                    (colv[:, 0:1], A["L0_xattn_ln_l_g"].unsqueeze(1)), (colv[:, 1:2], A["L0_xattn_ln_l_b"].unsqueeze(1)),
                    (colv[0:DC, 2:3], A["L0_xattn_ln_x_g"].unsqueeze(1)),
                    (colv[0:DC, 3:4], A["L0_xattn_ln_x_b"].unsqueeze(1)),
                    (gates[:, 0:2], A["g_xattn"].partition_broadcast(P)),
                    (gates[:, 2:4], A["g_ffn"].partition_broadcast(P)),
                    (gq[:, :], A["L0_xattn_qn_g"].partition_broadcast(P)),
                    (gk[:, :], A["L0_xattn_kn_g"].partition_broadcast(P)),
                    (mask8[:, :], A["mask_BxS2_bk0"].rearrange("b k -> (b k)").unsqueeze(0)),
                    (bo0[:, :], A["L0_xattn_bo"].partition_broadcast(P)),
                    (wr0[:, :], A["L0_ffn_Wr"])):
                sp.dma_start(dst, src).then_inc(vec_in, 16)
            sp.wait_ge(const_ready, 1)
            for b in range(B):
                sp.dma_start(mcol8[:, b:b + 1], A["mask_BxS2_bk0"][b, 0:P].unsqueeze(1)).then_inc(vec_in, 16)
                for j in range(H0):
                    sp.dma_start(mcol8[64 * j:64 * j + KR, 2 + b:3 + b],
                                 A["mask_BxS2_bk0"][b, P:CK].unsqueeze(1)).then_inc(vec_in, 16)

            def expert_loads(layer, e, b):
                into = ffn_sem[layer][("w_in_a", "w_in_b")[b]]
                w = LAYERS[layer].blocks * P
                if layer == 0:
                    srcs = [A["L0_ffn_Wg"][e, :, :].rearrange("a p n -> p (a n)"),
                            A["L0_ffn_Wu"][e, :, :].rearrange("a p n -> p (a n)")]
                    sp.dma_start(raw[:, b, 0:w], srcs[0]).then_inc(into, 16)
                    sp.dma_start(raw[:, b, w:2 * w], srcs[1]).then_inc(into, 16)
                    down = A["L0_ffn_Wd"][e, :, :]
                else:
                    sp.dma_start(raw[:, b, 0:2 * w], A["L1_ffn_We1"][e, :, :].rearrange("a p n -> p (a n)")).then_inc(into, 32)
                    down = A["L1_ffn_We2"][e, :, :]
                sp.dma_start(raw[:, b, 2 * w:3 * w].rearrange("p (c n) -> p c n", n=P),
                             down.rearrange("a (c p) n -> p (a c) n", p=P)).then_inc(into, 16)

            def first_loads(layer):
                for b in range(2):
                    expert_loads(layer, slice(b, b + 1), b)

            def later_loads(layer):
                L, q = LAYERS[layer], ffn_sem[layer]
                with sp.Fori(1, L.pairs) as k:
                    for b in range(2):
                        sp.wait_ge(q["w_split"], 2 * k + b - 1)
                        expert_loads(layer, bass.ds(2 * k + b, 1), b)

            first_loads(0)
            sp.wait_ge(const_ready, 7)
            for dst, src in (
                    (w1[:, 0, :], A["L1_xattn_wq"]), (w1[:, 1, :], A["L1_xattn_wo"]),
                    (w1c[:, 0, :], A["L1_xattn_wk"]), (w1c[:, 1, :], A["L1_xattn_wv"]),
                    (b1[:, 0, :], A["L1_xattn_bq"].partition_broadcast(P)),
                    (b1[:, 1, :], A["L1_xattn_bk"].partition_broadcast(P)),
                    (b1[:, 2, :], A["L1_xattn_bv"].partition_broadcast(P)),
                    (b1[:, 3, :], A["L1_xattn_bo"].partition_broadcast(P)),
                    (br[:, :], A["L1_ffn_br"].partition_broadcast(P)),
                    (wr1[:, :], A["L1_ffn_Wr"]),
                    (beR[0:72, :], A["L1_ffn_be1"].rearrange("e (c n) -> (e c) n", n=P)),
                    (beR[72:76, :], A["L1_ffn_bs1"].rearrange("(c n) -> c n", n=P)),
                    (be2[0:E1, :], A["L1_ffn_be2"]), (be2[LO:LO + E1, :], A["L1_ffn_be2"]),
                    (be2[E1:E1 + 1, :], A["L1_ffn_bs2"].unsqueeze(0)),
                    (be2[LO + E1:LO + E1 + 1, :], A["L1_ffn_bs2"].unsqueeze(0))):
                sp.dma_start(dst, src).then_inc(w1_in, 16)
            later_loads(0)
            sp.wait_ge(ffn_sem[0]["w_split"], E0)
            first_loads(1)
            later_loads(1)
            sp.wait_ge(ffn_sem[1]["w_split"], E1 - 1)
            sp.dma_start(raw[:, 0, 0:4 * P], A["L1_ffn_Ws1"]).then_inc(ffn_sem[1]["w_in_a"], 32)
            sp.dma_start(raw[:, 0, 4 * P:6 * P].rearrange("p (c n) -> p c n", n=P),
                         A["L1_ffn_Ws2"].rearrange("(c p) n -> p c n", p=P)).then_inc(ffn_sem[1]["w_in_a"], 16)
            for m in range(2):
                sp.wait_ge(y_added, 2 + m + 1)
                sp.dma_start(out.rearrange("b (t p) d -> p (b t) d", p=P)[:, 4 * m:4 * m + 4, :],
                             xres[:, 4 * m:4 * m + 4, :]).then_inc(out_done, 16)
            sp.wait_ge(out_done, 32)

        N_W0, N_VEC, N_W1 = 4 * 16, (11 + 6) * 16, 16 * 16

        def turned_to0(i):
            if i < 4:
                part, packed = divmod(i, 2)
                return k_b0[:, part, :, :, :] if packed else k_a0[:, part, :, :, 0:P]
            b, r = divmod(i - 4, 6)
            if r < 2:
                return q_s0[:, r, b * COLS:(b + 1) * COLS].rearrange("p (a k) -> p a k", a=4)
            part, h = divmod(r - 2, 2)
            return k_a0[:, part, b, h, P:5 * P].rearrange("p (a k) -> p a k", a=4)

        def turned_from0(i, a):
            if i < 4:
                part, packed = divmod(i, 2)
                b, h = divmod(a, 2)
                return st_c0[part][:, 2 * packed + b, h, :].bitcast(F32)
            b, r = divmod(i - 4, 6)
            if r < 2:
                return st_q0[:, 4 * b + a, r, :]
            part, h = divmod(r - 2, 2)
            return st_k0[:, part, 4 * b + a, h, :]

        def turned_bank0(i):
            shape = "p (a k) -> p a k" if i >= 4 else "p (b h k) -> p b h k"
            return ps[:, i % 8, :].rearrange(shape, k=P, **({} if i >= 4 else {"b": B}))

        BY_DVE = (11, 13, 15)

        def row_scores1(pe, t):
            b = t // TB
            pe.wait_ge(q1_turned, t + 1)
            for g in range(G1 + 1):
                if t >= 1 and g < G1:
                    pe.wait_ge(mx1_used, 5 * (t - 1) + g + 1)
                if t >= 2 and g == G1:
                    pe.wait_ge(mx1_used, 5 * (t - 1))
                if g < G1:
                    pe.matmul(ps[:, g, :], q_s1[:, g, t * P:(t + 1) * P],
                              k_a1[:, b, g, :, :].rearrange("p j k -> p (j k)"), start=True, stop=True)\
                        .then_inc(mx1_psum, 1)
                    continue
                for gg in range(G1):
                    last = pe.matmul(ps[:, 4 + t % 2, gg * P:(gg + 1) * P], q_s1[:, gg, t * P:(t + 1) * P],
                                     k_b1[:, b, gg, :], start=True, stop=True)
                last.then_inc(mx1_psum, 1)

        @block.gpsimd
        def _(pool):
            do = linked(pool, pool_link)
            pool.memset(mcol8[:, :], 0).then_inc(const_ready, 1)
            pool.memset(zero[:, :], 0.0)
            pool.memset(euler[:, :], math.e)
            pool.memset(half[:, :], -0.5).then_inc(const_ready, 1)
            do(pool.memset(ident[:, :], 0.0))
            pool.affine_select(out=ident[:, :], in_=ident[:, :], compare_op=ALU.not_equal, fill=1.0, base=0,
                               pattern=[[-1, P]], channel_multiplier=1).then_inc(const_ready, 1)
            pool.memset(comb_st[:, :, :], 0.0).then_inc(zeroed, 1)
            pool.memset(cT[:, 2:4, :], 0.0).then_inc(zeroed, 1)
            pool.memset(rT[:, 2:4, :], 0.0).then_inc(zeroed, 1)
            for q in ffn_sem:
                for name, count in HEAD_START.items():
                    pool.sem_inc(q[name], count)

            def power(count, dst, exponents, x=None):
                pool.wait_ge(var_ready, count)
                pool.tensor_tensor(dst, dst if x is None else x, exponents, ALU.pow).then_inc(rstd_ready, 1)

            pool.wait_ge(const_ready, 3)
            power(1, crstd[:, :], half[:, 0:4])
            power(2, rstd[:, :], half[:, 0:T])
            for x in (hh, hl):
                pool.memset(x[:, :, :].bitcast(F32), 0.0).then_inc(zeroed, 1)
            pool.memset(v_a[:, 0:2560], 1.0).then_inc(zeroed, 1)
            pool.memset(v_b[:, :], 0.0).then_inc(zeroed, 1)
            power(3, crn[:, :, :], half[:, 0:8].rearrange("p (a b) -> p a b", a=4), css[:, :, :])
            for m in range(2):
                tiles = slice(TB * m, TB * m + TB)
                power(4 + m, rn[:, tiles, :], half[:, 0:16].rearrange("p (a b) -> p a b", a=TB), ss[:, tiles, :])
            selF = probs[:, :, :].rearrange("p a n -> p (a n)")[:, 0:13 * P].rearrange("p (e m) -> p e m", e=13)
            do(pool.memset(selF, 0.0))
            for base in (0, -LO):
                do(pool.affine_select(out=selF, in_=selF, compare_op=ALU.not_equal, fill=1.0, base=base,
                                      pattern=[[-1, 13], [0, P]], channel_multiplier=1))
            do(pool.tensor_copy(sel[:, :, :], selF))
            for h in range(H0):
                last = pool.tensor_copy(selpk[:, 64 * h:64 * h + 64], sel[:, h, 0:64].bitcast(F32))
            last.then_inc(const_ready, 1)
            do(pool.iota(revi[:, :], pattern=[[-1, 16]], base=12, channel_multiplier=0))
            pool.tensor_copy(rev[:, :], revi[:, :]).then_inc(const_ready, 1)
            do(pool.memset(pad1[:, :], 0.0))
            for j in range(4):
                rows = pad1[32 * j:32 * j + 32, :]
                do(pool.affine_select(out=rows, in_=rows, compare_op=ALU.is_ge, fill=-BIG, base=KR - 1,
                                      pattern=[[0, 1]], channel_multiplier=-1))
            pool.memset(beR[:, :], 0.0).then_inc(const_ready, 1)
            pool.memset(be2[:, :], 0.0).then_inc(const_ready, 1)
            pool.wait_ge(turn_psum, 16)
            pool.memset(stage[:, 4096:6144], 0.0).then_inc(zeroed, 1)
            pool.memset(stage[:, 0:4096], 0.0).then_inc(zeroed, 1)

            def ffn(layer, between):
                L, q = LAYERS[layer], ffn_sem[layer]

                def split_up(e, k, b, blocks):
                    w = 2 * blocks * P
                    pool.wait_ge(q[("w_in_a", "w_in_b")[b]], 48 * (k + 1))
                    pool.tensor_tensor(wh[:, b, 0:w], raw[:, b, 0:w], zero[:, 0:1].broadcast_to([P, w]), ALU.add)\
                        .then_inc(q["w_high"], 1)
                    if layer == 1:
                        cols = slice(6 * e, 6 * e + 2 * blocks) if isinstance(e, int) else bass.ds(6 * e, 6)
                        pool.tensor_copy(biases[:, b, 0:2 * blocks], beT[:, cols])
                    pool.wait_ge(q["w_high"], 2 * e + 1)
                    pool.tensor_tensor(wl[:, b, 0:w], raw[:, b, 0:w], wh[:, b, 0:w].bitcast(F32),
                                       ALU.subtract).then_inc(q["up_split"], 1)

                def split_down(e, b, blocks):
                    cols = slice(2 * blocks * P, 3 * blocks * P)
                    pool.tensor_tensor(wh[:, b, cols], raw[:, b, cols], zero[:, 0:1].broadcast_to([P, blocks * P]),
                                       ALU.add).then_inc(q["w_high"], 1)
                    expert = slice(e, e + 1) if isinstance(e, int) else bass.ds(e, 1)
                    pool.tensor_copy(selp[:, b:b + 1, :], sel[:, expert, :])
                    pool.wait_ge(q["w_high"], 2 * e + 2)
                    pool.tensor_tensor(wl[:, b, cols], raw[:, b, cols], wh[:, b, cols].bitcast(F32),
                                       ALU.subtract).then_inc(q["w_split"], 1)

                def add_y(m, n):
                    pool.wait_ge(q["y_used"], m + 3)
                    pool.wait_ge(q["y_summed"], m + 1)
                    part = yT[:, n * COLS:(n + 1) * COLS]
                    pool.tensor_tensor(part, part, ytmp[:, n, :], ALU.add).then_inc(q["y_summed"], 1)

                if layer == 1:
                    pool.wait_ge(beT_ready, 1)
                    pool.wait_ge(ffn_sem[0]["down_done"], LAYERS[0].pairs * LAYERS[0].steps + 2)
                for e in range(2):
                    split_up(e, 0, e, L.blocks)
                    split_down(e, e, L.blocks)
                between()
                with pool.Fori(0, L.pairs - 1) as k:
                    for b in range(2):
                        used = L.steps * k + (b + 1) * 2 * L.blocks
                        pool.wait_ge(q["hid_ready"], used + 1)
                        split_up(2 * k + 2 + b, k + 1, b, L.blocks)
                        for n in range(2):
                            add_y(4 * k + 2 * b + n, n)
                        pool.wait_ge(q["down_done"], used + 2)
                        split_down(2 * k + 2 + b, b, L.blocks)
                k = L.pairs - 1
                for b in range(2):
                    used = L.steps * k + (b + 1) * 2 * L.blocks
                    if b == 0 and L.shared_blocks:
                        pool.wait_ge(q["hid_ready"], used + 1)
                        split_up(2 * k + 2, k + 1, 0, L.shared_blocks)
                    for n in range(2):
                        add_y(4 * k + 2 * b + n, n)
                    if b == 0 and L.shared_blocks:
                        pool.wait_ge(q["down_done"], used + 2)
                        split_down(2 * k + 2, 0, L.shared_blocks)
                if L.shared_blocks:
                    for n in range(2):
                        add_y(4 * k + 4 + n, n)

            def gap_exponential(count):
                pool.wait_ge(gap_ready, count)
                pool.tensor_tensor(small[:, 15, 0:T], euler[:, :], small[:, 15, 0:T], ALU.pow).then_inc(e_ready, 1)

            def before_layer0():
                power(6, rstd[:, 0:TB], half[:, 0:TB])
                pool.wait_ge(pv_done, 22)
                pool.memset(k_a[:, 0:4096].bitcast(F32), 0.0).then_inc(zeroed, 1)
                power(7, rstd[:, TB:T], half[:, 0:TB])
                gap_exponential(1)
                do(pool.memset(yT[:, :], 0.0))
                pool.sem_inc(ffn_sem[0]["y_summed"], 2)
                do(pool.memset(v_b[:, :], 0.0))
                do(pool.memset(v_a[:, :], 0.0))
                for j in range(4):
                    do(pool.memset(v_b[32 * j:32 * j + 32, :].rearrange("p (b g s) -> p b g s", b=B, g=G1)
                                   [:, :, :, 64 + 8 * j:72 + 8 * j], 1.0))
                for b in range(B):
                    last = pool.memset(v_a1[:, b, :, :].rearrange("p a (r s) -> p a r s", s=136)[:, :, :, 64:72], 1.0)
                last.then_inc(zeroed, 1)

            def before_layer1():
                power(10, rstd[:, 0:TB], half[:, 0:TB])
                power(11, rstd[:, TB:T], half[:, 0:TB])
                gap_exponential(2)
                pool.wait_ge(y_init, 2)
                pool.sem_inc(ffn_sem[1]["y_summed"], 2)

            ffn(0, before_layer0)
            power(8, rstd[:, 0:TB], half[:, 0:TB])
            power(9, rstd[:, TB:T], half[:, 0:TB])
            ffn(1, before_layer1)

        @block.scalar
        def _(act):
            def copy(dst, src):
                return act.activation(dst, src, ACT.Copy)

            def gate(layer, k, s, last):
                L, q = LAYERS[layer], ffn_sem[layer]
                u, j, blocks = L.place(s, last)
                g = L.steps * k + s
                act.wait_ge(q["g_ready"], g + 1)
                act.wait_ge(q["hid_ready"], max(g, 1) if isinstance(g, int) else g)
                bias = 0.0
                if layer == 1:
                    act.wait_ge(q["up_split"], 2 * k + u // 2 + 1)
                    bias = biases[:, (u // 2) % 2, blocks + j:blocks + j + 1]
                act.activation(act_out[:, s % 2, :], ps[:, s % 2, :], L.function, bias=bias)\
                    .then_inc(q["act_ready"], 1)

            def first_gates(layer):
                for s in range(2):
                    gate(layer, 0, s, False)

            def ffn(layer):
                L, q = LAYERS[layer], ffn_sem[layer]

                def high(k, s, last):
                    u, j, blocks = L.place(s, last)
                    g = L.steps * k + s
                    act.wait_ge(q["hid_ready"], g + 2)
                    act.wait_ge(q["down_done"], g + 1)
                    copy(hh[:, s % 2, :], ps[:, 2 + s % 4, :]).then_inc(q["hh_ready"], 1)
                    if j == 0:
                        m, n = 4 * k + u, u % 2
                        act.wait_ge(q["c_ready"], m + 1)
                        act.wait_ge(q["y_used"], m + 1)
                        copy(cbs[:, n, :], ps[:, 6 + n, :]).then_inc(q["c_copied"], 1)

                with act.Fori(0, L.pairs - 1) as k:
                    for s in range(L.steps):
                        high(k, s, False)
                        gate(layer, k, s + 2, False)
                k = L.pairs - 1
                for s in range(L.last_steps()):
                    high(k, s, True)
                    if s + 2 < L.last_steps():
                        gate(layer, k, s + 2, True)

            def exponentials(units, base, bias_of, between):
                for u in range(units):
                    if u in between:
                        between[u]()
                    act.wait_ge(scores_ready, base + u + 1)
                    if u >= 4:
                        act.wait_ge(pv_done, base + u - 3)
                    act.activation(probs[:, u % 4, :], ps[:, u % 4, :], ACT.Exp, bias=bias_of(u))\
                        .then_inc(probs_ready, 1)

            def turned_tokens(index, m, bank, parts):
                act.wait_ge(zT_psum, 2 * index + m + 1)
                cols = slice(m * COLS, (m + 1) * COLS)
                copy(zT[:, cols], ps[:, bank, :]).then_inc(zT_ready, 1)
                if parts:
                    copy(zh[:, cols], ps[:, bank, :]).then_inc(zh_ready, 1)

            def combine_columns(count):
                for m in range(2):
                    act.wait_ge(comb_psum, count + m + 1)
                    copy(combT[:, m * COLS:(m + 1) * COLS], ps[:, OWN[m], :]).then_inc(comb_ready, 1)

            act.wait_ge(vec_in, N_VEC)
            act.activation(tg[:, :], gates[:, :], ACT.Tanh).then_inc(gate_ready, 1)
            act.wait_ge(wT_psum, 1)
            copy(wcat[:, :], ps[:, 2, 0:3 * P])
            copy(wkvT[:, :], ps[0:DC, 3, 0:2 * P])
            copy(woT[:, :], ps[:, 3, 2 * P:3 * P]).then_inc(wT_ready, 1)
            act.wait_ge(cT_psum, 1)
            act.wait_ge(zeroed, 3)
            gain, shift = colv[0:DC, 2:3], colv[0:DC, 3:4]
            act.activation(cT[:, 0:2, :], ps[0:DC, 4, 0:2 * P].rearrange("p (b k) -> p b k", b=B), ACT.Identity,
                           scale=gain, bias=shift)
            copy(rT[:, 0:2, :], ps[0:DC, 5, 0:2 * P].rearrange("p (b k) -> p b k", b=B))
            for b in range(B):
                left = slice(2 * P + 32 * b, 2 * P + 32 * b + KR)
                for j in range(H0):
                    act.activation(cT[:, 2 + b, 64 * j:64 * j + KR], ps[0:DC, 4, left], ACT.Identity,
                                   scale=gain, bias=shift)
                for j in range(4):
                    last = copy(rT[:, 2 + b, 32 * j:32 * j + KR], ps[0:DC, 5, left])
            last.then_inc(cT_ready, 1)
            for m in range(2):
                act.wait_ge(zT_psum, m + 1)
                act.activation(zT[:, m * COLS:(m + 1) * COLS], ps[:, m, :], ACT.Identity,
                               scale=colv[:, 0:1], bias=colv[:, 1:2]).then_inc(zT_ready, 1)
            act.wait_ge(cproj_psum, 1)
            for m in range(2):
                copy(ckv[:, 2 * m:2 * m + 2, :], ps[:, 6 + m, :].rearrange("p (b c) -> p b c", b=B))\
                    .then_inc(cproj_used, 1)
            for t in range(T):
                act.wait_ge(proj_psum, t + 1)
                copy(qkv[:, t, :], ps[:, t % 4, 0:3 * P]).then_inc(proj_used, 1)
            act.wait_ge(zeroed, 7)
            act.wait_ge(proj_used, T)
            for b in range(B):
                for h in range(H0):
                    vals = slice(2 * P + HD0 * h, 2 * P + HD0 * h + HD0)
                    copy(v_a0[:, 5 * b + 1:5 * b + 5, h, 0:HD0], qkv[:, TB * b:TB * b + TB, vals])
            act.wait_ge(cproj_used, 2)
            for b in range(B):
                copy(v_a0[:, 5 * b, :, 0:HD0], ckv[:, b, P:2 * P].rearrange("p (h c) -> p h c", h=H0))
                for h in range(H0):
                    rows = slice(64 * h, 64 * h + 64)
                    last = copy(v_b0[rows, b, h, 0:HD0], ckv[rows, 2 + b, P + HD0 * h:P + HD0 * h + HD0])
            last.then_inc(kv_ready, 1)
            for i in range(16):
                if i in BY_DVE:
                    continue
                act.wait_ge(turn_psum, i + 1)
                copy(turned_to0(i), turned_bank0(i)).then_inc(turned_a, 1)
            for m in range(2):
                act.wait_ge(shift_psum, m + 1)
                copy(combT[:, m * COLS:(m + 1) * COLS], ps[:, m, :]).then_inc(shift_ready, 1)

            def bias0(u):
                b, r = divmod(u, 11)
                if r == 0:
                    return mcol[:, 2 + b:3 + b]
                return mcol[:, b:b + 1] if r % 5 == 1 else 0.0

            exponentials(22, 0, bias0, {TURN0 + 2: lambda: turned_tokens(1, 0, OWN[0], True)})

            first_gates(0)
            act.wait_ge(zeroed, 10)
            for i in range(4):
                act.wait_ge(k1_psum, i + 1)
                bank = ps[:, 5 + i % 2, :].rearrange("p (g k) -> p g k", g=G1)
                if i >= 2:
                    copy(k_b1[:, i - 2, :, :], bank).then_inc(k1_ready, 1)
                    continue
                for j in range(4):
                    rows = slice(32 * j, 32 * j + 32)
                    last = copy(k_a1[rows, i, :, j, :], bank[rows, :, :])
                last.then_inc(k1_ready, 1)
            turned_tokens(1, 1, OWN[1], True)
            combine_columns(0)
            ffn(0)

            act.wait_ge(beT_psum, 1)
            copy(beT[:, :], ps[:, 7, 0:76]).then_inc(beT_ready, 1)
            act.wait_ge(zeroed, 11)
            for b in range(B):
                copy(v_a1[:, b, :, :].rearrange("p a (r s) -> p a r s", s=136)[:, :, :, 0:8],
                     ckv[:, b, P:2 * P].rearrange("p (a r d) -> p a r d", a=2, r=8))
            vb = v_b[:, :].rearrange("p (b g s) -> p b g s", b=B, g=G1)
            for j in range(4):
                rows = slice(32 * j, 32 * j + 32)
                last = copy(vb[rows, :, :, 8 * j:8 * j + 8],
                            ckv[rows, 2:4, P:2 * P].rearrange("p b (g j d) -> p b g j d", g=G1, j=4)[:, :, :, j, :])
            last.then_inc(v1_ready, 1)
            for m in range(2):
                turned_tokens(2, m, m, False)

            def queries(done, t):
                copy(q_s1[:, :, t * P:(t + 1) * P], ps[:, 6 if done is q1_turned else 7, :]
                     .rearrange("p (g k) -> p g k", g=G1)).then_inc(done, 1)

            for t in range(T + 1):
                if t < T:
                    act.wait_ge(q1_turn_psum, t + 1)
                    queries(q1_turned, t)
                if t >= 2:
                    act.wait_ge(q1_full_psum, t - 1)
                    queries(q1_full, t - 2)
            act.wait_ge(q1_full_psum, T)
            queries(q1_full, T - 1)
            exponentials(40, 22, lambda u: pad1[:, :] if u % 5 == 4 else 0.0,
                         {TURN1 + 2: lambda: turned_tokens(3, 0, OWN[0], True)})

            first_gates(1)
            turned_tokens(3, 1, OWN[1], True)
            combine_columns(2)
            for m in range(2):
                act.wait_ge(yinit_psum, m + 1)
                copy(yT[:, m * COLS:(m + 1) * COLS], ps[:, OWN[m], :]).then_inc(y_init, 1)
            ffn(1)

        @block.tensor
        def _(pe):
            def turn(dst, src, rows=P):
                return pe.transpose(dst, src, ident[0:rows, 0:rows])

            def up(layer, k, s, last):
                L, q = LAYERS[layer], ffn_sem[layer]
                u, j, blocks = L.place(s, last)
                g = L.steps * k + s
                e, b, n = 2 * k + u // 2, (u // 2) % 2, u % 2
                if j == 0 and n == 0:
                    pe.wait_ge(q["up_split"], e + 1)
                if not isinstance(g, int) or g >= 2:
                    pe.wait_ge(q["act_ready"], g - 1)
                    pe.wait_ge(q["hl_ready"], g - 1)
                cols = slice(n * COLS, (n + 1) * COLS)
                for bank, at, done in ((s % 2, layer, "g_ready"), (2 + s % 4, 1 - layer, "u_ready")):
                    w = slice((at * blocks + j) * P, (at * blocks + j + 1) * P)
                    pe.matmul(ps[:, bank, :], wl[:, b, w], zh[:, cols], start=True, stop=False)
                    pe.matmul(ps[:, bank, :], wh[:, b, w], zl[:, cols], start=False, stop=False)
                    pe.matmul(ps[:, bank, :], wh[:, b, w], zh[:, cols], start=False, stop=True)\
                        .then_inc(q[done], 1)

            def turn_result(layer, m):
                q, units = ffn_sem[layer], 2 * LAYERS[layer].all_experts
                pe.wait_ge(q["y_summed"], units + m + 1)
                for t in range(TB):
                    last = turn(ps[:, m, t * P:(t + 1) * P], yT[:, (TB * m + t) * P:(TB * m + t + 1) * P])
                last.then_inc(y_turned, 1)

            def first_ups(layer):
                for s in range(LEAD):
                    up(layer, 0, s, False)

            def ffn(layer):
                L, q = LAYERS[layer], ffn_sem[layer]

                def spread(m, e, b, n):
                    if n == 0:
                        pe.wait_ge(q["w_split"], e + 1)
                    pe.wait_ge(q["y_used"], m + 1)
                    pe.matmul(ps[:, 6 + n, :], selp[:, b, :], combT[:, n * COLS:(n + 1) * COLS],
                              start=True, stop=True).then_inc(q["c_ready"], 1)

                def down(k, s, last):
                    u, j, blocks = L.place(s, last)
                    g = L.steps * k + s
                    m, b, n = 4 * k + u, (u // 2) % 2, u % 2
                    if j == 0:
                        pe.wait_ge(q["c_copied"], m + 3)
                    pe.wait_ge(q["hh_ready"], g + 1)
                    pe.wait_ge(q["hl_ready"], g + 3)
                    w = slice((2 * blocks + j) * P, (2 * blocks + j + 1) * P)
                    bank = ps[:, 6 + n, :]
                    pe.matmul(bank, wl[:, b, w], hh[:, s % 2, :], start=(j == 0), stop=False)
                    pe.matmul(bank, wh[:, b, w], hl[:, s % 2, :], start=False, stop=False)
                    pe.matmul(bank, wh[:, b, w], hh[:, s % 2, :], start=False, stop=(j == blocks - 1))\
                        .then_inc(q["down_done"], 1)
                    if j == blocks - 1 and not (last and s + 1 == L.last_steps()):
                        spread(m + 1, 2 * k + (u + 1) // 2, ((u + 1) // 2) % 2, (u + 1) % 2)

                spread(0, 0, 0, 0)
                with pe.Fori(0, L.pairs - 1) as k:
                    for s in range(L.steps):
                        up(layer, k, s + LEAD, False)
                        down(k, s, False)
                k = L.pairs - 1
                for s in range(L.last_steps()):
                    if s + LEAD < L.last_steps():
                        up(layer, k, s + LEAD, True)
                    if s + 1 == L.last_steps():
                        turn_result(layer, 0)
                    down(k, s, True)
                turn_result(layer, 1)

            def turn_tokens(index, m, bank):
                for t in range(TB * m, TB * m + TB):
                    pe.wait_ge(z_ready, T * index + t + 1)
                    last = turn(ps[:, bank, t % TB * P:(t % TB + 1) * P], z[:, t, :])
                last.then_inc(zT_psum, 1)

            def attend(units, base, scores, values, between):
                def score(u):
                    if u >= 4:
                        pe.wait_ge(probs_ready, base + u - 3)
                    scores(u, ps[:, u % 4, :]).then_inc(scores_ready, 1)

                score(0)
                score(1)
                for u in range(units):
                    if u in between:
                        between[u]()
                    if u + 2 < units:
                        score(u + 2)
                    pe.wait_ge(probs_ready, base + u + 1)
                    values(u, probs[:, u % 4, :]).then_inc(pv_done, 1)

            def project_out(layer, m, w):
                pe.wait_ge(oT_ready, 4 * layer + 2 * m + 2)
                for t in range(TB * m, TB * m + TB):
                    last = pe.matmul(ps[:, OWN[m], t % TB * P:(t % TB + 1) * P], oT[:, t * P:(t + 1) * P], w,
                                     start=True, stop=True)
                last.then_inc(o_psum, 1)

            def turn_attended(layer, m):
                pe.wait_ge(res_ready, 2 * layer + m + 1)
                turn_tokens(2 * layer + 1, m, OWN[m])

            def route(layer, m, w, experts):
                pe.wait_ge(zT_ready, 4 * layer + 2 + m + 1)
                for t in range(TB * m, TB * m + TB):
                    last = pe.matmul(ps[:, OWN[m] - 1, t * 16:t * 16 + experts], zT[:, t * P:(t + 1) * P], w,
                                     start=True, stop=True)
                last.then_inc(route_psum, 1)

            def turn_combine(layer):
                pe.wait_ge(comb_staged, layer + 1)
                for t in range(T):
                    last = turn(ps[:, OWN[t // TB], t % TB * P:(t % TB + 1) * P], comb_st[:, t, :])
                    if t % TB == TB - 1:
                        last.then_inc(comb_psum, 1)

            def wait_parts(layer, m):
                pe.wait_ge(zh_ready, 2 * layer + m + 1)
                pe.wait_ge(zl_ready, 2 * layer + m + 1)

            def before_experts(layer):
                wait_parts(layer, 1)
                pe.wait_ge(comb_ready, 2 * layer + 2)

            def keys1():
                pe.wait_ge(w1_in, N_W1)
                for m in range(4):
                    last = pe.matmul(ps[:, 6 + m // 2, m % 2 * 256:m % 2 * 256 + 256], rT[:, m, :],
                                     w1c[:, :, :].rearrange("p a c -> p (a c)"), start=True, stop=True)
                last.then_inc(kv1_psum, 1)

            def turn_keys1(i):
                pe.wait_ge(k1_staged, 1)
                if i >= 2:
                    pe.wait_ge(k1_ready, i - 1)
                for g in range(G1):
                    last = turn(ps[:, 5 + i % 2, g * P:(g + 1) * P],
                                st_k1[:, i, 4 * g:4 * g + 4, :].rearrange("p h c -> p (h c)"))
                last.then_inc(k1_psum, 1)

            pe.wait_ge(const_ready, 3)
            pe.wait_ge(w0_in, N_W0)
            turn(ps[:, 2, 0:P], wq0[:, :])
            turn(ps[:, 2, P:2 * P], wlkv[:, 0, :])
            turn(ps[:, 2, 2 * P:3 * P], wlkv[:, 1, :])
            turn(ps[0:DC, 3, 0:P], wkv[:, 0, :])
            turn(ps[0:DC, 3, P:2 * P], wkv[:, 1, :])
            turn(ps[:, 3, 2 * P:3 * P], wo0[:, :]).then_inc(wT_psum, 1)
            pe.wait_ge(ctx_in, 32)
            pe.wait_ge(cz_ready, 4)
            for bank, src in ((4, ctx_z), (5, ctx_rows)):
                for b in range(B):
                    turn(ps[0:DC, bank, b * P:(b + 1) * P], src[:, b, :])
                    last = turn(ps[0:DC, bank, 2 * P + 32 * b:2 * P + 32 * b + KR], src[0:KR, 2 + b, :], KR)
            last.then_inc(cT_psum, 1)
            for m in range(2):
                turn_tokens(0, m, m)
            pe.wait_ge(wT_ready, 1)
            pe.wait_ge(cT_ready, 1)
            for m in range(4):
                last = pe.matmul(ps[:, 6 + m // 2, m % 2 * 256:m % 2 * 256 + 256], cT[:, m, :], wkvT[:, :],
                                 start=True, stop=True)
            last.then_inc(cproj_psum, 1)
            pe.wait_ge(zT_ready, 2)
            for t in range(T):
                if t >= 4:
                    pe.wait_ge(proj_used, t - 3)
                pe.matmul(ps[:, t % 4, 0:3 * P], zT[:, t * P:(t + 1) * P], wcat[:, :], start=True, stop=True)\
                    .then_inc(proj_psum, 1)
            pe.wait_ge(proj_used, T)
            pe.wait_ge(cproj_used, 2)
            for i in range(16):
                pe.wait_ge(staged, 1 + (i >= 4) + (i >= 6) + (i >= 10) + (i >= 12))
                if i >= 8:
                    pe.wait_ge(turned_a, i - 7)
                for a in range(4):
                    last = turn(ps[:, i % 8, a * P:(a + 1) * P], turned_from0(i, a))
                last.then_inc(turn_psum, 1)
            pe.wait_ge(turned_a, 16 - len(BY_DVE))
            pe.wait_ge(turned_v, len(BY_DVE))
            pe.wait_ge(const_ready, 4)
            for u in range(2 * T):
                t, h = divmod(u, 2)
                b = t // TB
                if u >= 4:
                    pe.wait_ge(mx_used, u - 3)
                q = q_s0[:, h, t * P:(t + 1) * P]
                lat, con = ps[:, 2 * (u % 4), :], ps[:, 2 * (u % 4) + 1, :]
                pe.matmul(lat, q, k_a0[:, 0, b, h, P:5 * P], start=True, stop=True)
                pe.matmul(con[:, 0:P], q, k_a0[:, 0, b, h, 0:P], start=True, stop=False, skip_group_check=True)
                pe.matmul(con[:, P:CK], q, k_b0[:, 0, b, h, 64 * h:64 * h + KR], start=True, stop=False,
                          skip_group_check=True)
                pe.matmul(con[:, 0:CK], sel[0:1, 0, :], mask_row[:, b, :], start=False, stop=True,
                          skip_group_check=True).then_inc(mx_psum, 1)
            pe.wait_ge(mx_used, 2 * T)
            pe.wait_ge(shift_staged, 1)
            for t in range(T):
                last = turn(ps[:, t // 4, t % 4 * P:(t % 4 + 1) * P], comb_st[:, t, :])
                if t % 4 == 3:
                    last.then_inc(shift_psum, 1)

            def scores0(u, bank):
                b, r = divmod(u, 11)
                h, block = divmod(r - 1, 5)
                n = slice(b * COLS, (b + 1) * COLS)
                for i, h in enumerate((0, 1) if r == 0 else (h,)):
                    for part in range(2):
                        k = k_b0[:, part, b, h, :] if r == 0 else k_a0[:, part, b, h, block * P:(block + 1) * P]
                        pe.matmul(bank, k, q_s0[:, h, n], start=(i == 0 and part == 0), stop=False)
                return pe.matmul(bank, selpk[:, :] if r == 0 else sel[:, h, :], combT[:, n], start=False, stop=True)

            def values0(u, p):
                b, r = divmod(u, 11)
                if r > 0:
                    h, block = divmod(r - 1, 5)
                    return pe.matmul(ps[:, 4 + 2 * b + h, :], v_a0[:, 5 * b + block, h, :], p,
                                     start=False, stop=(block == 4), skip_group_check=True)
                for h in range(H0):
                    last = pe.matmul(ps[:, 4 + 2 * b + h, :], v_b0[:, b, h, :], p, start=True, stop=False,
                                     skip_group_check=True)
                return last

            pe.wait_ge(shift_ready, 2)
            pe.wait_ge(kv_ready, 2)
            attend(22, 0, scores0, values0,
                   {KEYS1: keys1, 11: lambda: pe.wait_ge(k1_staged, 1),
                    PROJECT0: lambda: project_out(0, 0, woT[:, :]), TURN0: lambda: turn_attended(0, 0),
                    ROUTE0: lambda: route(0, 0, wr0[:, :], E0)})

            wait_parts(0, 0)
            first_ups(0)
            turn_keys1(0)
            project_out(0, 1, woT[:, :])
            for i in range(1, 4):
                turn_keys1(i)
            turn_attended(0, 1)
            pe.wait_ge(k1_ready, 4)
            route(0, 1, wr0[:, :], E0)
            turn_combine(0)
            before_experts(0)
            ffn(0)

            turn(ps[:, 7, 0:P], beR[:, :]).then_inc(beT_psum, 1)
            for m in range(2):
                turn_tokens(2, m, m)
                pe.wait_ge(zT_ready, 4 + m + 1)
                for t in range(TB * m, TB * m + TB):
                    last = pe.matmul(ps[:, 2 + m, t % TB * P:(t % TB + 1) * P], zT[:, t * P:(t + 1) * P],
                                     w1[:, 0, :], start=True, stop=True)
                last.then_inc(q1_psum, 1)
            pe.wait_ge(beT_ready, 1)

            def turn_queries(t, bank, done):
                for g in range(G1):
                    last = turn(ps[:, bank, g * P:(g + 1) * P],
                                st_q1[:, t, 4 * g:4 * g + 4, :].rearrange("p h c -> p (h c)"))
                last.then_inc(done, 1)

            def full_queries(t):
                pe.wait_ge(shift1_staged, t + 1)
                if t >= 1:
                    pe.wait_ge(q1_full, t)
                turn_queries(t, 7, q1_full_psum)

            for t in range(T):
                pe.wait_ge(q1_staged, t // 4 + 1)
                if t >= 1:
                    pe.wait_ge(q1_turned, t)
                turn_queries(t, 6, q1_turn_psum)
                if t == 1:
                    pe.wait_ge(q1_staged, 2)
                if t >= 1:
                    row_scores1(pe, t - 1)
                if t >= 2:
                    full_queries(t - 2)
            row_scores1(pe, T - 1)
            full_queries(T - 2)
            full_queries(T - 1)

            def scores1(u, bank):
                b, r = divmod(u, 20)
                g, j = divmod(r, 5)
                k = k_b1[:, b, g, :] if j == 4 else k_a1[:, b, g, j, :]
                return pe.matmul(bank, k, q_s1[:, g, b * COLS:(b + 1) * COLS], start=True, stop=True)

            def values1(u, p):
                b, r = divmod(u, 20)
                g, j = divmod(r, 5)
                a, c = divmod(g, 2)
                if j == 4:
                    v = v_b1[:, b, a, c * P:(c + 1) * P]
                else:
                    v = v_a1[:, b, a, (4 * c + j) * P:(4 * c + j + 1) * P]
                return pe.matmul(ps[:, 4 + 2 * b + a, :], v, p, start=(c == 0 and j == 0), stop=(c == 1 and j == 4))

            pe.wait_ge(q1_full, T)
            pe.wait_ge(mx1_used, 5 * T)
            pe.wait_ge(v1_ready, 1)
            attend(40, 22, scores1, values1,
                   {PROJECT1: lambda: project_out(1, 0, w1[:, 1, :]), TURN1: lambda: turn_attended(1, 0),
                    ROUTE1: lambda: route(1, 0, wr1[:, :], E1)})

            wait_parts(1, 0)
            first_ups(1)
            project_out(1, 1, w1[:, 1, :])
            turn_attended(1, 1)
            route(1, 1, wr1[:, :], E1)
            turn_combine(1)
            before_experts(1)
            for m in range(2):
                pe.matmul(ps[:, OWN[m], :], be2[:, :], combT[:, m * COLS:(m + 1) * COLS].bitcast(F32),
                          start=True, stop=True).then_inc(yinit_psum, 1)
            pe.wait_ge(y_init, 2)
            ffn(1)

        @block.vector
        def _(dve):
            do = linked(dve, dve_link)

            def statistics(x, st, out_mv, parts):
                for i, (rows, m) in enumerate(parts):
                    do(dve.bn_stats(st[0:rows, m, :], x[0:rows, m, :]), i == len(parts) - 1)
                for i, (rows, m) in enumerate(parts):
                    do(dve.bn_aggr(out_mv[0:rows, m, :], st[0:rows, m, :]), i == len(parts) - 1)

            def variance(tiles, twice=False):
                statistics(xres, stats, mv, [(P, t) for t in tiles])
                part = slice(tiles[0], tiles[-1] + 1)
                var = mv[:, part, 1:2].rearrange("p t o -> p (t o)")
                a, c = (1 + LN_EPS, LN_EPS * LN_EPS) if twice else (1.0, LN_EPS)
                dve.tensor_scalar(rstd[:, part], var, a, c, ALU.mult, ALU.add).then_inc(var_ready, 1)

            def scale_tokens(tiles, count):
                dve.wait_ge(rstd_ready, count)
                for t in tiles:
                    dve.tensor_scalar(z[:, t, :], xres[:, t, :], mv[:, t, 0:1], rstd[:, t:t + 1],
                                      ALU.subtract, ALU.mult).then_inc(z_ready, 1)

            def add_bias(index, bias):
                dve.wait_ge(gate_ready, 1)
                dve.wait_ge(z_ready, T * (index + 1))
                do(dve.scalar_tensor_tensor(out=xres[:, :, :], in0=bias.unsqueeze(1).broadcast_to([P, T, D]),
                                            scalar=tg[:, index // 2:index // 2 + 1], in1=xres[:, :, :],
                                            op0=ALU.mult, op1=ALU.add))

            def divide_by_sums(layer, b, i):
                dve.wait_ge(pv_done, (11 * b + (6, 11)[i], 22 + 20 * b + 10 * (i + 1))[layer])
                bank = ps[:, 4 + 2 * b + i, :]
                before = 4 * layer + 2 * b + i
                if before:
                    dve.wait_ge(oT_ready, before)
                do(dve.reciprocal(rcp, bank[64:P, :]))
                dve.tensor_tensor(oT[64 * i:64 * i + 64, b * COLS:(b + 1) * COLS], bank[0:64, :],
                                  rcp, ALU.mult).then_inc(oT_ready, 1)

            def add_attention(layer, m):
                dve.wait_ge(o_psum, 2 * layer + m + 1)
                part = xres[:, 4 * m:4 * m + 4, :].rearrange("p t d -> p (t d)")
                dve.scalar_tensor_tensor(out=part, in0=ps[:, OWN[m], :], scalar=tg[:, layer:layer + 1],
                                         in1=part, op0=ALU.mult, op1=ALU.add).then_inc(res_ready, 1)
                dve.wait_ge(res_ready, 2 * layer + m + 1)

            def low_tokens(layer, m):
                dve.wait_ge(zh_ready, 2 * layer + m + 1)
                cols = slice(m * COLS, (m + 1) * COLS)
                dve.tensor_tensor(zl[:, cols], ps[:, OWN[m], :], zh[:, cols].bitcast(F32), ALU.subtract)\
                    .then_inc(zl_ready, 1)

            def logits(layer, m, experts):
                dve.wait_ge(route_psum, 2 * layer + m + 1)
                tiles = slice(TB * m, TB * m + TB)
                src = ps[:, OWN[m] - 1, 0:T * 16].rearrange("p (t e) -> p t e", t=T)[:, tiles, 0:experts]
                dst = small[:, 0, 0:T * experts].rearrange("p (t e) -> p t e", t=T)[:, tiles, :]
                if layer == 0:
                    do(dve.tensor_copy(dst, src))
                else:
                    do(dve.tensor_tensor(dst, src, br[:, :].unsqueeze(1).broadcast_to([P, TB, experts]), ALU.add))

            def add_result(layer, m):
                dve.wait_ge(y_turned, 2 * layer + m + 1)
                part = xres[:, 4 * m:4 * m + 4, :].rearrange("p t d -> p (t d)")
                dve.tensor_tensor(part, part, ps[:, m, :], ALU.add).then_inc(y_added, 1)
                dve.wait_ge(y_added, 2 * layer + m + 1)

            def multiply(layer, k, s, last):
                bank = ps[:, 2 + s % 4, :]
                L, q = LAYERS[layer], ffn_sem[layer]
                u, j, blocks = L.place(s, last)
                g = L.steps * k + s
                dve.wait_ge(q["act_ready"], g + 1)
                dve.wait_ge(q["u_ready"], g + 1)
                if layer == 0:
                    ins = dve.tensor_tensor(bank, bank, act_out[:, s % 2, :], ALU.mult)
                else:
                    ins = dve.scalar_tensor_tensor(
                        out=bank, in0=bank, scalar=biases[:, (u // 2) % 2, j:j + 1],
                        in1=act_out[:, s % 2, :], op0=ALU.add, op1=ALU.mult)
                ins.then_inc(q["hid_ready"], 1)

            def attended(layer, experts, count):
                for i in range(2):
                    divide_by_sums(layer, 0, i)
                add_attention(layer, 0)
                variance(range(0, TB))
                scale_tokens(range(0, TB), count)
                logits(layer, 0, experts)
                low_tokens(layer, 0)
                for i in range(2):
                    divide_by_sums(layer, 1, i)
                multiply(layer, 0, 0, False)
                add_attention(layer, 1)
                variance(range(TB, T))
                multiply(layer, 0, 1, False)
                scale_tokens(range(TB, T), count + 1)
                low_tokens(layer, 1)
                logits(layer, 1, experts)

            def choose(layer, experts):
                def v(i, n=experts):
                    return small[:, i, 0:T * n].rearrange("p (t e) -> p t e", t=T)

                def row(i):
                    return small[:, i, 0:T]

                def over(i, n=experts):
                    return small[:, i, 0:T].unsqueeze(2).broadcast_to([P, T, n])

                first = rev[:, 0:experts].unsqueeze(1).broadcast_to([P, T, experts])
                dve.wait_ge(const_ready, 7)
                if layer == 1:
                    do(dve.tensor_scalar(v(0), v(0), 1.0 / TAU, None, ALU.mult))
                for i, source in ((0, 0), (1, 5)):
                    do(dve.tensor_reduce(row(13 + i), v(source), AX.X, ALU.max))
                    do(dve.tensor_tensor(v(3), v(source), over(13 + i), ALU.is_equal))
                    do(dve.tensor_tensor(v(3), v(3), first, ALU.mult))
                    do(dve.tensor_reduce(row(4), v(3), AX.X, ALU.max))
                    do(dve.tensor_tensor(v(1 + i), v(3), over(4), ALU.is_equal))
                    if i == 0:
                        do(dve.scalar_tensor_tensor(out=v(5), in0=v(1), scalar=-BIG, in1=v(0), op0=ALU.mult, op1=ALU.add))
                dve.tensor_tensor(row(15), row(14), row(13), ALU.subtract).then_inc(gap_ready, 1)
                dve.wait_ge(e_ready, layer + 1)
                do(dve.tensor_scalar(row(6), row(15), 1.0, None, ALU.add))
                do(dve.reciprocal(row(7), row(6)))
                scale = DEPTH_SCALE if layer == 0 else 1.0
                do(dve.tensor_scalar(row(7), row(7), tg[:, 2 + layer:3 + layer], scale, ALU.mult, ALU.mult))
                do(dve.tensor_tensor(row(8), row(15), row(7), ALU.mult))
                do(dve.tensor_tensor(v(9), v(1), over(7), ALU.mult))
                do(dve.tensor_tensor(v(10), v(2), over(8), ALU.mult))
                cols = LAYERS[layer].all_experts
                w = comb_w[:, :, 0:cols]
                do(dve.tensor_tensor(comb_w[:, :, 0:experts], v(9), v(10), ALU.add))
                if cols > experts:
                    do(dve.tensor_copy(comb_w[:, :, experts:cols], tg[:, 3:4].unsqueeze(1).broadcast_to([P, T, 1])))
                do(dve.tensor_copy(comb_st[:, :, 0:cols].bitcast(F32R), w))
                dve.tensor_tensor(comb_st[:, :, LO:LO + cols].bitcast(F32R), w, comb_st[:, :, 0:cols], ALU.subtract)\
                    .then_inc(comb_staged, 1)

            def ffn(layer):
                L, q = LAYERS[layer], ffn_sem[layer]

                def low(k, s):
                    g = L.steps * k + s
                    dve.wait_ge(q["hid_ready"], g + 2)
                    dve.wait_ge(q["hh_ready"], g + 1)
                    dve.wait_ge(q["down_done"], g + 1)
                    dve.tensor_tensor(hl[:, s % 2, :], ps[:, 2 + s % 4, :], hh[:, s % 2, :].bitcast(F32),
                                      ALU.subtract).then_inc(q["hl_ready"], 1)

                def weigh(k, u, end):
                    m, n = 4 * k + u, u % 2
                    dve.wait_ge(q["down_done"], L.steps * k + end + 2)
                    dve.wait_ge(q["c_copied"], m + 3)
                    dve.wait_ge(q["y_summed"], m + 1)
                    dve.tensor_tensor(ytmp[:, n, :], ps[:, 6 + n, :], cbs[:, n, :], ALU.mult).then_inc(q["y_used"], 1)

                low(0, 0)
                with dve.Fori(0, L.pairs - 1) as k:
                    for s in range(1, L.steps + 1):
                        multiply(layer, k, s + 1, False)
                        low(k, s)
                        if s % L.blocks == 0:
                            weigh(k, s // L.blocks - 1, s)
                k, total = L.pairs - 1, L.last_steps()
                for s in range(1, total + 1):
                    if s + 1 < total:
                        multiply(layer, k, s + 1, True)
                    if s < total:
                        low(k, s)
                    else:
                        add_result(layer, 0)
                    u, j, blocks = L.place(s - 1, True)
                    if j == blocks - 1:
                        weigh(k, u, s)

            do(dve.memset(crstd[:, :], 1.0))
            dve.wait_ge(ctx_in, 32)
            statistics(ctx_rows, cstats, cmv, [(P, 0), (P, 1), (KR, 2), (KR, 3)])
            do(dve.tensor_scalar(crstd[:, 0:2], cmv[:, 0:2, 1:2].rearrange("p a o -> p (a o)"), LN_EPS, None, ALU.add))
            dve.tensor_scalar(crstd[0:KR, 2:4], cmv[0:KR, 2:4, 1:2].rearrange("p a o -> p (a o)"), LN_EPS, None,
                              ALU.add).then_inc(var_ready, 1)
            dve.wait_ge(rstd_ready, 1)
            for m in range(4):
                rows = slice(0, P if m < 2 else KR)
                dve.tensor_scalar(ctx_z[rows, m, :], ctx_rows[rows, m, :], cmv[rows, m, 0:1], crstd[rows, m:m + 1],
                                  ALU.subtract, ALU.mult).then_inc(cz_ready, 1)
            dve.wait_ge(x_in, 16)
            variance(range(T), twice=True)
            scale_tokens(range(T), 2)
            dve.wait_ge(vec_in, N_VEC)
            add_bias(0, bo0[:, :])
            do(dve.tensor_scalar(mask_row[:, :, :].rearrange("p b k -> p (b k)"), mask8[:, :], BIG, -BIG, ALU.mult, ALU.add))
            do(dve.tensor_scalar(mcol[:, :], mcol8[:, :], BIG, -BIG, ALU.mult, ALU.add))
            do(dve.tensor_tensor(gqk[:, :], gq[:, :], gk[:, :], ALU.mult))
            do(dve.tensor_scalar(gqk[:, :], gqk[:, :], HD0 ** -0.5, None, ALU.mult))

            dve.wait_ge(cproj_used, 2)
            ckeys = ckv[:, :, 0:P].rearrange("p m (h c) -> p m h c", h=H0)
            csq = stage[:, 0:4 * P].rearrange("p (m h c) -> p m h c", m=4, h=H0)
            do(dve.tensor_tensor(csq, ckeys, ckeys, ALU.mult))
            do(dve.tensor_reduce(css[:, :, :], csq, AX.X, ALU.add))
            dve.tensor_scalar(css[:, :, :], css[:, :, :], 1.0 / HD0, RMS_EPS2, ALU.mult, ALU.max).then_inc(var_ready, 1)
            qk = qkv[:, :, 0:2 * P].rearrange("p t (h c) -> p t h c", h=4)
            sq = stage[:, 0:2048].rearrange("p (t h c) -> p t h c", t=T, h=4)
            for m in range(2):
                tiles = slice(TB * m, TB * m + TB)
                dve.wait_ge(proj_used, TB * m + TB)
                do(dve.tensor_tensor(sq[:, tiles], qk[:, tiles], qk[:, tiles], ALU.mult))
                do(dve.tensor_reduce(ss[:, tiles, :], sq[:, tiles], AX.X, ALU.add))
                dve.tensor_scalar(ss[:, tiles, :], ss[:, tiles, :], 1.0 / HD0, RMS_EPS2, ALU.mult, ALU.max)\
                    .then_inc(var_ready, 1)
            dve.wait_ge(rstd_ready, 3)
            do(dve.tensor_tensor(ckeys, ckeys, crn[:, :, :].unsqueeze(3).broadcast_to([P, 4, H0, HD0]), ALU.mult))
            dve.wait_ge(zeroed, 5)
            for rows, blocks, heads in ((slice(0, P), slice(0, 2), slice(0, 2)),
                                        (slice(0, 64), slice(2, 4), slice(0, 1)), (slice(64, P), slice(2, 4), slice(1, 2))):
                src = ckeys[rows, blocks, heads, :]
                for dup in range(2):
                    do(dve.tensor_copy(st_c0[0][rows, blocks, heads, 64 * dup:64 * dup + 64], src))
                for dup in range(2):
                    last = dve.tensor_tensor(st_c0[1][rows, blocks, heads, 64 * dup:64 * dup + 64], src,
                                             st_c0[0][rows, blocks, heads, 0:64].bitcast(F32), ALU.subtract)
            last.then_inc(staged, 1)
            for m in range(2):
                tiles = slice(TB * m, TB * m + TB)
                dve.wait_ge(rstd_ready, 4 + m)
                do(dve.tensor_tensor(qk[:, tiles], qk[:, tiles],
                                     rn[:, tiles, :].unsqueeze(3).broadcast_to([P, TB, 4, HD0]), ALU.mult))
                for h in range(H0):
                    qh = qk[:, tiles, h, :]
                    do(dve.tensor_tensor(qh, qh, gqk[:, :].unsqueeze(1).broadcast_to([P, TB, HD0]), ALU.mult),
                       h == H0 - 1)
                qq, kk = qk[:, tiles, 0:2, :], qk[:, tiles, 2:4, :]
                q_hi, q_lo = st_q0[:, tiles, :, 0:64], st_q0[:, tiles, :, 64:P]
                do(dve.tensor_copy(q_hi.bitcast(F32R), qq), False)
                k_hi = [st_k0[:, 0, tiles, :, 64 * dup:64 * dup + 64] for dup in range(2)]
                k_lo = [st_k0[:, 1, tiles, :, 64 * dup:64 * dup + 64] for dup in range(2)]
                do(dve.tensor_copy(k_hi[0].bitcast(F32R), kk), False)
                do(dve.tensor_copy(k_hi[1].bitcast(F32R), kk))
                dve.tensor_tensor(q_lo.bitcast(F32R), qq, q_hi, ALU.subtract).then_inc(staged, 1)
                for dup in range(2):
                    last = dve.tensor_tensor(k_lo[dup].bitcast(F32R), kk, k_hi[0], ALU.subtract)
                last.then_inc(staged, 1)
            dve.wait_ge(zeroed, 7)
            for h in range(H0):
                last = dve.memset(v_b0[64 * h:64 * h + 64, :, h, 64:P], 1.0)
            last.then_inc(kv_ready, 1)
            for i in BY_DVE:
                dve.wait_ge(turn_psum, i + 1)
                dve.tensor_copy(turned_to0(i), turned_bank0(i)).then_inc(turned_v, 1)
            for u in range(2 * T):
                t, h = divmod(u, 2)
                dve.wait_ge(mx_psum, u + 1)
                row = ps[:, 2 * (u % 4):2 * (u % 4) + 2, :].rearrange("p a n -> p (a n)")[:, 0:COLS + CK]
                dve.tensor_reduce(mx[:, t, h:h + 1], row, AX.X, ALU.max).then_inc(mx_used, 1)
            dve.wait_ge(mx_used, 2 * T)
            dve.wait_ge(zeroed, 1)
            dve.tensor_scalar(comb_st[:, :, 0:2].bitcast(F32R), mx[:, :, 0:H0],
                              -1.0, None, ALU.mult).then_inc(shift_staged, 1)
            dve.wait_ge(w1_in, N_W1)
            dve.wait_ge(kv_ready, 2)
            for m in range(2):
                dve.wait_ge(kv1_psum, 1)
                do(dve.tensor_tensor(ckv[:, 2 * m:2 * m + 2, :], ps[:, 6 + m, :].rearrange("p (b c) -> p b c", b=B),
                                     b1[:, 1:3, :].rearrange("p a c -> p (a c)").unsqueeze(1).broadcast_to([P, B, 2 * P]),
                                     ALU.add))
            dve.wait_ge(zeroed, 8)
            for rows, blocks, j in [(slice(0, P), slice(0, 2), None)] + \
                    [(slice(32 * j, 32 * j + 32), slice(2, 4), j) for j in range(4)]:
                heads = slice(0, H1) if j is None else slice(j, H1, 4)
                src = ckv[rows, blocks, 0:P].rearrange("p m (h d) -> p m h d", h=H1)[:, :, heads, :]
                dst = st_k1[rows, blocks, heads, :]
                do(dve.tensor_copy(dst[:, :, :, 0:8].bitcast(F32R), src))
                dve.tensor_copy(dst[:, :, :, 8:16].bitcast(F32R), src)
                dve.tensor_tensor(dst[:, :, :, 16:24].bitcast(F32R), src, dst[:, :, :, 0:8], ALU.subtract)
                last = dve.memset(dst[:, :, :, 24:25], 1.0)
            last.then_inc(k1_staged, 1)
            do(dve.tensor_scalar(b1[:, 0, :], b1[:, 0, :], HD1 ** -0.5, None, ALU.mult))
            attended(0, E0, 6)

            choose(0, E0)
            ffn(0)
            variance(range(0, TB))
            add_result(0, 1)
            scale_tokens(range(0, TB), 8)
            variance(range(TB, T))
            scale_tokens(range(TB, T), 9)
            dve.wait_ge(zeroed, 9)
            for m in range(2):
                dve.wait_ge(q1_psum, m + 1)
                dst = qkv[:, 4 * m:4 * m + 4, 0:P]
                do(dve.scalar_tensor_tensor(out=dst, in0=ps[:, 2 + m, :].rearrange("p (t c) -> p t c", t=4),
                                            scalar=HD1 ** -0.5, in1=b1[:, 0, :].unsqueeze(1).broadcast_to([P, 4, P]),
                                            op0=ALU.mult, op1=ALU.add))
                src = dst.rearrange("p t (h d) -> p t h d", h=H1)
                st = st_q1[:, 4 * m:4 * m + 4, :, :]
                do(dve.tensor_copy(st[:, :, :, 0:8].bitcast(F32R), src))
                dve.tensor_copy(st[:, :, :, 16:24].bitcast(F32R), src)
                dve.tensor_tensor(st[:, :, :, 8:16].bitcast(F32R), src, st[:, :, :, 0:8], ALU.subtract)\
                    .then_inc(q1_staged, 1)
            for t in range(T):
                for g in range(G1 + 1):
                    dve.wait_ge(mx1_psum, 5 * t + g + 1)
                    if g < G1:
                        dve.tensor_reduce(mx[:, t, 4 * g:4 * g + 4], ps[:, g, :].rearrange("p (j k) -> p j k", j=4),
                                          AX.X, ALU.max).then_inc(mx1_used, 1)
                    else:
                        dve.tensor_reduce(mx[:, t, H1:2 * H1], ps[:, 4 + t % 2, :].rearrange("p (h k) -> p h k", h=H1)
                                          [:, :, 0:KR], AX.X, ALU.max).then_inc(mx1_used, 1)
                dve.wait_ge(mx1_used, 5 * t + 5)
                do(dve.tensor_tensor(small[:, t % 2, 0:H1], mx[:, t, 0:H1], mx[:, t, H1:2 * H1], ALU.max))
                dve.tensor_scalar(st_q1[:, t, :, 24:25].rearrange("p h o -> p (h o)").bitcast(F32R),
                                  small[:, t % 2, 0:H1], -1.0, None, ALU.mult).then_inc(shift1_staged, 1)
            add_bias(2, b1[:, 3, :])
            attended(1, E1, 10)

            choose(1, E1)
            ffn(1)
            add_result(1, 1)


_INS = ["x", "ctx_768", "mask_BxS2_bk0", "g_xattn", "g_ffn", "L0_xattn_ln_x_g", "L0_xattn_ln_x_b",
        "L0_xattn_ln_l_g", "L0_xattn_ln_l_b", "L0_xattn_qn_g", "L0_xattn_kn_g", "L0_xattn_Wq", "L0_xattn_Wkv",
        "L0_xattn_Wlkv", "L0_xattn_Wo", "L0_xattn_bo", "L0_ffn_Wr", "L0_ffn_Wg", "L0_ffn_Wu", "L0_ffn_Wd",
        "L1_xattn_wq", "L1_xattn_bq", "L1_xattn_wk", "L1_xattn_bk", "L1_xattn_wv", "L1_xattn_bv", "L1_xattn_wo",
        "L1_xattn_bo", "L1_ffn_Ws1", "L1_ffn_bs1", "L1_ffn_Ws2", "L1_ffn_bs2", "L1_ffn_We1", "L1_ffn_be1",
        "L1_ffn_We2", "L1_ffn_be2", "L1_ffn_Wr", "L1_ffn_br"]


def kernel(**inputs):
    import numpy as np
    import concourse.bacc as bacc
    from concourse.bass_utils import run_bass_kernel_spmd

    nc = bacc.Bacc("TRN2", target_bir_lowering=False, num_devices=1)
    arrays, aps = {}, {}
    for name in _INS:
        a = np.ascontiguousarray(inputs[name])
        arrays[f"in_{name}"] = a
        aps[name] = nc.dram_tensor(f"in_{name}", a.shape, mybir.dt.from_np(a.dtype), kind="ExternalInput").ap()
    out = nc.dram_tensor("out_x", (B, S, D), F32, kind="ExternalOutput").ap()
    flamingo(nc, aps, out)
    r = run_bass_kernel_spmd(nc, [arrays], core_ids=[0])
    return r.results[0]["out_x"]
```

```python
import math
from contextlib import ExitStack

import concourse.bass as bass
from concourse import mybir
from concourse.alu_op_type import AluOpType as ALU

ACT = mybir.ActivationFunctionType
AX = mybir.AxisListType
F32 = mybir.dt.float32
F32R = mybir.dt.float32r
U8 = mybir.dt.uint8
I32 = mybir.dt.int32

P = 128
B, S, D = 2, 512, 128
T = B * S // P
TB = S // P
N = B * S
CK, DC = 154, 96
KR = CK - P
H0, HD0 = 2, 64
H1, HD1 = 16, 8
G1 = 4
E0, E1 = 8, 12
LN_EPS = 1e-5
RMS_EPS2 = 1e-16
TAU = 1.5
DEPTH_SCALE = 1.0 / 12 ** 0.5
BIG = 1e30
LO = 16

BANKS = 8
COLS = 512


class Layer:

    def __init__(self, experts, blocks, function, shared_blocks):
        self.experts, self.blocks, self.function = experts, blocks, function
        self.shared_blocks = shared_blocks
        self.pairs = experts // 2
        self.steps = 4 * blocks
        self.all_experts = experts + (1 if shared_blocks else 0)
        self.first = blocks - 1

    def place(self, s, last):
        if last and s >= self.steps and self.shared_blocks:
            r = s - self.steps
            return 4 + r // self.shared_blocks, r % self.shared_blocks, self.shared_blocks
        return s // self.blocks, s % self.blocks, self.blocks

    def last_steps(self):
        return self.steps + 2 * self.shared_blocks


def flamingo(nc, A, out):
    with ExitStack() as ctx:
        def sb(name, shape, dt=F32):
            return ctx.enter_context(nc.sbuf_tensor(name, shape, dt))

        def sem(name):
            return ctx.enter_context(nc.semaphore(name))

        xres = sb("xres", [P, T, D])
        z = sb("z", [P, T, D])
        zT = sb("zT", [P, N])
        ident = sb("ident", [P, P])
        sel = sb("sel", [P, 13, P], F32R)
        rev = sb("rev", [P, 16])
        revi = sb("revi", [P, 16], I32)
        zero = sb("zero", [P, 1])
        half = sb("half", [P, 16])
        euler = sb("euler", [P, T])
        stats = sb("stats", [P, T, 6])
        mv = sb("mv", [P, T, 2])
        rstd = sb("rstd", [P, T])
        cstats = sb("cstats", [P, 4, 6])
        cmv = sb("cmv", [P, 4, 2])
        crstd = sb("crstd", [P, 4])
        ctx_rows = sb("ctx_rows", [P, 4, DC])
        ctx_z = sb("ctx_z", [P, 4, DC])
        cT = sb("cT", [DC, 4, P])
        rT = sb("rT", [DC, 4, P])
        gates = sb("gates", [P, 4])
        tg = sb("tg", [P, 4])
        colv = sb("colv", [P, 4])
        gq = sb("gq", [P, HD0])
        gk = sb("gk", [P, HD0])
        gqk = sb("gqk", [P, HD0])
        bo0 = sb("bo0", [P, D])
        b1 = sb("b1", [P, 4, D])
        br = sb("br", [P, E1])
        wr0 = sb("wr0", [P, E0])
        wr1 = sb("wr1", [P, E1])
        wq0 = sb("wq0", [P, P])
        wlkv = sb("wlkv", [P, 2, P])
        wkv = sb("wkv", [P, 2, DC])
        wo0 = sb("wo0", [P, P])
        wcat = sb("wcat", [P, 3 * P])
        wkvT = sb("wkvT", [DC, 2 * P])
        woT = sb("woT", [P, P])
        w1 = sb("w1", [P, 2, P])
        w1c = sb("w1c", [DC, 2, P])
        beR = sb("beR", [P, P])
        beT = sb("beT", [P, 76])
        be2 = sb("be2", [P, P])
        mask8 = sb("mask8", [1, B * CK], U8)
        ones_row = sb("ones_row", [1, P], F32R)
        mask_row = sb("mask_row", [1, B, CK], F32R)
        mcol8 = sb("mcol8", [P, 4], U8)
        mcol = sb("mcol", [P, 4])
        pad1 = sb("pad1", [P, 1])
        qkv = sb("qkv", [P, T, 3 * P])
        ckv = sb("ckv", [P, 4, 2 * P])
        ss = sb("ss", [P, T, 4])
        rn = sb("rn", [P, T, 4])
        css = sb("css", [P, 4, 2])
        crn = sb("crn", [P, 4, 2])
        stage = sb("stage", [P, 6144])
        q_s = sb("q_s", [P, 4096], F32R)
        k_a = sb("k_a", [P, 5120], F32R)
        k_b = sb("k_b", [P, 1024], F32R)
        v_a = sb("v_a", [P, 4352])
        v_b = sb("v_b", [P, 1280])
        probs = sb("probs", [P, 4, COLS])
        mx = sb("mx", [P, T, 32])
        top = sb("top", [P, T, 8])
        small = sb("small", [P, 16, T * 12])
        comb_st = sb("comb_st", [P, T, P])
        combT = sb("combT", [P, N], F32R)
        comb_w = sb("comb_w", [P, T, 13])
        biases = sb("biases", [P, 2, 6])
        selp = sb("selp", [P, 2, P], F32R)
        selpk = sb("selpk", [P, P], F32R)
        raw = sb("raw", [P, 2, 1536])
        wh = sb("wh", [P, 2, 1536], F32R)
        wl = sb("wl", [P, 2, 1536], F32R)
        zh, zl = q_s[:, 0:N], q_s[:, N:2 * N]
        spare = qkv[:, :, :].rearrange("p t c -> p (t c)")
        hh = q_s[:, 2 * N:3 * N].rearrange("p (a n) -> p a n", a=2)
        hl = q_s[:, 3 * N:4 * N].rearrange("p (a n) -> p a n", a=2)
        act_out = spare[:, 0:N].rearrange("p (a n) -> p a n", a=2)
        yT = spare[:, 2 * N:3 * N]
        oT = zT
        cbs = probs[:, 0:2, :]
        ytmp = probs[:, 2:4, :]
        rcp = z[0:64, TB:T, :].rearrange("p t d -> p (t d)")
        ps = ctx.enter_context(nc.psum_tensor("ps", [P, BANKS, COLS], F32))

        dve_link, pool_link = sem("dve_link"), sem("pool_link")
        x_in, ctx_in, w0_in, vec_in, w1_in = (sem(n) for n in ("x_in", "ctx_in", "w0_in", "vec_in", "w1_in"))
        const_ready, zeroed = sem("const_ready"), sem("zeroed")
        var_ready, rstd_ready, z_ready, zT_psum, zT_ready = (
            sem(n) for n in ("var_ready", "rstd_ready", "z_ready", "zT_psum", "zT_ready"))
        gate_ready = sem("gate_ready")
        wT_psum, wT_ready, cT_psum, cT_ready, cz_ready = (
            sem(n) for n in ("wT_psum", "wT_ready", "cT_psum", "cT_ready", "cz_ready"))
        proj_psum, proj_used, cproj_psum, cproj_used = (
            sem(n) for n in ("proj_psum", "proj_used", "cproj_psum", "cproj_used"))
        staged, turn_psum, turned_a, turned_v = (sem(n) for n in ("staged", "turn_psum", "turned_a", "turned_v"))
        kv_ready = sem("kv_ready")
        rT_ready, qk_ready, high_ready = (sem(n) for n in ("rT_ready", "qk_ready", "high_ready"))
        mx_psum, mx_used, zh_ready, zl_ready = (sem(n) for n in ("mx_psum", "mx_used", "zh_ready", "zl_ready"))
        q1_psum, kv1_psum, k1_staged, k1_psum, k1_ready, v1_ready, q1_staged, q1_turned = (
            sem(n) for n in (
                "q1_psum", "kv1_psum", "k1_staged", "k1_psum", "k1_ready", "v1_ready", "q1_staged", "q1_turned"))
        q1_turn_psum, q1_full_psum, q1_full, mx1_psum, mx1_used, shift1_staged = (
            sem(n) for n in ("q1_turn_psum", "q1_full_psum", "q1_full", "mx1_psum", "mx1_used", "shift1_staged"))
        beT_psum, beT_ready, bias_psum, bias_added, logits_ready = (
            sem(n) for n in ("beT_psum", "beT_ready", "bias_psum", "bias_added", "logits_ready"))
        shift_staged, shift_psum, shift_ready = sem("shift_staged"), sem("shift_psum"), sem("shift_ready")
        scores_ready, probs_ready, pv_done = sem("scores_ready"), sem("probs_ready"), sem("pv_done")
        oT_ready, o_psum, res_ready = sem("oT_ready"), sem("o_psum"), sem("res_ready")
        route_psum, gap_ready, e_ready, comb_staged, comb_psum, comb_ready = (
            sem(n) for n in ("route_psum", "gap_ready", "e_ready", "comb_staged", "comb_psum", "comb_ready"))
        y_turned, y_added, out_done = sem("y_turned"), sem("y_added"), sem("out_done")
        ffn_sem = [{n: sem(f"{n}_{i}") for n in (
            "w_in_a", "w_in_b", "w_high", "up_split", "w_split", "g_ready", "u_ready", "act_ready", "hid_ready",
            "hh_ready", "hl_ready", "down_done", "y_used", "y_summed", "c_ready", "c_copied")} for i in range(2)]
        HEAD_START = {"hid_ready": 1, "hl_ready": 2, "down_done": 2, "y_used": 2, "c_copied": 2}

        LAYERS = [Layer(E0, 4, ACT.Silu, 0), Layer(E1, 3, ACT.Gelu, 2)]

        def linked(eng, link):
            count = [0]

            def do(ins, wait=True):
                count[0] += 1
                ins.then_inc(link, 1)
                if wait:
                    eng.wait_ge(link, count[0])
            return do

        st_q0 = stage[:, 0:2048].rearrange("p (t h c) -> p t h c", t=T, h=H0)
        st_k0 = stage[:, 2048:6144].rearrange("p (s t h c) -> p s t h c", s=2, t=T, h=H0)
        st_c0 = [x[:, :, :].rearrange("p a (m h c) -> p (a m) h c", m=2, h=H0) for x in (hh, hl)]
        q_s0 = q_s[:, 0:2048].rearrange("p (h n) -> p h n", h=H0)
        k_a0 = k_a[:, :].rearrange("p (s b h k) -> p s b h k", s=2, b=B, h=H0)
        k_b0 = k_b[:, :].rearrange("p (s b h k) -> p s b h k", s=2, b=B, h=H0)
        v_a0 = v_a[:, 0:2560].rearrange("p (t h c) -> p t h c", h=H0, c=P)
        v_b0 = v_b[:, 0:512].rearrange("p (b h c) -> p b h c", b=B, h=H0)
        st_q1 = stage[:, 0:4096].rearrange("p (t h c) -> p t h c", t=T, h=H1)
        st_k1 = stage[:, 4096:6144].rearrange("p (m h c) -> p m h c", m=4, h=H1)
        q_s1 = q_s[:, :].rearrange("p (g n) -> p g n", g=G1)
        k_a1 = k_a[:, 0:4096].rearrange("p (b g j k) -> p b g j k", b=B, g=G1, j=4)
        k_b1 = k_b[:, :].rearrange("p (b g k) -> p b g k", b=B, g=G1)
        v_a1 = v_a[:, :].rearrange("p (b a c) -> p b a c", b=B, a=2)
        v_b1 = v_b[:, :].rearrange("p (b a c) -> p b a c", b=B, a=2)

        OWN = (5, 7)
        KEYS1, PROJECT0, TURN0, ROUTE0 = 3, 14, 18, 20
        PROJECT1, TURN1, ROUTE1 = 26, 33, 37
        LEAD = 3

        block = ctx.enter_context(nc.Block())

        @block.sync
        def _(sp):
            x_rows = A["x"].rearrange("b (t p) d -> p (b t) d", p=P)
            sp.dma_start(xres[:, :, :], x_rows).then_inc(x_in, 16)
            sp.dma_start(ctx_rows[:, 0:2, :], A["ctx_768"][:, 0:P, :].rearrange("b p c -> p b c")).then_inc(ctx_in, 16)
            sp.dma_start(ctx_rows[0:KR, 2:4, :],
                         A["ctx_768"][:, P:CK, :].rearrange("b p c -> p b c")).then_inc(ctx_in, 16)
            for dst, src in (
                    (wq0[:, :], A["L0_xattn_Wq"]),
                    (wlkv[:, :, :], A["L0_xattn_Wlkv"].rearrange("(a p) c -> p a c", p=P)),
                    (wkv[:, :, :], A["L0_xattn_Wkv"].rearrange("(a p) c -> p a c", p=P)),
                    (wo0[:, :], A["L0_xattn_Wo"])):
                sp.dma_start(dst, src).then_inc(w0_in, 16)
            for dst, src in (
                    (colv[:, 0:1], A["L0_xattn_ln_l_g"].unsqueeze(1)), (colv[:, 1:2], A["L0_xattn_ln_l_b"].unsqueeze(1)),
                    (colv[0:DC, 2:3], A["L0_xattn_ln_x_g"].unsqueeze(1)),
                    (colv[0:DC, 3:4], A["L0_xattn_ln_x_b"].unsqueeze(1)),
                    (gates[:, 0:2], A["g_xattn"].partition_broadcast(P)),
                    (gates[:, 2:4], A["g_ffn"].partition_broadcast(P)),
                    (gq[:, :], A["L0_xattn_qn_g"].partition_broadcast(P)),
                    (gk[:, :], A["L0_xattn_kn_g"].partition_broadcast(P)),
                    (mask8[:, :], A["mask_BxS2_bk0"].rearrange("b k -> (b k)").unsqueeze(0)),
                    (bo0[:, :], A["L0_xattn_bo"].partition_broadcast(P)),
                    (wr0[:, :], A["L0_ffn_Wr"])):
                sp.dma_start(dst, src).then_inc(vec_in, 16)
            sp.wait_ge(const_ready, 1)
            for b in range(B):
                sp.dma_start(mcol8[:, b:b + 1], A["mask_BxS2_bk0"][b, 0:P].unsqueeze(1)).then_inc(vec_in, 16)
                for j in range(H0):
                    sp.dma_start(mcol8[64 * j:64 * j + KR, 2 + b:3 + b],
                                 A["mask_BxS2_bk0"][b, P:CK].unsqueeze(1)).then_inc(vec_in, 16)

            def expert_loads(layer, e, b):
                into = ffn_sem[layer][("w_in_a", "w_in_b")[b]]
                w = LAYERS[layer].blocks * P
                if layer == 0:
                    srcs = [A["L0_ffn_Wg"][e, :, :].rearrange("a p n -> p (a n)"),
                            A["L0_ffn_Wu"][e, :, :].rearrange("a p n -> p (a n)")]
                    sp.dma_start(raw[:, b, 0:w], srcs[0]).then_inc(into, 16)
                    sp.dma_start(raw[:, b, w:2 * w], srcs[1]).then_inc(into, 16)
                    down = A["L0_ffn_Wd"][e, :, :]
                else:
                    sp.dma_start(raw[:, b, 0:2 * w], A["L1_ffn_We1"][e, :, :].rearrange("a p n -> p (a n)")).then_inc(into, 32)
                    down = A["L1_ffn_We2"][e, :, :]
                sp.dma_start(raw[:, b, 2 * w:3 * w].rearrange("p (c n) -> p c n", n=P),
                             down.rearrange("a (c p) n -> p (a c) n", p=P)).then_inc(into, 16)

            def first_loads(layer):
                for b in range(2):
                    expert_loads(layer, slice(b, b + 1), b)

            def later_loads(layer):
                L, q = LAYERS[layer], ffn_sem[layer]
                with sp.Fori(1, L.pairs) as k:
                    for b in range(2):
                        sp.wait_ge(q["w_split"], 2 * k + b - 1)
                        expert_loads(layer, bass.ds(2 * k + b, 1), b)

            first_loads(0)
            sp.wait_ge(const_ready, 7)
            for dst, src in (
                    (w1[:, 0, :], A["L1_xattn_wq"]), (w1[:, 1, :], A["L1_xattn_wo"]),
                    (w1c[:, 0, :], A["L1_xattn_wk"]), (w1c[:, 1, :], A["L1_xattn_wv"]),
                    (b1[:, 0, :], A["L1_xattn_bq"].partition_broadcast(P)),
                    (b1[:, 1, :], A["L1_xattn_bk"].partition_broadcast(P)),
                    (b1[:, 2, :], A["L1_xattn_bv"].partition_broadcast(P)),
                    (b1[:, 3, :], A["L1_xattn_bo"].partition_broadcast(P)),
                    (br[:, :], A["L1_ffn_br"].partition_broadcast(P)),
                    (wr1[:, :], A["L1_ffn_Wr"]),
                    (beR[0:72, :], A["L1_ffn_be1"].rearrange("e (c n) -> (e c) n", n=P)),
                    (beR[72:76, :], A["L1_ffn_bs1"].rearrange("(c n) -> c n", n=P)),
                    (be2[0:E1, :], A["L1_ffn_be2"]), (be2[LO:LO + E1, :], A["L1_ffn_be2"]),
                    (be2[E1:E1 + 1, :], A["L1_ffn_bs2"].unsqueeze(0)),
                    (be2[LO + E1:LO + E1 + 1, :], A["L1_ffn_bs2"].unsqueeze(0))):
                sp.dma_start(dst, src).then_inc(w1_in, 16)
            later_loads(0)
            sp.wait_ge(ffn_sem[0]["w_split"], E0)
            first_loads(1)
            later_loads(1)
            sp.wait_ge(ffn_sem[1]["w_split"], E1 - 1)
            sp.dma_start(raw[:, 0, 0:4 * P], A["L1_ffn_Ws1"]).then_inc(ffn_sem[1]["w_in_a"], 32)
            sp.dma_start(raw[:, 0, 4 * P:6 * P].rearrange("p (c n) -> p c n", n=P),
                         A["L1_ffn_Ws2"].rearrange("(c p) n -> p c n", p=P)).then_inc(ffn_sem[1]["w_in_a"], 16)
            for m in range(2):
                sp.wait_ge(y_added, 2 + m + 1)
                sp.dma_start(out.rearrange("b (t p) d -> p (b t) d", p=P)[:, 4 * m:4 * m + 4, :],
                             xres[:, 4 * m:4 * m + 4, :]).then_inc(out_done, 16)
            sp.wait_ge(out_done, 32)

        N_W0, N_VEC, N_W1 = 4 * 16, (11 + 6) * 16, 16 * 16

        def turned_to0(i):
            if i < 4:
                part, packed = divmod(i, 2)
                return k_b0[:, part, :, :, :] if packed else k_a0[:, part, :, :, 0:P]
            b, r = divmod(i - 4, 6)
            if r < 2:
                return q_s0[:, r, b * COLS:(b + 1) * COLS].rearrange("p (a k) -> p a k", a=4)
            part, h = divmod(r - 2, 2)
            return k_a0[:, part, b, h, P:5 * P].rearrange("p (a k) -> p a k", a=4)

        def turned_from0(i, a):
            if i < 4:
                part, packed = divmod(i, 2)
                b, h = divmod(a, 2)
                return st_c0[part][:, 2 * packed + b, h, :].bitcast(F32)
            b, r = divmod(i - 4, 6)
            if r < 2:
                return st_q0[:, 4 * b + a, r, :]
            part, h = divmod(r - 2, 2)
            return st_k0[:, part, 4 * b + a, h, :]

        def turned_bank0(i):
            shape = "p (a k) -> p a k" if i >= 4 else "p (b h k) -> p b h k"
            return ps[:, i % 8, :].rearrange(shape, k=P, **({} if i >= 4 else {"b": B}))

        def parts0(tiles):
            qk = qkv[:, :, 0:2 * P].rearrange("p t (h c) -> p t h c", h=4)
            return (st_q0[:, tiles, :, 0:64], st_q0[:, tiles, :, 64:P],
                    [st_k0[:, 0, tiles, :, 64 * dup:64 * dup + 64] for dup in range(2)],
                    [st_k0[:, 1, tiles, :, 64 * dup:64 * dup + 64] for dup in range(2)],
                    qk[:, tiles, 0:2, :], qk[:, tiles, 2:4, :])

        BY_DVE = (11, 13, 15)

        def row_scores1(pe, t, between):
            b = t // TB
            pe.wait_ge(q1_turned, t + 1)
            for g in range(G1 + 1):
                if g == 2:
                    between()
                if t >= 1 and g < G1:
                    pe.wait_ge(mx1_used, 3 * (t - 1) + g // 2 + 1)
                if t >= 2 and g == G1:
                    pe.wait_ge(mx1_used, 3 * (t - 1))
                if g < G1:
                    pe.matmul(ps[:, g, :], q_s1[:, g, t * P:(t + 1) * P],
                              k_a1[:, b, g, :, :].rearrange("p j k -> p (j k)"), start=True, stop=True)\
                        .then_inc(mx1_psum, 1)
                    continue
                for gg in range(G1):
                    last = pe.matmul(ps[:, 4 + t % 2, gg * P:(gg + 1) * P], q_s1[:, gg, t * P:(t + 1) * P],
                                     k_b1[:, b, gg, :], start=True, stop=True)
                last.then_inc(mx1_psum, 1)

        @block.gpsimd
        def _(pool):
            do = linked(pool, pool_link)
            pool.memset(mcol8[:, :], 0).then_inc(const_ready, 1)
            pool.memset(zero[:, :], 0.0)
            pool.memset(euler[:, :], math.e)
            pool.memset(half[:, :], -0.5).then_inc(const_ready, 1)
            do(pool.memset(ident[:, :], 0.0))
            pool.affine_select(out=ident[:, :], in_=ident[:, :], compare_op=ALU.not_equal, fill=1.0, base=0,
                               pattern=[[-1, P]], channel_multiplier=1).then_inc(const_ready, 1)
            pool.memset(comb_st[:, :, :], 0.0).then_inc(zeroed, 1)
            pool.memset(cT[:, 2:4, :], 0.0).then_inc(zeroed, 1)
            pool.memset(rT[:, 2:4, :], 0.0).then_inc(zeroed, 1)
            for q in ffn_sem:
                for name, count in HEAD_START.items():
                    pool.sem_inc(q[name], count)

            def power(count, dst, exponents, x=None):
                pool.wait_ge(var_ready, count)
                pool.tensor_tensor(dst, dst if x is None else x, exponents, ALU.pow).then_inc(rstd_ready, 1)

            pool.wait_ge(const_ready, 3)
            power(1, crstd[:, :], half[:, 0:4])
            power(2, rstd[:, :], half[:, 0:T])
            for x in (hh, hl):
                pool.memset(x[:, :, :].bitcast(F32), 0.0).then_inc(zeroed, 1)
            pool.memset(v_a[:, 0:2560], 1.0).then_inc(zeroed, 1)
            pool.memset(v_b[:, :], 0.0).then_inc(zeroed, 1)
            power(3, crn[:, :, :], half[:, 0:8].rearrange("p (a b) -> p a b", a=4), css[:, :, :])
            for m in range(2):
                tiles = slice(TB * m, TB * m + TB)
                power(4 + m, rn[:, tiles, :], half[:, 0:16].rearrange("p (a b) -> p a b", a=TB), ss[:, tiles, :])
            selF = probs[:, :, :].rearrange("p a n -> p (a n)")[:, 0:13 * P].rearrange("p (e m) -> p e m", e=13)
            do(pool.memset(selF, 0.0))
            for base in (0, -LO):
                do(pool.affine_select(out=selF, in_=selF, compare_op=ALU.not_equal, fill=1.0, base=base,
                                      pattern=[[-1, 13], [0, P]], channel_multiplier=1))
            do(pool.tensor_copy(sel[:, :, :], selF))
            for h in range(H0):
                last = pool.tensor_copy(selpk[:, 64 * h:64 * h + 64], sel[:, h, 0:64].bitcast(F32))
            last.then_inc(const_ready, 1)
            do(pool.iota(revi[:, :], pattern=[[-1, 16]], base=12, channel_multiplier=0))
            pool.tensor_copy(rev[:, :], revi[:, :]).then_inc(const_ready, 1)
            do(pool.memset(pad1[:, :], 0.0))
            for j in range(4):
                rows = pad1[32 * j:32 * j + 32, :]
                do(pool.affine_select(out=rows, in_=rows, compare_op=ALU.is_ge, fill=-BIG, base=KR - 1,
                                      pattern=[[0, 1]], channel_multiplier=-1))
            pool.memset(beR[:, :], 0.0).then_inc(const_ready, 1)
            pool.memset(be2[:, :], 0.0).then_inc(const_ready, 1)
            pool.wait_ge(turn_psum, 16)
            pool.memset(stage[:, 4096:6144], 0.0).then_inc(zeroed, 1)
            pool.memset(stage[:, 0:4096], 0.0).then_inc(zeroed, 1)

            def ffn(layer, between):
                L, q = LAYERS[layer], ffn_sem[layer]

                def split_up(e, k, b, blocks):
                    w = 2 * blocks * P
                    pool.wait_ge(q[("w_in_a", "w_in_b")[b]], 48 * (k + 1))
                    pool.tensor_tensor(wh[:, b, 0:w], raw[:, b, 0:w], zero[:, 0:1].broadcast_to([P, w]), ALU.add)\
                        .then_inc(q["w_high"], 1)
                    if layer == 1:
                        cols = slice(6 * e, 6 * e + 2 * blocks) if isinstance(e, int) else bass.ds(6 * e, 6)
                        pool.tensor_copy(biases[:, b, 0:2 * blocks], beT[:, cols])
                    pool.wait_ge(q["w_high"], 2 * e + 1)
                    pool.tensor_tensor(wl[:, b, 0:w], raw[:, b, 0:w], wh[:, b, 0:w].bitcast(F32),
                                       ALU.subtract).then_inc(q["up_split"], 1)

                def split_down(e, b, blocks):
                    cols = slice(2 * blocks * P, 3 * blocks * P)
                    pool.tensor_tensor(wh[:, b, cols], raw[:, b, cols], zero[:, 0:1].broadcast_to([P, blocks * P]),
                                       ALU.add).then_inc(q["w_high"], 1)
                    expert = slice(e, e + 1) if isinstance(e, int) else bass.ds(e, 1)
                    pool.tensor_copy(selp[:, b:b + 1, :], sel[:, expert, :])
                    pool.wait_ge(q["w_high"], 2 * e + 2)
                    pool.tensor_tensor(wl[:, b, cols], raw[:, b, cols], wh[:, b, cols].bitcast(F32),
                                       ALU.subtract).then_inc(q["w_split"], 1)

                def add_y(m, n):
                    pool.wait_ge(q["y_used"], m + 3)
                    pool.wait_ge(q["y_summed"], m + 1)
                    part = yT[:, n * COLS:(n + 1) * COLS]
                    pool.tensor_tensor(part, part, ytmp[:, n, :], ALU.add).then_inc(q["y_summed"], 1)

                if layer == 1:
                    pool.wait_ge(beT_ready, 1)
                    pool.wait_ge(ffn_sem[0]["down_done"], LAYERS[0].pairs * LAYERS[0].steps + 2)
                for e in range(2):
                    split_up(e, 0, e, L.blocks)
                    split_down(e, e, L.blocks)
                between()
                with pool.Fori(0, L.pairs - 1) as k:
                    for b in range(2):
                        used = L.steps * k + (b + 1) * 2 * L.blocks
                        pool.wait_ge(q["hid_ready"], used + 1)
                        split_up(2 * k + 2 + b, k + 1, b, L.blocks)
                        for n in range(2):
                            add_y(4 * k + 2 * b + n, n)
                        pool.wait_ge(q["down_done"], used + 2)
                        split_down(2 * k + 2 + b, b, L.blocks)
                k = L.pairs - 1
                for b in range(2):
                    used = L.steps * k + (b + 1) * 2 * L.blocks
                    if b == 0 and L.shared_blocks:
                        pool.wait_ge(q["hid_ready"], used + 1)
                        split_up(2 * k + 2, k + 1, 0, L.shared_blocks)
                    for n in range(2):
                        add_y(4 * k + 2 * b + n, n)
                    if b == 0 and L.shared_blocks:
                        pool.wait_ge(q["down_done"], used + 2)
                        split_down(2 * k + 2, 0, L.shared_blocks)
                if L.shared_blocks:
                    for n in range(2):
                        add_y(4 * k + 4 + n, n)

            def gap_exponential(count):
                pool.wait_ge(gap_ready, count)
                pool.tensor_tensor(small[:, 15, 0:T], euler[:, :], small[:, 15, 0:T], ALU.pow).then_inc(e_ready, 1)

            def before_layer0():
                power(6, rstd[:, 0:TB], half[:, 0:TB])
                pool.wait_ge(pv_done, 22)
                pool.memset(k_a[:, 0:4096].bitcast(F32), 0.0).then_inc(zeroed, 1)
                power(7, rstd[:, TB:T], half[:, 0:TB])
                gap_exponential(1)
                do(pool.memset(yT[:, :], 0.0))
                pool.sem_inc(ffn_sem[0]["y_summed"], 2)
                do(pool.memset(v_b[:, :], 0.0))
                do(pool.memset(v_a[:, :], 0.0))
                for j in range(4):
                    do(pool.memset(v_b[32 * j:32 * j + 32, :].rearrange("p (b g s) -> p b g s", b=B, g=G1)
                                   [:, :, :, 64 + 8 * j:72 + 8 * j], 1.0))
                for b in range(B):
                    last = pool.memset(v_a1[:, b, :, :].rearrange("p a (r s) -> p a r s", s=136)[:, :, :, 64:72], 1.0)
                last.then_inc(zeroed, 1)

            def before_layer1():
                power(10, rstd[:, 0:TB], half[:, 0:TB])
                power(11, rstd[:, TB:T], half[:, 0:TB])
                gap_exponential(2)
                do(pool.memset(yT[:, :], 0.0))
                pool.sem_inc(ffn_sem[1]["y_summed"], 2)

            ffn(0, before_layer0)
            power(8, rstd[:, 0:TB], half[:, 0:TB])
            power(9, rstd[:, TB:T], half[:, 0:TB])
            ffn(1, before_layer1)

        @block.scalar
        def _(act):
            def copy(dst, src):
                return act.activation(dst, src, ACT.Copy)

            def gate(layer, k, s, last):
                L, q = LAYERS[layer], ffn_sem[layer]
                u, j, blocks = L.place(s, last)
                g = L.steps * k + s
                act.wait_ge(q["g_ready"], g + 1)
                act.wait_ge(q["hid_ready"], max(g, 1) if isinstance(g, int) else g)
                bias = 0.0
                if layer == 1:
                    act.wait_ge(q["up_split"], 2 * k + u // 2 + 1)
                    bias = biases[:, (u // 2) % 2, blocks + j:blocks + j + 1]
                act.activation(act_out[:, s % 2, :], ps[:, s % 2, :], L.function, bias=bias)\
                    .then_inc(q["act_ready"], 1)

            def first_gates(layer):
                for s in range(2):
                    gate(layer, 0, s, False)

            def high(layer, k, s, last):
                L, q = LAYERS[layer], ffn_sem[layer]
                g = L.steps * k + s
                act.wait_ge(q["hid_ready"], g + 2)
                act.wait_ge(q["down_done"], g + 1)
                copy(hh[:, s % 2, :], ps[:, 2 + s % 4, :]).then_inc(q["hh_ready"], 1)

            def first_steps(layer, steps):
                for s in steps:
                    high(layer, 0, s, False)
                    gate(layer, 0, s + 2, False)

            def ffn(layer):
                L, q = LAYERS[layer], ffn_sem[layer]

                def combine_weights(k, u):
                    m, n = 4 * k + u, u % 2
                    act.wait_ge(q["c_ready"], m + 1)
                    act.wait_ge(q["y_used"], m + 1)
                    copy(cbs[:, n, :], ps[:, 7 - n, :]).then_inc(q["c_copied"], 1)

                with act.Fori(0, L.pairs - 1) as k:
                    for s in range(L.first, L.first + L.steps):
                        high(layer, k, s, False)
                        if s % L.blocks == 0:
                            combine_weights(k, s // L.blocks - 1)
                        gate(layer, k, s + 2, False)
                k = L.pairs - 1
                for s in range(L.first, L.last_steps()):
                    high(layer, k, s, True)
                    u, j, _ = L.place(s, True)
                    if j == 0:
                        combine_weights(k, u - 1)
                    if s + 2 < L.last_steps():
                        gate(layer, k, s + 2, True)
                combine_weights(k, u)

            def exponentials(units, base, bias_of, between):
                for u in range(units):
                    if u in between:
                        between[u]()
                    act.wait_ge(scores_ready, base + u + 1)
                    if u >= 4:
                        act.wait_ge(pv_done, base + u - 3)
                    act.activation(probs[:, u % 4, :], ps[:, u % 4, :], ACT.Exp, bias=bias_of(u))\
                        .then_inc(probs_ready, 1)

            def turned_tokens(index, m, bank, parts):
                act.wait_ge(zT_psum, 2 * index + m + 1)
                cols = slice(m * COLS, (m + 1) * COLS)
                copy(zT[:, cols], ps[:, bank, :]).then_inc(zT_ready, 1)
                if parts:
                    copy(zh[:, cols], ps[:, bank, :]).then_inc(zh_ready, 1)

            def combine_columns(count):
                for m in range(2):
                    act.wait_ge(comb_psum, count + m + 1)
                    copy(combT[:, m * COLS:(m + 1) * COLS], ps[:, OWN[1], :]).then_inc(comb_ready, 1)

            act.wait_ge(vec_in, N_VEC)
            act.activation(tg[:, :], gates[:, :], ACT.Tanh).then_inc(gate_ready, 1)
            act.wait_ge(wT_psum, 1)
            copy(wcat[:, :], ps[:, 2, 0:3 * P])
            copy(wkvT[:, :], ps[0:DC, 3, 0:2 * P])
            copy(woT[:, :], ps[:, 3, 2 * P:3 * P]).then_inc(wT_ready, 1)
            act.wait_ge(cT_psum, 1)
            act.wait_ge(zeroed, 3)
            gain, shift = colv[0:DC, 2:3], colv[0:DC, 3:4]
            act.activation(cT[:, 0:2, :], ps[0:DC, 4, 0:2 * P].rearrange("p (b k) -> p b k", b=B), ACT.Identity,
                           scale=gain, bias=shift)
            for b in range(B):
                left = slice(2 * P + 32 * b, 2 * P + 32 * b + KR)
                for j in range(H0):
                    last = act.activation(cT[:, 2 + b, 64 * j:64 * j + KR], ps[0:DC, 4, left], ACT.Identity,
                                          scale=gain, bias=shift)
            last.then_inc(cT_ready, 1)
            for m in range(2):
                act.wait_ge(zT_psum, m + 1)
                act.activation(zT[:, m * COLS:(m + 1) * COLS], ps[:, m, :], ACT.Identity,
                               scale=colv[:, 0:1], bias=colv[:, 1:2]).then_inc(zT_ready, 1)
            copy(rT[:, 0:2, :], ps[0:DC, 5, 0:2 * P].rearrange("p (b k) -> p b k", b=B))
            for b in range(B):
                left = slice(2 * P + 32 * b, 2 * P + 32 * b + KR)
                for j in range(4):
                    last = copy(rT[:, 2 + b, 32 * j:32 * j + KR], ps[0:DC, 5, left])
            last.then_inc(rT_ready, 1)
            act.wait_ge(cproj_psum, 1)
            for m in range(2):
                copy(ckv[:, 2 * m:2 * m + 2, :], ps[:, 6 + m, :].rearrange("p (b c) -> p b c", b=B))\
                    .then_inc(cproj_used, 1)
            for t in range(T):
                act.wait_ge(proj_psum, t + 1)
                copy(qkv[:, t, :], ps[:, t % 4, 0:3 * P]).then_inc(proj_used, 1)
            act.wait_ge(zeroed, 7)
            act.wait_ge(proj_used, T)
            for b in range(B):
                for h in range(H0):
                    vals = slice(2 * P + HD0 * h, 2 * P + HD0 * h + HD0)
                    copy(v_a0[:, 5 * b + 1:5 * b + 5, h, 0:HD0], qkv[:, TB * b:TB * b + TB, vals])
            act.wait_ge(cproj_used, 2)
            for b in range(B):
                copy(v_a0[:, 5 * b, :, 0:HD0], ckv[:, b, P:2 * P].rearrange("p (h c) -> p h c", h=H0))
                for h in range(H0):
                    rows = slice(64 * h, 64 * h + 64)
                    last = copy(v_b0[rows, b, h, 0:HD0], ckv[rows, 2 + b, P + HD0 * h:P + HD0 * h + HD0])
            last.then_inc(kv_ready, 1)
            for i in range(16):
                if i in (0, 10):
                    m = int(i > 0)
                    tiles = slice(TB * m, TB * m + TB)
                    q_hi, _, k_hi, k_lo, qq, kk = parts0(tiles)
                    act.wait_ge(qk_ready, m + 1)
                    copy(q_hi.bitcast(F32R), qq)
                    copy(k_hi[0].bitcast(F32R), kk).then_inc(high_ready, 1)
                if i in BY_DVE:
                    continue
                act.wait_ge(turn_psum, i + 1)
                copy(turned_to0(i), turned_bank0(i)).then_inc(turned_a, 1)
            for m in range(2):
                act.wait_ge(shift_psum, m + 1)
                copy(combT[:, m * COLS:(m + 1) * COLS], ps[:, m, :]).then_inc(shift_ready, 1)

            def bias0(u):
                b, r = divmod(u, 11)
                if r == 0:
                    return mcol[:, 2 + b:3 + b]
                return mcol[:, b:b + 1] if r % 5 == 1 else 0.0

            exponentials(22, 0, bias0, {TURN0 + 2: lambda: turned_tokens(1, 0, OWN[0], True)})

            first_gates(0)
            first_steps(0, (0, 1))
            turned_tokens(1, 1, OWN[1], True)
            first_steps(0, (2,))
            combine_columns(0)
            ffn(0)

            act.wait_ge(zeroed, 10)
            for i in range(4):
                act.wait_ge(k1_psum, i + 1)
                bank = ps[:, 2 + i, :].rearrange("p (g k) -> p g k", g=G1)
                if i >= 2:
                    copy(k_b1[:, i - 2, :, :], bank).then_inc(k1_ready, 1)
                    continue
                for j in range(4):
                    rows = slice(32 * j, 32 * j + 32)
                    last = copy(k_a1[rows, i, :, j, :], bank[rows, :, :])
                last.then_inc(k1_ready, 1)
            act.wait_ge(beT_psum, 1)
            copy(beT[:, :], ps[:, 7, 0:76]).then_inc(beT_ready, 1)
            for m in range(2):
                turned_tokens(2, m, m, False)
            act.wait_ge(zeroed, 11)
            for b in range(B):
                copy(v_a1[:, b, :, :].rearrange("p a (r s) -> p a r s", s=136)[:, :, :, 0:8],
                     ckv[:, b, P:2 * P].rearrange("p (a r d) -> p a r d", a=2, r=8))
            vb = v_b[:, :].rearrange("p (b g s) -> p b g s", b=B, g=G1)
            for j in range(4):
                rows = slice(32 * j, 32 * j + 32)
                last = copy(vb[rows, :, :, 8 * j:8 * j + 8],
                            ckv[rows, 2:4, P:2 * P].rearrange("p b (g j d) -> p b g j d", g=G1, j=4)[:, :, :, j, :])
            last.then_inc(v1_ready, 1)

            def queries(done, t):
                copy(q_s1[:, :, t * P:(t + 1) * P], ps[:, 6 if done is q1_turned else 7, :]
                     .rearrange("p (g k) -> p g k", g=G1)).then_inc(done, 1)

            for t in range(T + 3):
                if t < T:
                    act.wait_ge(q1_turn_psum, t + 1)
                    queries(q1_turned, t)
                if t >= 3:
                    act.wait_ge(q1_full_psum, t - 2)
                    queries(q1_full, t - 3)
            exponentials(40, 22, lambda u: pad1[:, :] if u % 5 == 4 else 0.0,
                         {TURN1 + 2: lambda: turned_tokens(3, 0, OWN[0], True)})

            first_gates(1)
            first_steps(1, (0,))
            high(1, 0, 1, False)
            turned_tokens(3, 1, OWN[1], True)
            gate(1, 0, 3, False)
            combine_columns(2)
            ffn(1)

        @block.tensor
        def _(pe):
            def turn(dst, src, rows=P):
                return pe.transpose(dst, src, ident[0:rows, 0:rows])

            def up(layer, k, s, last):
                L, q = LAYERS[layer], ffn_sem[layer]
                u, j, blocks = L.place(s, last)
                g = L.steps * k + s
                e, b, n = 2 * k + u // 2, (u // 2) % 2, u % 2
                if j == 0 and n == 0:
                    pe.wait_ge(q["up_split"], e + 1)
                if not isinstance(g, int) or g >= 2:
                    pe.wait_ge(q["act_ready"], g - 1)
                    pe.wait_ge(q["hl_ready"], g - 1)
                cols = slice(n * COLS, (n + 1) * COLS)
                if isinstance(g, int) and g == 3:
                    pe.wait_ge(logits_ready, 2 * layer + 1)
                for bank, at, done in ((s % 2, layer, "g_ready"), (2 + s % 4, 1 - layer, "u_ready")):
                    w = slice((at * blocks + j) * P, (at * blocks + j + 1) * P)
                    pe.matmul(ps[:, bank, :], wl[:, b, w], zh[:, cols], start=True, stop=False)
                    pe.matmul(ps[:, bank, :], wh[:, b, w], zl[:, cols], start=False, stop=False)
                    pe.matmul(ps[:, bank, :], wh[:, b, w], zh[:, cols], start=False, stop=True)\
                        .then_inc(q[done], 1)

            def turn_result(layer, m):
                q, units = ffn_sem[layer], 2 * LAYERS[layer].all_experts
                pe.wait_ge(q["y_summed"], units + m + 1)
                for t in range(TB):
                    last = turn(ps[:, m, t * P:(t + 1) * P], yT[:, (TB * m + t) * P:(TB * m + t + 1) * P])
                last.then_inc(y_turned, 1)

            def turn_keys1(i):
                pe.wait_ge(k1_staged, 1)
                for g in range(G1):
                    last = turn(ps[:, 2 + i, g * P:(g + 1) * P],
                                st_k1[:, i, 4 * g:4 * g + 4, :].rearrange("p h c -> p (h c)"))
                last.then_inc(k1_psum, 1)

            def down_biases():
                for t in range(T):
                    last = pe.matmul(ps[:, 2 + t // TB, t % TB * P:(t % TB + 1) * P],
                                     combT[:, t * P:(t + 1) * P].bitcast(F32), be2[:, :], start=True, stop=True)
                    if t % TB == TB - 1:
                        last.then_inc(bias_psum, 1)

            def down(layer, k, s, last):
                L, q = LAYERS[layer], ffn_sem[layer]
                u, j, blocks = L.place(s, last)
                g = L.steps * k + s
                m, b, n = 4 * k + u, (u // 2) % 2, u % 2
                if j == 0:
                    if n == 0:
                        pe.wait_ge(q["w_split"], 2 * k + u // 2 + 1)
                    pe.wait_ge(q["c_copied"], m + 2)
                pe.wait_ge(q["hh_ready"], g + 1)
                pe.wait_ge(q["hl_ready"], g + 3)
                w = slice((2 * blocks + j) * P, (2 * blocks + j + 1) * P)
                bank = ps[:, 6 + n, :]
                pe.matmul(bank, wl[:, b, w], hh[:, s % 2, :], start=(j == 0), stop=False)
                pe.matmul(bank, wh[:, b, w], hl[:, s % 2, :], start=False, stop=False)
                pe.matmul(bank, wh[:, b, w], hh[:, s % 2, :], start=False, stop=(j == blocks - 1))\
                    .then_inc(q["down_done"], 1)

            def ups(layer, steps):
                for s in steps:
                    up(layer, 0, s, False)

            def ffn(layer):
                L, q = LAYERS[layer], ffn_sem[layer]

                def spread(m, b, n):
                    pe.wait_ge(comb_ready, 2 * layer + 2)
                    pe.wait_ge(q["y_used"], m + 2)
                    pe.matmul(ps[:, 7 - n, :], selp[:, b, :], combT[:, n * COLS:(n + 1) * COLS],
                              start=True, stop=True).then_inc(q["c_ready"], 1)

                def step(k, s, last):
                    u, j, blocks = L.place(s, last)
                    if j == blocks - 1:
                        spread(4 * k + u, (u // 2) % 2, u % 2)
                    down(layer, k, s, last)

                with pe.Fori(0, L.pairs - 1) as k:
                    for s in range(L.first, L.first + L.steps):
                        up(layer, k, s + LEAD, False)
                        step(k, s, False)
                k, total = L.pairs - 1, L.last_steps()
                for s in range(L.first, total):
                    if s + LEAD < total:
                        up(layer, k, s + LEAD, True)
                    if s == total - 2:
                        if layer == 0:
                            turn_keys1(0)
                            turn_keys1(1)
                        else:
                            down_biases()
                    if s == total - 1:
                        turn_result(layer, 0)
                    step(k, s, True)
                if layer == 0:
                    turn_keys1(2)
                    turn_keys1(3)
                turn_result(layer, 1)

            def turn_tokens(index, m, bank):
                for t in range(TB * m, TB * m + TB):
                    pe.wait_ge(z_ready, T * index + t + 1)
                    last = turn(ps[:, bank, t % TB * P:(t % TB + 1) * P], z[:, t, :])
                last.then_inc(zT_psum, 1)

            def attend(units, base, scores, values, between):
                def score(u):
                    if u >= 4:
                        pe.wait_ge(probs_ready, base + u - 3)
                    scores(u, ps[:, u % 4, :]).then_inc(scores_ready, 1)

                score(0)
                score(1)
                for u in range(units):
                    if u in between:
                        between[u]()
                    if u + 2 < units:
                        score(u + 2)
                    pe.wait_ge(probs_ready, base + u + 1)
                    values(u, probs[:, u % 4, :]).then_inc(pv_done, 1)

            def project_out(layer, m, w):
                pe.wait_ge(oT_ready, 4 * layer + 2 * m + 2)
                for t in range(TB * m, TB * m + TB):
                    last = pe.matmul(ps[:, OWN[m], t % TB * P:(t % TB + 1) * P], oT[:, t * P:(t + 1) * P], w,
                                     start=True, stop=True)
                last.then_inc(o_psum, 1)

            def turn_attended(layer, m):
                pe.wait_ge(res_ready, 2 * layer + m + 1)
                turn_tokens(2 * layer + 1, m, OWN[m])

            def route(layer, m, w, experts):
                pe.wait_ge(zT_ready, 4 * layer + 2 + m + 1)
                pe.wait_ge(zl_ready, 2 * layer + m + 1)
                for t in range(TB * m, TB * m + TB):
                    last = pe.matmul(ps[:, OWN[m], t * 16:t * 16 + experts], zT[:, t * P:(t + 1) * P], w,
                                     start=True, stop=True)
                last.then_inc(route_psum, 1)

            def turn_combine(layer):
                pe.wait_ge(comb_staged, layer + 1)
                for t in range(T):
                    if t == TB:
                        pe.wait_ge(comb_ready, 2 * layer + 1)
                    last = turn(ps[:, OWN[1], t % TB * P:(t % TB + 1) * P], comb_st[:, t, :])
                    if t % TB == TB - 1:
                        last.then_inc(comb_psum, 1)

            def wait_parts(layer, m):
                pe.wait_ge(zh_ready, 2 * layer + m + 1)
                pe.wait_ge(zl_ready, 2 * layer + m + 1)

            def keys1():
                pe.wait_ge(w1_in, N_W1)
                pe.wait_ge(rT_ready, 1)
                for m in range(4):
                    last = pe.matmul(ps[:, 6 + m // 2, m % 2 * 256:m % 2 * 256 + 256], rT[:, m, :],
                                     w1c[:, :, :].rearrange("p a c -> p (a c)"), start=True, stop=True)
                last.then_inc(kv1_psum, 1)

            pe.wait_ge(const_ready, 3)
            pe.wait_ge(w0_in, N_W0)
            turn(ps[:, 2, 0:P], wq0[:, :])
            turn(ps[:, 2, P:2 * P], wlkv[:, 0, :])
            turn(ps[:, 2, 2 * P:3 * P], wlkv[:, 1, :])
            turn(ps[0:DC, 3, 0:P], wkv[:, 0, :])
            turn(ps[0:DC, 3, P:2 * P], wkv[:, 1, :])
            turn(ps[:, 3, 2 * P:3 * P], wo0[:, :]).then_inc(wT_psum, 1)
            pe.wait_ge(ctx_in, 32)
            pe.wait_ge(cz_ready, 4)
            for bank, src in ((4, ctx_z), (5, ctx_rows)):
                for b in range(B):
                    turn(ps[0:DC, bank, b * P:(b + 1) * P], src[:, b, :])
                    last = turn(ps[0:DC, bank, 2 * P + 32 * b:2 * P + 32 * b + KR], src[0:KR, 2 + b, :], KR)
            last.then_inc(cT_psum, 1)
            for m in range(2):
                turn_tokens(0, m, m)
            pe.wait_ge(wT_ready, 1)
            pe.wait_ge(cT_ready, 1)
            for m in range(4):
                last = pe.matmul(ps[:, 6 + m // 2, m % 2 * 256:m % 2 * 256 + 256], cT[:, m, :], wkvT[:, :],
                                 start=True, stop=True)
            last.then_inc(cproj_psum, 1)
            pe.wait_ge(zT_ready, 2)
            for t in range(T):
                if t >= 4:
                    pe.wait_ge(proj_used, t - 3)
                pe.matmul(ps[:, t % 4, 0:3 * P], zT[:, t * P:(t + 1) * P], wcat[:, :], start=True, stop=True)\
                    .then_inc(proj_psum, 1)
            pe.wait_ge(proj_used, T)
            pe.wait_ge(cproj_used, 2)
            for i in range(16):
                pe.wait_ge(staged, 1 + (i >= 4) + (i >= 6) + (i >= 10) + (i >= 12))
                if i >= 8:
                    pe.wait_ge(turned_a, i - 7)
                for a in range(4):
                    last = turn(ps[:, i % 8, a * P:(a + 1) * P], turned_from0(i, a))
                last.then_inc(turn_psum, 1)
            pe.wait_ge(turned_a, 16 - len(BY_DVE))
            pe.wait_ge(turned_v, len(BY_DVE))
            for u in range(2 * T):
                t, h = divmod(u, 2)
                b = t // TB
                if u >= 4:
                    pe.wait_ge(mx_used, u - 3)
                q = q_s0[:, h, t * P:(t + 1) * P]
                lat, con = ps[:, 2 * (u % 4), :], ps[:, 2 * (u % 4) + 1, :]
                pe.matmul(lat, q, k_a0[:, 0, b, h, P:5 * P], start=True, stop=True)
                pe.matmul(con[:, 0:P], q, k_a0[:, 0, b, h, 0:P], start=True, stop=False, skip_group_check=True)
                pe.matmul(con[:, P:CK], q, k_b0[:, 0, b, h, 64 * h:64 * h + KR], start=True, stop=False,
                          skip_group_check=True)
                pe.matmul(con[:, 0:CK], ones_row[:, :], mask_row[:, b, :], start=False, stop=True,
                          skip_group_check=True).then_inc(mx_psum, 1)
            pe.wait_ge(mx_used, 2 * T)
            pe.wait_ge(shift_staged, 1)
            for t in range(T):
                last = turn(ps[:, t // 4, t % 4 * P:(t % 4 + 1) * P], comb_st[:, t, :])
                if t % 4 == 3:
                    last.then_inc(shift_psum, 1)

            def scores0(u, bank):
                b, r = divmod(u, 11)
                h, block = divmod(r - 1, 5)
                n = slice(b * COLS, (b + 1) * COLS)
                for i, h in enumerate((0, 1) if r == 0 else (h,)):
                    for part in range(2):
                        k = k_b0[:, part, b, h, :] if r == 0 else k_a0[:, part, b, h, block * P:(block + 1) * P]
                        pe.matmul(bank, k, q_s0[:, h, n], start=(i == 0 and part == 0), stop=False)
                return pe.matmul(bank, selpk[:, :] if r == 0 else sel[:, h, :], combT[:, n], start=False, stop=True)

            def values0(u, p):
                b, r = divmod(u, 11)
                if r > 0:
                    h, block = divmod(r - 1, 5)
                    return pe.matmul(ps[:, 4 + 2 * b + h, :], v_a0[:, 5 * b + block, h, :], p,
                                     start=False, stop=(block == 4), skip_group_check=True)
                for h in range(H0):
                    last = pe.matmul(ps[:, 4 + 2 * b + h, :], v_b0[:, b, h, :], p, start=True, stop=False,
                                     skip_group_check=True)
                return last

            pe.wait_ge(const_ready, 4)
            pe.wait_ge(shift_ready, 2)
            pe.wait_ge(kv_ready, 2)
            attend(22, 0, scores0, values0,
                   {KEYS1: keys1, 11: lambda: pe.wait_ge(k1_staged, 1),
                    PROJECT0: lambda: project_out(0, 0, woT[:, :]), TURN0: lambda: turn_attended(0, 0),
                    ROUTE0: lambda: route(0, 0, wr0[:, :], E0)})

            wait_parts(0, 0)
            ups(0, range(LEAD))
            project_out(0, 1, woT[:, :])
            ups(0, (3,))
            down(0, 0, 0, False)
            turn_attended(0, 1)
            down(0, 0, 1, False)
            route(0, 1, wr0[:, :], E0)
            ups(0, (4,))
            down(0, 0, 2, False)
            ups(0, (5,))
            turn_combine(0)
            ffn(0)

            turn(ps[:, 7, 0:P], beR[:, :]).then_inc(beT_psum, 1)
            pe.wait_ge(k1_ready, 2)
            for m in range(2):
                turn_tokens(2, m, m)
                pe.wait_ge(zT_ready, 4 + m + 1)
                for t in range(TB * m, TB * m + TB):
                    last = pe.matmul(ps[:, 2 + m, t % TB * P:(t % TB + 1) * P], zT[:, t * P:(t + 1) * P],
                                     w1[:, 0, :], start=True, stop=True)
                last.then_inc(q1_psum, 1)
            pe.wait_ge(beT_ready, 1)
            pe.wait_ge(k1_ready, 4)

            def turn_queries(t, bank, done):
                for g in range(G1):
                    last = turn(ps[:, bank, g * P:(g + 1) * P],
                                st_q1[:, t, 4 * g:4 * g + 4, :].rearrange("p h c -> p (h c)"))
                last.then_inc(done, 1)

            def full_queries(t):
                pe.wait_ge(shift1_staged, t + 1)
                if t >= 1:
                    pe.wait_ge(q1_full, t)
                turn_queries(t, 7, q1_full_psum)

            for t in range(T):
                pe.wait_ge(q1_staged, t // 4 + 1)
                if t >= 1:
                    pe.wait_ge(q1_turned, t)
                turn_queries(t, 6, q1_turn_psum)
                if t == 1:
                    pe.wait_ge(q1_staged, 2)
                if t >= 1:
                    row_scores1(pe, t - 1, lambda: full_queries(t - 3) if t >= 3 else None)
            row_scores1(pe, T - 1, lambda: full_queries(T - 3))
            full_queries(T - 2)
            full_queries(T - 1)

            def scores1(u, bank):
                b, r = divmod(u, 20)
                g, j = divmod(r, 5)
                k = k_b1[:, b, g, :] if j == 4 else k_a1[:, b, g, j, :]
                return pe.matmul(bank, k, q_s1[:, g, b * COLS:(b + 1) * COLS], start=True, stop=True)

            def values1(u, p):
                b, r = divmod(u, 20)
                g, j = divmod(r, 5)
                a, c = divmod(g, 2)
                if j == 4:
                    v = v_b1[:, b, a, c * P:(c + 1) * P]
                else:
                    v = v_a1[:, b, a, (4 * c + j) * P:(4 * c + j + 1) * P]
                return pe.matmul(ps[:, 4 + 2 * b + a, :], v, p, start=(c == 0 and j == 0), stop=(c == 1 and j == 4))

            pe.wait_ge(q1_full, T)
            pe.wait_ge(mx1_used, 3 * T)
            pe.wait_ge(v1_ready, 1)
            attend(40, 22, scores1, values1,
                   {PROJECT1: lambda: project_out(1, 0, w1[:, 1, :]), TURN1: lambda: turn_attended(1, 0),
                    ROUTE1: lambda: route(1, 0, wr1[:, :], E1)})

            wait_parts(1, 0)
            ups(1, range(LEAD))
            project_out(1, 1, w1[:, 1, :])
            down(1, 0, 0, False)
            turn_attended(1, 1)
            down(1, 0, 1, False)
            route(1, 1, wr1[:, :], E1)
            ups(1, (3, 4))
            turn_combine(1)
            ffn(1)

        @block.vector
        def _(dve):
            do = linked(dve, dve_link)

            def statistics(x, st, out_mv, parts):
                for i, (rows, m) in enumerate(parts):
                    do(dve.bn_stats(st[0:rows, m, :], x[0:rows, m, :]), i == len(parts) - 1)
                for i, (rows, m) in enumerate(parts):
                    do(dve.bn_aggr(out_mv[0:rows, m, :], st[0:rows, m, :]), i == len(parts) - 1)

            def variance(tiles, twice=False):
                statistics(xres, stats, mv, [(P, t) for t in tiles])
                part = slice(tiles[0], tiles[-1] + 1)
                var = mv[:, part, 1:2].rearrange("p t o -> p (t o)")
                a, c = (1 + LN_EPS, LN_EPS * LN_EPS) if twice else (1.0, LN_EPS)
                dve.tensor_scalar(rstd[:, part], var, a, c, ALU.mult, ALU.add).then_inc(var_ready, 1)

            def scale_tokens(tiles, count):
                dve.wait_ge(rstd_ready, count)
                for t in tiles:
                    dve.tensor_scalar(z[:, t, :], xres[:, t, :], mv[:, t, 0:1], rstd[:, t:t + 1],
                                      ALU.subtract, ALU.mult).then_inc(z_ready, 1)

            def add_bias(index, bias):
                dve.wait_ge(gate_ready, 1)
                dve.wait_ge(z_ready, T * (index + 1))
                do(dve.scalar_tensor_tensor(out=xres[:, :, :], in0=bias.unsqueeze(1).broadcast_to([P, T, D]),
                                            scalar=tg[:, index // 2:index // 2 + 1], in1=xres[:, :, :],
                                            op0=ALU.mult, op1=ALU.add))

            def divide_by_sums(layer, b, i):
                dve.wait_ge(pv_done, (11 * b + (6, 11)[i], 22 + 20 * b + 10 * (i + 1))[layer])
                bank = ps[:, 4 + 2 * b + i, :]
                before = 4 * layer + 2 * b + i
                if before:
                    dve.wait_ge(oT_ready, before)
                do(dve.reciprocal(rcp, bank[64:P, :]))
                dve.tensor_tensor(oT[64 * i:64 * i + 64, b * COLS:(b + 1) * COLS], bank[0:64, :],
                                  rcp, ALU.mult).then_inc(oT_ready, 1)

            def add_attention(layer, m):
                dve.wait_ge(o_psum, 2 * layer + m + 1)
                part = xres[:, 4 * m:4 * m + 4, :].rearrange("p t d -> p (t d)")
                dve.scalar_tensor_tensor(out=part, in0=ps[:, OWN[m], :], scalar=tg[:, layer:layer + 1],
                                         in1=part, op0=ALU.mult, op1=ALU.add).then_inc(res_ready, 1)
                dve.wait_ge(res_ready, 2 * layer + m + 1)

            def low_tokens(layer, m):
                dve.wait_ge(zh_ready, 2 * layer + m + 1)
                cols = slice(m * COLS, (m + 1) * COLS)
                dve.tensor_tensor(zl[:, cols], ps[:, OWN[m], :], zh[:, cols].bitcast(F32), ALU.subtract)\
                    .then_inc(zl_ready, 1)

            def logits(layer, m, experts):
                dve.wait_ge(route_psum, 2 * layer + m + 1)
                tiles = slice(TB * m, TB * m + TB)
                src = ps[:, OWN[m], 0:T * 16].rearrange("p (t e) -> p t e", t=T)[:, tiles, 0:experts]
                dst = small[:, 0, 0:T * experts].rearrange("p (t e) -> p t e", t=T)[:, tiles, :]
                if layer == 0:
                    ins = dve.tensor_copy(dst, src)
                else:
                    ins = dve.scalar_tensor_tensor(out=dst, in0=src, scalar=1.0 / TAU,
                                                   in1=br[:, :].unsqueeze(1).broadcast_to([P, TB, experts]),
                                                   op0=ALU.mult, op1=ALU.add)
                ins.then_inc(logits_ready, 1)

            def add_down_biases():
                for m in range(2):
                    dve.wait_ge(bias_psum, m + 1)
                    part = xres[:, 4 * m:4 * m + 4, :].rearrange("p t d -> p (t d)")
                    dve.tensor_tensor(part, part, ps[:, 2 + m, :], ALU.add).then_inc(bias_added, 1)
                dve.wait_ge(bias_added, 2)

            def add_result(layer, m):
                dve.wait_ge(y_turned, 2 * layer + m + 1)
                part = xres[:, 4 * m:4 * m + 4, :].rearrange("p t d -> p (t d)")
                dve.tensor_tensor(part, part, ps[:, m, :], ALU.add).then_inc(y_added, 1)
                dve.wait_ge(y_added, 2 * layer + m + 1)

            def multiply(layer, k, s, last):
                bank = ps[:, 2 + s % 4, :]
                L, q = LAYERS[layer], ffn_sem[layer]
                u, j, blocks = L.place(s, last)
                g = L.steps * k + s
                dve.wait_ge(q["act_ready"], g + 1)
                dve.wait_ge(q["u_ready"], g + 1)
                if layer == 0:
                    ins = dve.tensor_tensor(bank, bank, act_out[:, s % 2, :], ALU.mult)
                else:
                    ins = dve.scalar_tensor_tensor(
                        out=bank, in0=bank, scalar=biases[:, (u // 2) % 2, j:j + 1],
                        in1=act_out[:, s % 2, :], op0=ALU.add, op1=ALU.mult)
                ins.then_inc(q["hid_ready"], 1)

            def low(layer, k, s):
                L, q = LAYERS[layer], ffn_sem[layer]
                g = L.steps * k + s
                dve.wait_ge(q["hid_ready"], g + 2)
                dve.wait_ge(q["hh_ready"], g + 1)
                dve.wait_ge(q["down_done"], g + 1)
                dve.tensor_tensor(hl[:, s % 2, :], ps[:, 2 + s % 4, :], hh[:, s % 2, :].bitcast(F32),
                                  ALU.subtract).then_inc(q["hl_ready"], 1)

            def attended(layer, experts, count):
                def multiply0(s):
                    multiply(layer, 0, s, False)

                for i in range(2):
                    divide_by_sums(layer, 0, i)
                add_attention(layer, 0)
                variance(range(0, TB))
                scale_tokens(range(0, TB), count)
                divide_by_sums(layer, 1, 0)
                low_tokens(layer, 0)
                logits(layer, 0, experts)
                divide_by_sums(layer, 1, 1)
                multiply0(0)
                add_attention(layer, 1)
                variance(range(TB, T))
                multiply0(1)
                low(layer, 0, 0)
                scale_tokens(range(TB, T), count + 1)
                multiply0(2)
                low(layer, 0, 1)
                low_tokens(layer, 1)
                if layer == 0:
                    multiply0(3)
                logits(layer, 1, experts)
                choose(layer, experts, (lambda: low(0, 0, 2)) if layer == 0 else (lambda: multiply0(3)))
                if layer == 0:
                    multiply0(4)
                low(layer, 0, LAYERS[layer].first)

            def choose(layer, experts, meanwhile):
                def v(i, n=experts):
                    return small[:, i, 0:T * n].rearrange("p (t e) -> p t e", t=T)

                def over(x, n=experts):
                    return x.unsqueeze(2).broadcast_to([P, T, n])

                def row(i):
                    return small[:, i, 0:T]

                logit, first_hot, second_hot, hot, rest, weights = v(0), v(1), v(2), v(3), v(4), v(5)
                first = rev[:, 0:experts].unsqueeze(1).broadcast_to([P, T, experts])
                dve.wait_ge(const_ready, 7)
                dve.wait_ge(logits_ready, 2 * layer + 2)
                for t in range(T):
                    do(dve.max(top[:, t, :], logit[:, t, :]), t == T - 1)
                dve.tensor_tensor(row(15), top[:, :, 1], top[:, :, 0], ALU.subtract).then_inc(gap_ready, 1)
                for i, (source, chosen) in enumerate(((logit, first_hot), (rest, second_hot))):
                    do(dve.tensor_tensor(hot, source, over(top[:, :, i]), ALU.is_equal))
                    do(dve.tensor_tensor(hot, hot, first, ALU.mult))
                    do(dve.tensor_reduce(row(14), hot, AX.X, ALU.max))
                    do(dve.tensor_tensor(chosen, hot, over(row(14)), ALU.is_equal))
                    if i == 0:
                        do(dve.scalar_tensor_tensor(out=rest, in0=first_hot, scalar=-BIG, in1=logit,
                                                    op0=ALU.mult, op1=ALU.add))
                meanwhile()
                dve.wait_ge(e_ready, layer + 1)
                do(dve.tensor_scalar(row(12), row(15), 1.0, None, ALU.add), False)
                do(dve.tensor_tensor(weights, second_hot, over(row(15)), ALU.mult))
                do(dve.reciprocal(row(13), row(12)), False)
                do(dve.tensor_tensor(weights, weights, first_hot, ALU.add))
                for dst in (comb_w[:, :, 0:experts], comb_st[:, :, 0:experts].bitcast(F32R)):
                    do(dve.scalar_tensor_tensor(out=dst, in0=over(row(13)), scalar=tg[:, 2 + layer:3 + layer],
                                                in1=weights, op0=ALU.mult, op1=ALU.mult), dst is not comb_w)
                cols = LAYERS[layer].all_experts
                dve.tensor_tensor(comb_st[:, :, LO:LO + cols].bitcast(F32R), comb_w[:, :, 0:cols], comb_st[:, :, 0:cols],
                                  ALU.subtract).then_inc(comb_staged, 1)

            def ffn(layer):
                L, q = LAYERS[layer], ffn_sem[layer]

                def weigh(k, u, end):
                    m, n = 4 * k + u, u % 2
                    dve.wait_ge(q["down_done"], L.steps * k + end + 2)
                    dve.wait_ge(q["c_copied"], m + 3)
                    dve.wait_ge(q["y_summed"], m + 1)
                    dve.tensor_tensor(ytmp[:, n, :], ps[:, 6 + n, :], cbs[:, n, :], ALU.mult).then_inc(q["y_used"], 1)

                start = L.first + 1
                with dve.Fori(0, L.pairs - 1) as k:
                    for s in range(start, start + L.steps):
                        multiply(layer, k, s + 1, False)
                        low(layer, k, s)
                        if s % L.blocks == 0:
                            weigh(k, s // L.blocks - 1, s)
                k, total = L.pairs - 1, L.last_steps()
                for s in range(start, total + 1):
                    if s + 1 < total:
                        multiply(layer, k, s + 1, True)
                    if s < total:
                        low(layer, k, s)
                    else:
                        if layer == 1:
                            add_down_biases()
                        add_result(layer, 0)
                    u, j, blocks = L.place(s - 1, True)
                    if j == blocks - 1:
                        weigh(k, u, s)

            do(dve.memset(crstd[:, :], 1.0))
            dve.wait_ge(ctx_in, 32)
            statistics(ctx_rows, cstats, cmv, [(P, 0), (P, 1), (KR, 2), (KR, 3)])
            do(dve.tensor_scalar(crstd[:, 0:2], cmv[:, 0:2, 1:2].rearrange("p a o -> p (a o)"), LN_EPS, None, ALU.add))
            dve.tensor_scalar(crstd[0:KR, 2:4], cmv[0:KR, 2:4, 1:2].rearrange("p a o -> p (a o)"), LN_EPS, None,
                              ALU.add).then_inc(var_ready, 1)
            dve.wait_ge(rstd_ready, 1)
            for m in range(4):
                rows = slice(0, P if m < 2 else KR)
                dve.tensor_scalar(ctx_z[rows, m, :], ctx_rows[rows, m, :], cmv[rows, m, 0:1], crstd[rows, m:m + 1],
                                  ALU.subtract, ALU.mult).then_inc(cz_ready, 1)
            dve.wait_ge(x_in, 16)
            variance(range(T), twice=True)
            scale_tokens(range(T), 2)
            dve.wait_ge(vec_in, N_VEC)
            add_bias(0, bo0[:, :])
            do(dve.tensor_scalar(tg[:, 2:3], tg[:, 2:3], DEPTH_SCALE, None, ALU.mult))
            dve.wait_ge(const_ready, 3)
            do(dve.tensor_scalar(ones_row[:, :], half[0:1, 0:1].broadcast_to([1, P]), -2.0, None, ALU.mult), False)
            do(dve.tensor_scalar(mask_row[:, :, :].rearrange("p b k -> p (b k)"), mask8[:, :], BIG, -BIG, ALU.mult, ALU.add))
            do(dve.tensor_scalar(mcol[:, :], mcol8[:, :], BIG, -BIG, ALU.mult, ALU.add))
            do(dve.tensor_tensor(gqk[:, :], gq[:, :], gk[:, :], ALU.mult))
            do(dve.tensor_scalar(gqk[:, :], gqk[:, :], HD0 ** -0.5, None, ALU.mult))

            dve.wait_ge(cproj_used, 2)
            ckeys = ckv[:, :, 0:P].rearrange("p m (h c) -> p m h c", h=H0)
            csq = stage[:, 0:4 * P].rearrange("p (m h c) -> p m h c", m=4, h=H0)
            do(dve.tensor_tensor(csq, ckeys, ckeys, ALU.mult))
            do(dve.tensor_reduce(css[:, :, :], csq, AX.X, ALU.add))
            dve.tensor_scalar(css[:, :, :], css[:, :, :], 1.0 / HD0, RMS_EPS2, ALU.mult, ALU.max).then_inc(var_ready, 1)
            qk = qkv[:, :, 0:2 * P].rearrange("p t (h c) -> p t h c", h=4)
            sq = stage[:, 0:2048].rearrange("p (t h c) -> p t h c", t=T, h=4)
            for m in range(2):
                tiles = slice(TB * m, TB * m + TB)
                dve.wait_ge(proj_used, TB * m + TB)
                do(dve.tensor_tensor(sq[:, tiles], qk[:, tiles], qk[:, tiles], ALU.mult))
                do(dve.tensor_reduce(ss[:, tiles, :], sq[:, tiles], AX.X, ALU.add))
                dve.tensor_scalar(ss[:, tiles, :], ss[:, tiles, :], 1.0 / HD0, RMS_EPS2, ALU.mult, ALU.max)\
                    .then_inc(var_ready, 1)
            dve.wait_ge(rstd_ready, 3)
            do(dve.tensor_tensor(ckeys, ckeys, crn[:, :, :].unsqueeze(3).broadcast_to([P, 4, H0, HD0]), ALU.mult))
            dve.wait_ge(zeroed, 5)
            for rows, blocks, heads in ((slice(0, P), slice(0, 2), slice(0, 2)),
                                        (slice(0, 64), slice(2, 4), slice(0, 1)), (slice(64, P), slice(2, 4), slice(1, 2))):
                src = ckeys[rows, blocks, heads, :]
                for dup in range(2):
                    do(dve.tensor_copy(st_c0[0][rows, blocks, heads, 64 * dup:64 * dup + 64], src))
                for dup in range(2):
                    last = dve.tensor_tensor(st_c0[1][rows, blocks, heads, 64 * dup:64 * dup + 64], src,
                                             st_c0[0][rows, blocks, heads, 0:64].bitcast(F32), ALU.subtract)
            last.then_inc(staged, 1)
            for m in range(2):
                tiles = slice(TB * m, TB * m + TB)
                dve.wait_ge(rstd_ready, 4 + m)
                do(dve.tensor_tensor(qk[:, tiles], qk[:, tiles],
                                     rn[:, tiles, :].unsqueeze(3).broadcast_to([P, TB, 4, HD0]), ALU.mult))
                for h in range(H0):
                    qh = qk[:, tiles, h, :]
                    do(dve.tensor_tensor(qh, qh, gqk[:, :].unsqueeze(1).broadcast_to([P, TB, HD0]), ALU.mult),
                       h == H0 - 1)
                q_hi, q_lo, k_hi, k_lo, qq, kk = parts0(tiles)
                dve.tensor_copy(k_hi[1].bitcast(F32R), kk).then_inc(qk_ready, 1)
                dve.wait_ge(high_ready, m + 1)
                dve.tensor_tensor(q_lo.bitcast(F32R), qq, q_hi, ALU.subtract).then_inc(staged, 1)
                for dup in range(2):
                    last = dve.tensor_tensor(k_lo[dup].bitcast(F32R), kk, k_hi[0], ALU.subtract)
                last.then_inc(staged, 1)
            dve.wait_ge(zeroed, 7)
            for h in range(H0):
                last = dve.memset(v_b0[64 * h:64 * h + 64, :, h, 64:P], 1.0)
            last.then_inc(kv_ready, 1)
            for i in BY_DVE:
                dve.wait_ge(turn_psum, i + 1)
                dve.tensor_copy(turned_to0(i), turned_bank0(i)).then_inc(turned_v, 1)
            for u in range(2 * T):
                t, h = divmod(u, 2)
                dve.wait_ge(mx_psum, u + 1)
                row = ps[:, 2 * (u % 4):2 * (u % 4) + 2, :].rearrange("p a n -> p (a n)")[:, 0:COLS + CK]
                dve.tensor_reduce(mx[:, t, h:h + 1], row, AX.X, ALU.max).then_inc(mx_used, 1)
            dve.wait_ge(mx_used, 2 * T)
            dve.wait_ge(zeroed, 1)
            dve.tensor_scalar(comb_st[:, :, 0:2].bitcast(F32R), mx[:, :, 0:H0],
                              -1.0, None, ALU.mult).then_inc(shift_staged, 1)
            dve.wait_ge(w1_in, N_W1)
            dve.wait_ge(kv_ready, 2)
            for m in range(2):
                dve.wait_ge(kv1_psum, 1)
                do(dve.tensor_tensor(ckv[:, 2 * m:2 * m + 2, :], ps[:, 6 + m, :].rearrange("p (b c) -> p b c", b=B),
                                     b1[:, 1:3, :].rearrange("p a c -> p (a c)").unsqueeze(1).broadcast_to([P, B, 2 * P]),
                                     ALU.add))
            dve.wait_ge(zeroed, 8)
            for rows, blocks, j in [(slice(0, P), slice(0, 2), None)] + \
                    [(slice(32 * j, 32 * j + 32), slice(2, 4), j) for j in range(4)]:
                heads = slice(0, H1) if j is None else slice(j, H1, 4)
                src = ckv[rows, blocks, 0:P].rearrange("p m (h d) -> p m h d", h=H1)[:, :, heads, :]
                dst = st_k1[rows, blocks, heads, :]
                do(dve.tensor_copy(dst[:, :, :, 0:8].bitcast(F32R), src))
                dve.tensor_copy(dst[:, :, :, 8:16].bitcast(F32R), src)
                dve.tensor_tensor(dst[:, :, :, 16:24].bitcast(F32R), src, dst[:, :, :, 0:8], ALU.subtract)
                last = dve.memset(dst[:, :, :, 24:25], 1.0)
            last.then_inc(k1_staged, 1)
            do(dve.tensor_scalar(b1[:, 0, :], b1[:, 0, :], HD1 ** -0.5, None, ALU.mult))
            do(dve.tensor_scalar(br[:, :], br[:, :], 1.0 / TAU, None, ALU.mult))
            attended(0, E0, 6)

            ffn(0)
            variance(range(0, TB))
            add_result(0, 1)
            scale_tokens(range(0, TB), 8)
            variance(range(TB, T))
            scale_tokens(range(TB, T), 9)
            dve.wait_ge(zeroed, 9)
            for m in range(2):
                dve.wait_ge(q1_psum, m + 1)
                dst = qkv[:, 4 * m:4 * m + 4, 0:P]
                do(dve.scalar_tensor_tensor(out=dst, in0=ps[:, 2 + m, :].rearrange("p (t c) -> p t c", t=4),
                                            scalar=HD1 ** -0.5, in1=b1[:, 0, :].unsqueeze(1).broadcast_to([P, 4, P]),
                                            op0=ALU.mult, op1=ALU.add))
                src = dst.rearrange("p t (h d) -> p t h d", h=H1)
                st = st_q1[:, 4 * m:4 * m + 4, :, :]
                do(dve.tensor_copy(st[:, :, :, 0:8].bitcast(F32R), src))
                dve.tensor_copy(st[:, :, :, 16:24].bitcast(F32R), src)
                dve.tensor_tensor(st[:, :, :, 8:16].bitcast(F32R), src, st[:, :, :, 0:8], ALU.subtract)\
                    .then_inc(q1_staged, 1)

            def shifts(t):
                dve.wait_ge(mx1_used, 3 * t + 3)
                do(dve.tensor_tensor(small[:, t % 2, 0:H1], mx[:, t, 0:H1], mx[:, t, H1:2 * H1], ALU.max))
                dve.tensor_scalar(st_q1[:, t, :, 24:25].rearrange("p h o -> p (h o)").bitcast(F32R),
                                  small[:, t % 2, 0:H1], -1.0, None, ALU.mult).then_inc(shift1_staged, 1)

            for t in range(T):
                for g in range(0, G1, 2):
                    dve.wait_ge(mx1_psum, 5 * t + g + 2)
                    dve.tensor_reduce(mx[:, t, 4 * g:4 * g + 8], ps[:, g:g + 2, :].rearrange("p g (j k) -> p (g j) k", j=4),
                                      AX.X, ALU.max).then_inc(mx1_used, 1)
                    if t >= 1 and g == 0:
                        shifts(t - 1)
                dve.wait_ge(mx1_psum, 5 * t + 5)
                dve.tensor_reduce(mx[:, t, H1:2 * H1], ps[:, 4 + t % 2, :].rearrange("p (h k) -> p h k", h=H1)
                                  [:, :, 0:KR], AX.X, ALU.max).then_inc(mx1_used, 1)
            shifts(T - 1)
            add_bias(2, b1[:, 3, :])
            shared = tg[:, 3:4].unsqueeze(1).broadcast_to([P, T, 1])
            do(dve.tensor_copy(comb_w[:, :, E1:E1 + 1], shared), False)
            do(dve.tensor_copy(comb_st[:, :, E1:E1 + 1].bitcast(F32R), shared))
            attended(1, E1, 10)

            ffn(1)
            add_result(1, 1)


_INS = ["x", "ctx_768", "mask_BxS2_bk0", "g_xattn", "g_ffn", "L0_xattn_ln_x_g", "L0_xattn_ln_x_b",
        "L0_xattn_ln_l_g", "L0_xattn_ln_l_b", "L0_xattn_qn_g", "L0_xattn_kn_g", "L0_xattn_Wq", "L0_xattn_Wkv",
        "L0_xattn_Wlkv", "L0_xattn_Wo", "L0_xattn_bo", "L0_ffn_Wr", "L0_ffn_Wg", "L0_ffn_Wu", "L0_ffn_Wd",
        "L1_xattn_wq", "L1_xattn_bq", "L1_xattn_wk", "L1_xattn_bk", "L1_xattn_wv", "L1_xattn_bv", "L1_xattn_wo",
        "L1_xattn_bo", "L1_ffn_Ws1", "L1_ffn_bs1", "L1_ffn_Ws2", "L1_ffn_bs2", "L1_ffn_We1", "L1_ffn_be1",
        "L1_ffn_We2", "L1_ffn_be2", "L1_ffn_Wr", "L1_ffn_br"]


def kernel(**inputs):
    import numpy as np
    import concourse.bacc as bacc
    from concourse.bass_utils import run_bass_kernel_spmd

    nc = bacc.Bacc("TRN2", target_bir_lowering=False, num_devices=1)
    arrays, aps = {}, {}
    for name in _INS:
        a = np.ascontiguousarray(inputs[name])
        arrays[f"in_{name}"] = a
        aps[name] = nc.dram_tensor(f"in_{name}", a.shape, mybir.dt.from_np(a.dtype), kind="ExternalInput").ap()
    out = nc.dram_tensor("out_x", (B, S, D), F32, kind="ExternalOutput").ap()
    flamingo(nc, aps, out)
    r = run_bass_kernel_spmd(nc, [arrays], core_ids=[0])
    return r.results[0]["out_x"]
```
